# Optimizing a Trainium2 kernel written in Bass

```python
import numpy as np
import jax
import jax.numpy as jnp

def _softmax(x, axis=-1):
    return jax.nn.softmax(x, axis=axis)

def _gelu(x):
    return jax.nn.gelu(x, approximate=True)

def _silu(x):
    return jax.nn.silu(x)

def _sigmoid(x):
    return jax.nn.sigmoid(x)

def _layernorm(x, axis=-1, eps=1e-05):
    m = jnp.mean(x, axis=axis, keepdims=True)
    v = jnp.var(x, axis=axis, keepdims=True)
    return (x - m) / jnp.sqrt(v + eps)

def _scatter_add(tgt, idx, src, axis=0):
    return tgt.at[idx].add(src)

def _segment_sum(src, seg, n):
    return jax.ops.segment_sum(src, seg, n)
kernel_name = 'mk_adj_preln_d4_adj_r2_cc9ec0'

def setup_inputs(seed: int=0):
    np.random.seed(seed)
    _w = jnp.asarray

    def _rec_inputs():
        import jax
        import jax.numpy as jnp
        _gk = jax.random.key(seed)
        x = -0.0005207 + 1.001 * jax.random.normal(jax.random.fold_in(_gk, 1), (16, 512, 128), jnp.float32)
        _a = jax.random.bernoulli(jax.random.fold_in(_gk, 2), 0.00390625, (16, 512, 512))
        _a = jnp.logical_or(_a, jnp.swapaxes(_a, -1, -2))
        _a = jnp.logical_or(_a, jnp.eye(512, dtype=bool))
        _af = _a.astype(jnp.float32)
        adj = _af
        _nm = jnp.ones((16, 512), dtype=bool)
        nodemask = jnp.where(_nm, 1.0, 0.0).astype(jnp.float32)
        return (x, adj, nodemask)
    x, adj, nodemask = _rec_inputs()

    def _L0_gnn_setup():
        import jax, jax.numpy as jnp
        import numpy as np
        DIM = 128
        HEADS = 8
        BS = 8
        N = 512
        NEG = -1000000000.0
        key = jax.random.key(seed)
        ks = jax.random.split(key, 8)
        feats = jax.random.normal(ks[0], (BS, N, DIM), dtype=jnp.float32)
        adj_mat = (jax.random.uniform(ks[1], (BS, N, N)) < 0.1).astype(jnp.float32)
        s = 1.0 / np.sqrt(DIM)
        fc_w = jax.random.normal(ks[2], (DIM, DIM * HEADS), dtype=jnp.float32) * s
        fc_b = jnp.zeros((DIM * HEADS,), dtype=jnp.float32)
        q_w = jax.random.normal(ks[3], (DIM, 1), dtype=jnp.float32) * s
        q_b = jnp.zeros((1,), dtype=jnp.float32)
        k_w = jax.random.normal(ks[4], (DIM, 1), dtype=jnp.float32) * s
        k_b = jnp.zeros((1,), dtype=jnp.float32)
        fp_w = jax.random.normal(ks[5], (DIM * HEADS, DIM), dtype=jnp.float32) * (1.0 / np.sqrt(DIM * HEADS))
        fp_b = jnp.zeros((DIM,), dtype=jnp.float32)
        return {'feats': feats, 'adj_mat': adj_mat, 'fc_w': fc_w, 'fc_b': fc_b, 'q_w': q_w, 'q_b': q_b, 'k_w': k_w, 'k_b': k_b, 'fp_w': fp_w, 'fp_b': fp_b}
    _L0_gnn_all = _L0_gnn_setup()
    _L0_gnn_in = {k: v for k, v in _L0_gnn_all.items() if k in ('fc_w', 'fc_b', 'q_w', 'q_b', 'k_w', 'k_b', 'fp_w', 'fp_b')}
    del _L0_gnn_all

    def _L1_gnn_setup():
        import jax, jax.numpy as jnp
        import numpy as np
        B, N, D = (8, 1024, 128)
        NEG = -9000000000000000.0
        key = jax.random.key(seed)
        ks = jax.random.split(key, 8)
        x = jax.random.normal(ks[0], (B, N, D), dtype=jnp.float32)
        adj = jax.random.randint(ks[1], (B, N, N), 0, 2).astype(jnp.float32)
        s = 1.0 / np.sqrt(D)
        W_w = jax.random.uniform(ks[2], (D, D), jnp.float32, -s, s)
        W_b = jax.random.uniform(ks[3], (D,), jnp.float32, -s, s)
        A = jax.random.normal(ks[4], (D, D), dtype=jnp.float32) * 0.02
        sg = 1.0 / np.sqrt(2 * D)
        gate_w = jax.random.uniform(ks[5], (1, 2 * D), jnp.float32, -sg, sg)
        gate_b = jax.random.uniform(ks[6], (1,), jnp.float32, -sg, sg)
        return {'x': x, 'adj': adj, 'W_w': W_w, 'W_b': W_b, 'A': A, 'gate_w': gate_w, 'gate_b': gate_b, 'use_adj': 1}
    _L1_gnn_all = _L1_gnn_setup()
    _L1_gnn_in = {k: v for k, v in _L1_gnn_all.items() if k in ('W_w', 'W_b', 'A', 'gate_w', 'gate_b')}
    del _L1_gnn_all

    def _L2_gnn_setup():
        import jax, jax.numpy as jnp
        import numpy as np
        B, N, D, C, L = (64, 256, 128, 128, 5)
        EDGE_P = 0.02

        def _gru_cell(m, h, w_ih, w_hh, b_ih, b_hh):
            gi = m @ w_ih.T + b_ih
            gh = h @ w_hh.T + b_hh
            i_r, i_z, i_n = jnp.split(gi, 3, axis=-1)
            h_r, h_z, h_n = jnp.split(gh, 3, axis=-1)
            r = jax.nn.sigmoid(i_r + h_r)
            z = jax.nn.sigmoid(i_z + h_z)
            n = jnp.tanh(i_n + r * h_n)
            return (1.0 - z) * n + z * h
        key = jax.random.key(seed)
        ks = jax.random.split(key, 8)
        x = jax.random.normal(ks[0], (B, N, D), dtype=jnp.float32)
        adj = (jax.random.uniform(ks[1], (B, N, N)) < EDGE_P).astype(jnp.float32)
        mask = jnp.ones((B, N), dtype=jnp.float32)
        s = 1.0 / np.sqrt(C).astype(np.float32)
        weight = jax.random.uniform(ks[2], (L, C, C), minval=-s, maxval=s, dtype=jnp.float32)
        w_ih = jax.random.uniform(ks[3], (3 * C, C), minval=-s, maxval=s, dtype=jnp.float32)
        w_hh = jax.random.uniform(ks[4], (3 * C, C), minval=-s, maxval=s, dtype=jnp.float32)
        b_ih = jax.random.uniform(ks[5], (3 * C,), minval=-s, maxval=s, dtype=jnp.float32)
        b_hh = jax.random.uniform(ks[6], (3 * C,), minval=-s, maxval=s, dtype=jnp.float32)
        return dict(x=x, adj=adj, mask=mask, weight=weight, w_ih=w_ih, w_hh=w_hh, b_ih=b_ih, b_hh=b_hh)
    _L2_gnn_all = _L2_gnn_setup()
    _L2_gnn_in = {k: v for k, v in _L2_gnn_all.items() if k in ('weight', 'w_ih', 'w_hh', 'b_ih', 'b_hh')}
    del _L2_gnn_all

    def _L3_gnn_setup():
        import jax, jax.numpy as jnp
        import numpy as np
        from jax import lax
        DIM = 128
        EPS = 1e-05

        def _bn(h, g, b, m, v):
            scale = g / jnp.sqrt(v + EPS)
            return h * scale[None, :, None] + (b - m * scale)[None, :, None]

        def _conv1d(h, w, pad):
            return lax.conv_general_dilated(h, w, window_strides=(1,), padding=[(pad, pad)], dimension_numbers=('NCH', 'OIH', 'NCH'))
        key = jax.random.key(seed)
        ks = jax.random.split(key, 16)
        bs, n, d = (16, 1024, DIM)
        s = 0.05
        return {'x': jax.random.normal(ks[0], (bs, n, d), jnp.float32), 'mask': jnp.ones((bs, n, n), jnp.float32), 'w_se': jax.random.normal(ks[1], (3, d), jnp.float32) * s, 'b_se': jnp.zeros((3,), jnp.float32), 'conv1_w': jax.random.normal(ks[2], (d, d, 1), jnp.float32) * s, 'bn1_g': jnp.ones((d,), jnp.float32), 'bn1_b': jnp.zeros((d,), jnp.float32), 'bn1_m': jnp.zeros((d,), jnp.float32), 'bn1_v': jnp.ones((d,), jnp.float32), 'conv2_w': jax.random.normal(ks[3], (d, d, 17), jnp.float32) * s, 'bn2_g': jnp.ones((d,), jnp.float32), 'bn2_b': jnp.zeros((d,), jnp.float32), 'bn2_m': jnp.zeros((d,), jnp.float32), 'bn2_v': jnp.ones((d,), jnp.float32), 'w_msg': jax.random.normal(ks[4], (d, d), jnp.float32) * s, 'b_msg': jnp.zeros((d,), jnp.float32), 'w_ih': jax.random.normal(ks[5], (3 * d, 2 * d), jnp.float32) * s, 'b_ih': jnp.zeros((3 * d,), jnp.float32), 'w_hh': jax.random.normal(ks[6], (3 * d, d), jnp.float32) * s, 'b_hh': jnp.zeros((3 * d,), jnp.float32)}
    _L3_gnn_all = _L3_gnn_setup()
    _L3_gnn_in = {k: v for k, v in _L3_gnn_all.items() if k in ('w_se', 'b_se', 'conv1_w', 'bn1_g', 'bn1_b', 'bn1_m', 'bn1_v', 'conv2_w', 'bn2_g', 'bn2_b', 'bn2_m', 'bn2_v', 'w_msg', 'b_msg', 'w_ih', 'b_ih', 'w_hh', 'b_hh')}
    del _L3_gnn_all
    return {'x': x, 'adj': adj, 'nodemask': nodemask, 'L0_gnn_fc_w': _L0_gnn_in['fc_w'], 'L0_gnn_fc_b': _L0_gnn_in['fc_b'], 'L0_gnn_q_w': _L0_gnn_in['q_w'], 'L0_gnn_q_b': _L0_gnn_in['q_b'], 'L0_gnn_k_w': _L0_gnn_in['k_w'], 'L0_gnn_k_b': _L0_gnn_in['k_b'], 'L0_gnn_fp_w': _L0_gnn_in['fp_w'], 'L0_gnn_fp_b': _L0_gnn_in['fp_b'], 'L1_gnn_W_w': _L1_gnn_in['W_w'], 'L1_gnn_W_b': _L1_gnn_in['W_b'], 'L1_gnn_A': _L1_gnn_in['A'], 'L1_gnn_gate_w': _L1_gnn_in['gate_w'], 'L1_gnn_gate_b': _L1_gnn_in['gate_b'], 'L2_gnn_weight': _L2_gnn_in['weight'], 'L2_gnn_w_ih': _L2_gnn_in['w_ih'], 'L2_gnn_w_hh': _L2_gnn_in['w_hh'], 'L2_gnn_b_ih': _L2_gnn_in['b_ih'], 'L2_gnn_b_hh': _L2_gnn_in['b_hh'], 'L3_gnn_w_se': _L3_gnn_in['w_se'], 'L3_gnn_b_se': _L3_gnn_in['b_se'], 'L3_gnn_conv1_w': _L3_gnn_in['conv1_w'], 'L3_gnn_bn1_g': _L3_gnn_in['bn1_g'], 'L3_gnn_bn1_b': _L3_gnn_in['bn1_b'], 'L3_gnn_bn1_m': _L3_gnn_in['bn1_m'], 'L3_gnn_bn1_v': _L3_gnn_in['bn1_v'], 'L3_gnn_conv2_w': _L3_gnn_in['conv2_w'], 'L3_gnn_bn2_g': _L3_gnn_in['bn2_g'], 'L3_gnn_bn2_b': _L3_gnn_in['bn2_b'], 'L3_gnn_bn2_m': _L3_gnn_in['bn2_m'], 'L3_gnn_bn2_v': _L3_gnn_in['bn2_v'], 'L3_gnn_w_msg': _L3_gnn_in['w_msg'], 'L3_gnn_b_msg': _L3_gnn_in['b_msg'], 'L3_gnn_w_ih': _L3_gnn_in['w_ih'], 'L3_gnn_b_ih': _L3_gnn_in['b_ih'], 'L3_gnn_w_hh': _L3_gnn_in['w_hh'], 'L3_gnn_b_hh': _L3_gnn_in['b_hh']}

def reference(x, adj, nodemask, L0_gnn_fc_w, L0_gnn_fc_b, L0_gnn_q_w, L0_gnn_q_b, L0_gnn_k_w, L0_gnn_k_b, L0_gnn_fp_w, L0_gnn_fp_b, L1_gnn_W_w, L1_gnn_W_b, L1_gnn_A, L1_gnn_gate_w, L1_gnn_gate_b, L2_gnn_weight, L2_gnn_w_ih, L2_gnn_w_hh, L2_gnn_b_ih, L2_gnn_b_hh, L3_gnn_w_se, L3_gnn_b_se, L3_gnn_conv1_w, L3_gnn_bn1_g, L3_gnn_bn1_b, L3_gnn_bn1_m, L3_gnn_bn1_v, L3_gnn_conv2_w, L3_gnn_bn2_g, L3_gnn_bn2_b, L3_gnn_bn2_m, L3_gnn_bn2_v, L3_gnn_w_msg, L3_gnn_b_msg, L3_gnn_w_ih, L3_gnn_b_ih, L3_gnn_w_hh, L3_gnn_b_hh):
    import jax
    import jax.numpy as jnp

    def _L0_gnn_ref(feats, adj_mat, fc_w, fc_b, q_w, q_b, k_w, k_b, fp_w, fp_b):
        import jax, jax.numpy as jnp
        import numpy as np
        DIM = 128
        HEADS = 8
        BS = 8
        N = 512
        NEG = -1000000000.0
        bs, n, dim = feats.shape
        feat_proj = (feats @ fc_w + fc_b).reshape(bs, n, HEADS, dim).transpose(0, 2, 1, 3)
        q = feat_proj @ q_w + q_b
        k = feat_proj @ k_w + k_b
        logits = q + jnp.swapaxes(k, -1, -2)
        masked = logits + (1.0 - adj_mat[:, None]) * NEG
        masked = jax.nn.leaky_relu(masked, negative_slope=0.01)
        attn = jax.nn.softmax(masked, axis=-1)
        out = attn @ feat_proj
        out = out.transpose(0, 2, 1, 3).reshape(bs, n, HEADS * dim)
        out = out @ fp_w + fp_b + feats
        return jax.nn.sigmoid(out)

    def _L1_gnn_ref(x, adj, W_w, W_b, A, gate_w, gate_b, use_adj):
        import jax, jax.numpy as jnp
        import numpy as np
        B, N, D = (8, 1024, 128)
        NEG = -9000000000000000.0
        h = jnp.einsum('bnf,of->bno', x, W_w) + W_b
        e = jnp.einsum('bjl,bkl->bjk', jnp.einsum('bnd,de->bne', h, A), h)
        e = e + jnp.swapaxes(e, 1, 2)
        if use_adj:
            att = jnp.where(adj > 0, e, jnp.full_like(e, NEG))
            att = jax.nn.softmax(att, axis=1)
            att = att * adj
        else:
            att = e
        h_prime = jax.nn.relu(jnp.einsum('bij,bjk->bik', att, h))
        gate_in = jnp.concatenate([x, h_prime], axis=-1)
        coeff = jax.nn.sigmoid(jnp.einsum('bnf,of->bno', gate_in, gate_w) + gate_b)
        return coeff * x + (1.0 - coeff) * h_prime

    def _L2_gnn_ref(x, adj, mask, weight, w_ih, w_hh, b_ih, b_hh):
        import jax, jax.numpy as jnp
        import numpy as np
        B, N, D, C, L = (64, 256, 128, 128, 5)
        EDGE_P = 0.02

        def _gru_cell(m, h, w_ih, w_hh, b_ih, b_hh):
            gi = m @ w_ih.T + b_ih
            gh = h @ w_hh.T + b_hh
            i_r, i_z, i_n = jnp.split(gi, 3, axis=-1)
            h_r, h_z, h_n = jnp.split(gh, 3, axis=-1)
            r = jax.nn.sigmoid(i_r + h_r)
            z = jax.nn.sigmoid(i_z + h_z)
            n = jnp.tanh(i_n + r * h_n)
            return (1.0 - z) * n + z * h
        A = (adj != 0).astype(x.dtype)
        h = x
        for l in range(weight.shape[0]):
            m = jnp.einsum('bnd,de->bne', h, weight[l])
            agg = jnp.einsum('bij,bid->bjd', A, m)
            h = _gru_cell(agg, h, w_ih, w_hh, b_ih, b_hh)
        return h * mask[..., None]

    def _L3_gnn_ref(x, mask, w_se, b_se, conv1_w, bn1_g, bn1_b, bn1_m, bn1_v, conv2_w, bn2_g, bn2_b, bn2_m, bn2_v, w_msg, b_msg, w_ih, b_ih, w_hh, b_hh):
        import jax, jax.numpy as jnp
        import numpy as np
        from jax import lax
        DIM = 128
        EPS = 1e-05

        def _bn(h, g, b, m, v):
            scale = g / jnp.sqrt(v + EPS)
            return h * scale[None, :, None] + (b - m * scale)[None, :, None]

        def _conv1d(h, w, pad):
            return lax.conv_general_dilated(h, w, window_strides=(1,), padding=[(pad, pad)], dimension_numbers=('NCH', 'OIH', 'NCH'))
        d = x.shape[-1]
        xc = jnp.transpose(x, (0, 2, 1))
        h = _bn(_conv1d(xc, conv1_w, 0), bn1_g, bn1_b, bn1_m, bn1_v)
        h = jax.nn.relu(h)
        h = _bn(_conv1d(h, conv2_w, 8), bn2_g, bn2_b, bn2_m, bn2_v)
        x_conv = jnp.transpose(jax.nn.relu(h + xc), (0, 2, 1))
        s = x @ w_se.T + b_se
        sq = jnp.sum(s * s, axis=-1)
        dist = sq[:, :, None] + sq[:, None, :] - 2.0 * jnp.einsum('bnd,bmd->bnm', s, s)
        A = jnp.exp(-dist) * mask
        msg = jax.nn.relu(x @ w_msg.T + b_msg)
        x_nmp = jnp.einsum('bnm,bmd->bnd', A, msg)
        x_in = jnp.concatenate([x_conv, x_nmp], axis=-1)
        gi = x_in @ w_ih.T + b_ih
        gh = x @ w_hh.T + b_hh
        gi_r, gi_z, gi_n = (gi[..., :d], gi[..., d:2 * d], gi[..., 2 * d:])
        gh_r, gh_z, gh_n = (gh[..., :d], gh[..., d:2 * d], gh[..., 2 * d:])
        r = jax.nn.sigmoid(gi_r + gh_r)
        z = jax.nn.sigmoid(gi_z + gh_z)
        nn_ = jnp.tanh(gi_n + r * gh_n)
        return (1.0 - z) * nn_ + z * x
    h = jnp.maximum(_layernorm(x, axis=-1), 0.0)
    x = x + _L0_gnn_ref(h, adj, L0_gnn_fc_w, L0_gnn_fc_b, L0_gnn_q_w, L0_gnn_q_b, L0_gnn_k_w, L0_gnn_k_b, L0_gnn_fp_w, L0_gnn_fp_b)
    h = jnp.maximum(_layernorm(x, axis=-1), 0.0)
    x = x + _L1_gnn_ref(h, adj, L1_gnn_W_w, L1_gnn_W_b, L1_gnn_A, L1_gnn_gate_w, L1_gnn_gate_b, 1)
    h = jnp.maximum(_layernorm(x, axis=-1), 0.0)
    x = x + _L2_gnn_ref(h, adj, nodemask, L2_gnn_weight, L2_gnn_w_ih, L2_gnn_w_hh, L2_gnn_b_ih, L2_gnn_b_hh)
    h = jnp.maximum(_layernorm(x, axis=-1), 0.0)
    x = x + _L3_gnn_ref(h, adj, L3_gnn_w_se, L3_gnn_b_se, L3_gnn_conv1_w, L3_gnn_bn1_g, L3_gnn_bn1_b, L3_gnn_bn1_m, L3_gnn_bn1_v, L3_gnn_conv2_w, L3_gnn_bn2_g, L3_gnn_bn2_b, L3_gnn_bn2_m, L3_gnn_bn2_v, L3_gnn_w_msg, L3_gnn_b_msg, L3_gnn_w_ih, L3_gnn_b_ih, L3_gnn_w_hh, L3_gnn_b_hh)
    return x

_drawn_inputs = setup_inputs


def setup_inputs(seed=0):
    import zlib

    import numpy as np

    out = dict(_drawn_inputs(seed))
    spreads = {'L0_gnn_fc_b': (0.0, 0.492),
     'L0_gnn_fp_b': (0.0, 0.487),
     'L3_gnn_b_se': (0.0, 2.0),
     'L3_gnn_bn1_g': (1.0, 0.6),
     'L3_gnn_bn1_b': (0.0, 0.549),
     'L3_gnn_bn1_m': (0.0, 0.466),
     'L3_gnn_bn1_v': (1.0, 0.6),
     'L3_gnn_bn2_g': (1.0, 0.6),
     'L3_gnn_bn2_b': (0.0, 0.8),
     'L3_gnn_bn2_m': (0.0, 0.8),
     'L3_gnn_bn2_v': (1.0, 0.6),
     'L3_gnn_b_msg': (0.0, 1.149),
     'L3_gnn_b_ih': (0.0, 0.394),
     'L3_gnn_b_hh': (0.0, 0.559)}
    factors = {'L0_gnn_q_w': 7.475,
     'L0_gnn_k_w': 3.818,
     'L1_gnn_W_b': 5.268,
     'L1_gnn_A': 3.163,
     'L2_gnn_b_hh': 3.309,
     'L3_gnn_w_se': 15.059}
    for name, (base, spread) in spreads.items():
        noise = np.random.default_rng([zlib.crc32(name.encode()), seed]).standard_normal(out[name].shape)
        drawn = base * np.exp(spread * noise) if base else spread * noise
        out[name] = jnp.asarray(drawn.astype(out[name].dtype))
    for name, factor in factors.items():
        out[name] = (out[name] * factor).astype(out[name].dtype)
    return out
```

```python
import numpy as np
import concourse.bass as bass
from concourse import mybir
from contextlib import ExitStack

F32 = mybir.dt.float32
F32R = mybir.dt.float32r
ALU = mybir.AluOpType
ACT = mybir.ActivationFunctionType

GRAPHS, NODES, DIM = 16, 512, 128
P = 128
TILES = NODES // P
SLOTS = 2
ROUNDS = GRAPHS // SLOTS
HEADS = 8
LAYERS2 = 5
TAPS = 17
PAD = TAPS // 2
EPS = 1e-5
NEG0 = -1000000000.0
NEG1 = -9000000000000000.0

WIDTHS = [("WI2", LAYERS2 * 3 * DIM), ("c2", TAPS * DIM), ("M", HEADS * DIM), ("hh2", 3 * DIM), ("Ww", DIM), ("As", DIM),
          ("c1", DIM), ("msg", DIM), ("ih3c", 3 * DIM), ("ih3n", 3 * DIM), ("hh3", 3 * DIM)]
WCOL = {}
_at = 0
for _name, _width in WIDTHS:
    WCOL[_name] = _at
    _at += _width
WALL = _at
WFIRST = WCOL["M"]

COLS = (["fcb%d" % h for h in range(HEADS)] + ["qw", "kw", "fpb", "Wb", "gateb", "qb", "kb",
        "bih2r", "bih2z", "bih2n", "bhh2r", "bhh2z", "bhh2n", "v1", "v2", "g1", "g2", "b1", "b2", "m1", "m2",
        "bih3r", "bih3z", "bih3n", "bhh3r", "bhh3z", "bhh3n", "gw1", "gw2",
        "se0", "se1", "se2", "se3", "se4", "bse", "e3", "e4"])
CI = {n: i for i, n in enumerate(COLS)}
DCOLS = ["rz2r", "rz2z", "hn2", "rz3r", "rz3z", "hn3", "s1", "s2", "sh1", "sh2", "gb", "bias2", "bias1", "qkw",
         "t1", "t2", "r1", "r2", "tq"]
DI = {n: i for i, n in enumerate(DCOLS)}

PER = {
    "stats": 1, "aggregated": 1, "variance": 1, "rstd": 1, "normed": 1, "h_banked": 1, "h_high": 2, "h_low": 1,
    "y_banked": 1, "residual": 1,
    "mask0": 1, "qk_banked": 1, "qk": 1, "q99": 1, "g_banked": 8, "g_act": 4, "g_dve": 4,
    "kb_banked": 1, "masked": 4, "relu": 4, "lifted": 4, "kmax_q": 1, "neg_max": 1, "exp_bias": 1, "exped": 4,
    "pt_banked": 4, "pt_dve": 3, "pt_act": 1,
    "rden": 1, "o_banked": 1, "o_added": 1,
    "acc_start": 1, "x_half": 1, "tanh0": 1,
    "mask1": 1, "h1_banked": 1, "h1_high": 2, "h1_low": 1, "t1_banked": 1, "t1_high": 1, "t1_low": 1, "h1n_banked": 1,
    "s_banked": 4, "s_masked": 4, "s_negmax": 4, "s_exped": 4, "att": 4, "rden1": 1, "h1_scaled": 1, "hp_banked": 1,
    "hp": 1, "gate_banked": 1, "gate": 1, "h_less_hp": 1, "gate_e": 1, "y1": 1,
    "adjacency": 1,
    "hn_rows": 1, "rows_high": 1, "rows_low": 1, "agg_banked": 1, "agg_high": 1, "agg_low": 1,
    "hn_banked": 1, "r_banked": 1, "z_banked": 1, "in_banked": 1, "hn": 1, "r": 1, "z": 1, "cand_a": 1, "cand_b": 1,
    "cand": 1, "zh": 1, "z_rest": 1, "z_cand": 1, "h_new": 1, "h_new_high": 1, "h_new_low": 1,
    "c1_banked": 1, "c1_high": 2, "c1_low": 1, "s3_banked": 1, "sq3": 1, "aug_banked": 2, "aug": 2, "msg_banked": 1,
    "msg": 1, "dist_banked": 4, "dist_exped": 4, "weights3": 4, "c2_banked": 1, "c2_scaled": 1, "xc_high": 2,
    "xc_low": 1, "nmp_banked": 1, "nmp_high": 1, "nmp_low": 1,
}


ALTERNATING = {"s_banked", "s_masked", "s_negmax", "s_exped", "att", "dist_banked", "dist_exped", "weights3"}


def build(nc, x, adj, adjt, nmask, c2w, wraw, prew, fcw, fpw, cols_d, rows_d, out):
    with ExitStack() as ctx:
        def sb(name, shape, dt=F32):
            return ctx.enter_context(nc.sbuf_tensor(name, shape, dt))

        def sem(name):
            return ctx.enter_context(nc.semaphore(name))

        SL = range(SLOTS)
        WH = sb("WH", [P, WALL], F32R)
        WLO = sb("WLO", [P, WALL], F32R)
        VQH = sb("VQH", [P, 2 * HEADS], F32R)
        VQL = sb("VQL", [P, 2 * HEADS], F32R)
        VQ = sb("VQ", [P, 2 * HEADS])
        CQ = sb("CQ", [P, 2 * HEADS])
        ident = sb("ident", [P, P])
        cols = sb("cols", [P, len(COLS)])
        dcols = sb("dcols", [P, len(DCOLS)])
        se2 = sb("se2", [P, 5])
        neg5 = sb("neg5", [5, 2, 5])
        ob = sb("ob", [P, DIM])
        rows = sb("rows", [1, 2, P])
        mhalf = sb("mhalf", [P, TILES])
        adjN = [sb(f"adjN{s}", [P, TILES, NODES]) for s in SL]
        adjT = [sb(f"adjT{s}", [P, TILES, NODES]) for s in SL]
        U = [sb(f"U{s}", [P, TILES, NODES]) for s in SL]
        AN = []
        PT = []
        for s in SL:
            with nc.sbuf_tensor(f"PT{s}", [P, TILES, NODES], F32) as pt:
                PT.append(pt)
            AN.append(sb(f"AN{s}", [P, TILES, NODES], F32R))
        F = [sb(f"F{s}", [P, 8, NODES]) for s in SL]
        G = [F[s][:, :, :].rearrange("p (t a) n -> p t (a n)", a=2) for s in SL]
        HS = [sb(f"HS{s}", [P, 2, NODES], F32R) for s in SL]
        R, tiles = [], []
        for s in SL:
            with nc.sbuf_tensor(f"tiles{s}", [P, TILES, NODES], F32) as t:
                tiles.append(t)
            R.append(sb(f"R{s}", [P, TILES, NODES], F32R))
        RELU = tiles[0]
        SC = [U[0], U[1], tiles[1]]
        C1, acc, Y = [], [], []
        for s in SL:
            with nc.sbuf_tensor(f"accY{s}", [P, 2, NODES], F32) as t:
                acc.append(t[:, 0, :])
                Y.append(t[:, 1, :])
            C1.append(sb(f"C1{s}", [P, 2, NODES + 2 * PAD], F32R))
        HT = [sb(f"HT{s}", [P, NODES]) for s in SL]
        hN = [sb(f"hN{s}", [P, NODES]) for s in SL]
        X = [sb(f"X{s}", [P, TILES, DIM]) for s in SL]
        xin = [sb(f"xin{s}", [P, TILES, DIM]) for s in SL]
        nm = [sb(f"nm{s}", [P, TILES]) for s in SL]
        QK = [sb(f"QK{s}", [P, TILES, 2 * HEADS]) for s in SL]
        Q99 = [sb(f"Q99{s}", [P, TILES, HEADS]) for s in SL]
        bst = [sb(f"bst{s}", [P, TILES, 6]) for s in SL]
        mv = [sb(f"mv{s}", [P, TILES, 2]) for s in SL]
        var = [sb(f"var{s}", [P, TILES]) for s in SL]
        rstd = [sb(f"rstd{s}", [P, TILES]) for s in SL]
        kmax = [sb(f"kmax{s}", [P, TILES]) for s in SL]
        kq = [sb(f"kq{s}", [P, TILES]) for s in SL]
        nmx = [sb(f"nmx{s}", [P, TILES]) for s in SL]
        den = [sb(f"den{s}", [P, TILES]) for s in SL]
        rden = [sb(f"rden{s}", [P, TILES]) for s in SL]
        B = [ctx.enter_context(nc.psum_tensor(f"banks{s}", [P, 4, 512], F32)) for s in SL]

        S = {name: sem(name) for name in PER}
        loaded = {n: [sem(f"{n}_loaded{s}") for s in SL] for n in ("xin", "adjN", "adjT", "nmask")}
        x_free = [sem(f"x_free{s}") for s in SL]
        w_loaded = sem("w_loaded")
        ones_ready = sem("ones_ready")
        ident_ready = sem("ident_ready")
        setup_dve = sem("setup_dve")
        setup_pool = sem("setup_pool")
        setup_pe = sem("setup_pe")
        setup_act = sem("setup_act")
        w_split = sem("w_split")

        def after(name, turn, s, k=None):
            n = PER[name]
            k = n if k is None else k
            return S[name], turn * (SLOTS * n) + (SLOTS * (k - 1) + s + 1 if name in ALTERNATING else s * n + k)

        def tile_out(turn, s, j):
            return after("pt_act", turn, s) if j == TILES - 1 else after("pt_dve", turn, s, j + 1)

        def col(name):
            return cols[:, CI[name]:CI[name] + 1]

        def dcol(name):
            return dcols[:, DI[name]:DI[name] + 1]

        def part(t):
            return slice(t * P, (t + 1) * P)

        stage = [F[s][:, :, :].rearrange("p t n -> p (t n)") for s in SL]
        HH = [HS[s][:, 0, :] for s in SL]
        HL = [HS[s][:, 1, :] for s in SL]

        tick_dve = sb("tick_dve", [P, 2 + TILES, SLOTS])
        tick_pool = sb("tick_pool", [P, SLOTS])

        WI2_BANKS = [(1, 1), (1, 2), (1, 3), (1, 0), (0, 3)]

        block = ctx.enter_context(nc.Block())

        @block.sync
        def _(sp):
            def load(dst, src, signal):
                sp.dma_start(dst, src).then_inc(signal, 16)

            def nodes(t, g):
                return t[bass.ds(g, 1), :, :].rearrange("g (t p) n -> p (g t) n", p=P)

            load(cols[:, :], cols_d, w_loaded)
            load(rows[:, :, :], rows_d, w_loaded)
            load(U[0][:, 0:2, :].rearrange("p t n -> p (t n)"), fcw, w_loaded)
            load(U[1][:, 0:2, :].rearrange("p t n -> p (t n)"), fpw, w_loaded)
            load(U[0][:, 2:4, :].rearrange("p t n -> p (t n)"), prew, w_loaded)
            load(stage[0][:, WCOL["c2"]:WFIRST], c2w, w_loaded)
            load(stage[1][:, HEADS * DIM:WALL - WFIRST], wraw[:, 0:WALL - WFIRST - HEADS * DIM], w_loaded)
            load(xin[1][:, 0, :], wraw[:, WALL - WFIRST - HEADS * DIM:WALL - WFIRST - HEADS * DIM + DIM], w_loaded)
            sp.wait_ge(setup_dve, 2)
            for s in SL:
                load(xin[s][:, :, :], nodes(x, s), loaded["xin"][s])
                load(adjN[s][:, :, :], nodes(adj, s), loaded["adjN"][s])
                load(adjT[s][:, :, :], nodes(adjt, s), loaded["adjT"][s])
                load(nm[s][:, :], nmask[s, :, :], loaded["nmask"][s])

            def round_of(it, more):
                for s in SL:
                    sp.wait_ge(*after("masked", it * HEADS + HEADS - 1, s))
                    load(adjN[s][:, :, :], nodes(adj, it * SLOTS + s), loaded["adjN"][s])
                if more:
                    for s in SL:
                        sp.wait_ge(*after("x_half", it, s))
                        load(xin[s][:, :, :], nodes(x, it * SLOTS + (SLOTS + s)), loaded["xin"][s])
                    for s in SL:
                        sp.wait_ge(*after("adjacency", it, s))
                        load(adjN[s][:, :, :], nodes(adj, it * SLOTS + (SLOTS + s)), loaded["adjN"][s])
                    for s in SL:
                        sp.wait_ge(*after("residual", it * 4 + 2, s))
                        load(nm[s][:, :], nmask[bass.ds(it * SLOTS + (SLOTS + s), 1), :, :].rearrange("g p t -> p (g t)"),
                             loaded["nmask"][s])
                    for s in SL:
                        sp.wait_ge(*after("weights3", it, s))
                        load(adjT[s][:, :, :], nodes(adjt, it * SLOTS + (SLOTS + s)), loaded["adjT"][s])
                for s in SL:
                    sp.wait_ge(*after("residual", it * 4 + 3, s))
                    sp.dma_start(nodes(out, it * SLOTS + s), X[s][:, :, :]).then_inc(x_free[s], 16)

            with sp.Fori(0, ROUNDS - 1) as it:
                round_of(it, True)
            round_of(ROUNDS - 1, False)
            for s in SL:
                sp.wait_ge(x_free[s], 16 * (ROUNDS + 1))

        @block.gpsimd
        def _(pool):
            pool.memset(ident[:, :], 0.0).then_inc(ident_ready, 1)
            pool.memset(mhalf[:, :], -0.5)
            pool.memset(neg5[:, :, :], 0.0).then_inc(setup_pool, 1)
            pool.wait_ge(ident_ready, 1)
            pool.affine_select(out=ident[:, :], in_=ident[:, :], compare_op=ALU.not_equal, fill=1.0, base=0,
                               pattern=[[-1, P]], channel_multiplier=1).then_inc(ident_ready, 1)
            pool.wait_ge(setup_pool, 1)
            pool.memset(neg5[:, 0, 3:4], -1.0)
            pool.memset(neg5[:, 1, 4:5], -1.0).then_inc(setup_pool, 1)
            pool.wait_ge(setup_dve, 1)
            pool.tensor_tensor(dcols[:, DI["r1"]:DI["r1"] + 2], dcols[:, DI["t1"]:DI["t1"] + 2], mhalf[:, 0:2],
                               ALU.pow).then_inc(setup_pool, 1)

            UNITS = HEADS * SLOTS
            with pool.Fori(0, ROUNDS) as it:
                def rstd_of(s, layer):
                    turn = it * 4 + layer
                    pool.wait_ge(*after("variance", turn, s))
                    pool.tensor_tensor(rstd[s][:, :], var[s][:, :], mhalf[:, :], ALU.pow).then_inc(S["rstd"], 1)

                for s in SL:
                    rstd_of(s, 0)
                for s in SL:
                    pool.wait_ge(loaded["adjN"][s], it * 32 + 16)
                    pool.tensor_tensor(tick_pool[:, s:s + 1], mhalf[:, 0:1], mhalf[:, 0:1], ALU.add)
                    pool.tensor_scalar(adjN[s][:, :, :], adjN[s][:, :, :], -1.0, -NEG0, ALU.add, ALU.mult)\
                        .then_inc(S["mask0"], 1)
                def lift(u, t):
                    turn = it * HEADS + u // SLOTS
                    pool.wait_ge(*after("relu", turn, u % SLOTS, t + 1))
                    pool.tensor_tensor(SC[u % 3][:, t, :], SC[u % 3][:, t, :], RELU[:, t, :], ALU.add)\
                        .then_inc(S["lifted"], 1)

                for u in range(UNITS):
                    for t in range(TILES):
                        lift(u, t)
                for s in SL:
                    rstd_of(s, 1)
                for t in range(TILES):
                    for s in SL:
                        pool.wait_ge(*after("s_exped", it, s, t + 1))
                        pool.tensor_tensor(PT[s][:, t, :], U[s][:, t, :], adjT[s][:, t, :], ALU.mult)\
                            .then_inc(S["att"], 1)
                for s in SL:
                    rstd_of(s, 2)
                for layer in range(LAYERS2 - 1):
                    for s in SL:
                        pool.wait_ge(*after("h_new_high", it * (LAYERS2 - 1) + layer, s))
                        pool.tensor_tensor(HL[s], HT[s][:, :], HH[s].bitcast(F32), ALU.subtract)\
                            .then_inc(S["h_new_low"], 1)
                for s in SL:
                    rstd_of(s, 3)
                for t in range(TILES):
                    for s in SL:
                        pool.wait_ge(*after("dist_exped", it, s, t + 1))
                        pool.tensor_tensor(PT[s][:, t, :], U[s][:, t, :], adjT[s][:, t, :], ALU.mult)\
                            .then_inc(S["weights3"], 1)

        @block.tensor
        def _(pe):
            def mm3(dst, w, xs, start=True, stop=True):
                pe.matmul(dst, w[0], xs[0], start=start, stop=False)
                pe.matmul(dst, w[0], xs[1], start=False, stop=False)
                return pe.matmul(dst, w[1], xs[0], start=False, stop=stop)

            def W(name, j=0, n=DIM):
                a = WCOL[name] + j * DIM
                return WH[:, a:a + n], WLO[:, a:a + n]

            pe.wait_ge(w_loaded, 8 * 16)
            fcT = U[0][:, 0:2, :].rearrange("p t n -> p (t n)")
            fp = U[1][:, 0:2, :].rearrange("p t n -> p (t n)")
            for h in range(HEADS):
                pe.matmul(B[0][:, h // 4, (h % 4) * DIM:(h % 4 + 1) * DIM], fcT[:, part(h)], fp[:, part(h)])
            for h in range(HEADS):
                pe.matmul(B[0][:, 2, 2 * h:2 * h + 2], fcT[:, part(h)], cols[:, CI["qw"]:CI["qw"] + 2])
            pe.wait_ge(setup_dve, 2)
            pe.matmul(B[0][:, 3, 0:HEADS], dcol("qkw").broadcast_to([P, P]), cols[:, 0:HEADS])
            for h in range(HEADS):
                pe.matmul(B[1][:, 0, 0:DIM], cols[:, h:h + 1].broadcast_to([P, P]), fp[:, part(h)], start=(h == 0), stop=False)
            pe.wait_ge(ident_ready, 2)
            pe.matmul(B[1][:, 0, 0:DIM], col("fpb").broadcast_to([P, P]), ident[:, :], start=False, stop=True)
            pre = U[0][:, 2:4, :].rearrange("p t n -> p (t n)")
            for layer, (b, bank) in enumerate(WI2_BANKS):
                last = pe.matmul(B[b][:, bank, P:4 * P], pre[:, part(layer)], pre[:, LAYERS2 * DIM:(LAYERS2 + 3) * DIM])
            last.then_inc(setup_pe, 1)
            pe.wait_ge(w_split, 4)

            with pe.Fori(0, ROUNDS) as it:
                def transpose_in(s, layer):
                    pe.wait_ge(*after("normed", it * 4 + layer, s))
                    for t in range(TILES):
                        last = pe.transpose(B[s][:, 0, part(t)], hN[s][:, part(t)], ident[:, :])
                    last.then_inc(S["h_banked"], 1)

                def transpose_out(s, layer, y):
                    for t in range(TILES):
                        last = pe.transpose(B[s][:, 1, part(t)], y[:, part(t)], ident[:, :])
                    last.then_inc(S["y_banked"], 1)

                for s in SL:
                    transpose_in(s, 0)
                for s in SL:
                    pe.wait_ge(*after("h_low", it * 4, s))
                    for t in range(TILES):
                        last = mm3(B[s][:, 1, 16 * t:16 * t + 16], (HH[s][:, part(t)], HL[s][:, part(t)]),
                                   (VQH[:, :], VQL[:, :]))
                    last.then_inc(S["qk_banked"], 1)
                    for t in range(TILES):
                        for half in range(2):
                            if t >= 1:
                                pe.wait_ge(*after("g_dve" if half else "g_act", it, s, t))
                            mm3(B[s][:, 2 + half, :], (HH[s][:, part(t)], HL[s][:, part(t)]),
                                W("M", 4 * half, 4 * DIM)).then_inc(S["g_banked"], 1)

                def rows_of(s, bank, column):
                    for t in range(TILES):
                        last = pe.transpose(B[s][:, bank, part(t)], column(t).broadcast_to([P, P]), ident[:, :])
                    return last

                def key_rows(u):
                    h, s = u // SLOTS, u % SLOTS
                    if h == 0:
                        pe.wait_ge(*after("qk", it, s))
                    else:
                        pe.wait_ge(*after("masked", it * HEADS + h - 1, s))
                    rows_of(s, 0, lambda t: QK[s][:, t, HEADS + h:HEADS + h + 1]).then_inc(S["kb_banked"], 1)

                UNITS = HEADS * SLOTS
                key_rows(0)
                key_rows(1)
                for u in range(UNITS + 1):
                    if u + 2 < UNITS:
                        key_rows(u + 2)
                    for j in range(TILES):
                        if u < UNITS:
                            h, s = u // SLOTS, u % SLOTS
                            turn = it * HEADS + h
                            if j == 0:
                                pe.wait_ge(*after("exped", turn, s))
                            if j >= 2:
                                pe.wait_ge(*tile_out(turn, s, j - 2))
                            elif u >= 1:
                                pe.wait_ge(*tile_out(it * HEADS + (u - 1) // SLOTS, (u - 1) % SLOTS, j + 2))
                            for t in range(TILES):
                                last = pe.transpose(B[j % 2][:, 1, part(t)], SC[u % 3][:, t, part(j)], ident[:, :])
                            last.then_inc(S["pt_banked"], 1)
                        if 1 <= u <= UNITS:
                            h, s = (u - 1) // SLOTS, (u - 1) % SLOTS
                            turn = it * HEADS + h
                            if j == 0:
                                if h < 2:
                                    pe.wait_ge(*after("g_act", it, s))
                                    pe.wait_ge(*after("g_dve", it, s))
                                else:
                                    pe.wait_ge(*after("o_added", turn - 2, s))
                                pe.wait_ge(*tile_out(turn, s, TILES - 2))
                                pe.wait_ge(*tile_out(turn, s, TILES - 1))
                            for k in range(TILES):
                                last = pe.matmul(B[s][:, 2 + h % 2, part(j)], PT[s][:, k, part(j)],
                                                 G[s][:, k, h * DIM:(h + 1) * DIM], start=(k == 0), stop=(k == TILES - 1))
                            if j == TILES - 1:
                                last.then_inc(S["o_banked"], 1)

                for s in SL:
                    transpose_in(s, 1)
                for s in SL:
                    pe.wait_ge(*after("h_low", it * 4 + 1, s))
                    pe.wait_ge(*after("residual", it * 4, s))
                    mm3(B[s][:, 1, :], W("Ww"), (HH[s], HL[s])).then_inc(S["h1_banked"], 1)
                for s in SL:
                    pe.wait_ge(*after("h1_low", it, s))
                    mm3(B[s][:, 2, :], W("As"), (R[s][:, 0, :], R[s][:, 1, :])).then_inc(S["t1_banked"], 1)
                    for t in range(TILES):
                        last = pe.transpose(B[s][:, 3, part(t)], F[s][:, 0, part(t)], ident[:, :])
                    last.then_inc(S["h1n_banked"], 1)
                for t in range(TILES):
                    for s in SL:
                        if t == 0:
                            pe.wait_ge(*after("t1_low", it, s))
                        if t >= 2:
                            pe.wait_ge(*after("s_masked", it, s, t - 1))
                        mm3(B[s][:, t % 2, :], (R[s][:, 2, part(t)], R[s][:, 3, part(t)]),
                            (R[s][:, 0, :], R[s][:, 1, :])).then_inc(S["s_banked"], 1)
                for s in SL:
                    pe.wait_ge(*after("h1_scaled", it, s))
                    for t in range(TILES):
                        pe.wait_ge(*after("att", it, s, t + 1))
                        last = pe.matmul(B[s][:, 2, :], F[s][:, 1, part(t)], PT[s][:, t, :], start=(t == 0),
                                         stop=(t == TILES - 1))
                    last.then_inc(S["hp_banked"], 1)
                for s in SL:
                    pe.matmul(B[s][:, 3, :], col("gw1").broadcast_to([P, P]), HT[s][:, :], start=True, stop=False)
                    pe.wait_ge(*after("hp", it, s))
                    pe.matmul(B[s][:, 3, :], col("gw2").broadcast_to([P, P]), F[s][:, 2, :], start=False, stop=True)\
                        .then_inc(S["gate_banked"], 1)
                for s in SL:
                    pe.wait_ge(*after("y1", it, s))
                    transpose_out(s, 1, Y[s])

                for s in SL:
                    transpose_in(s, 2)
                for n in range(LAYERS2 * SLOTS + 1):
                    s, layer = n % SLOTS, n // SLOTS
                    o, before = (n - 1) % SLOTS, (n - 1) // SLOTS
                    turn = it * LAYERS2 + layer
                    h, agg, agg_o = (HH[s], HL[s]), (R[s][:, 2, :], R[s][:, 3, :]), (R[o][:, 2, :], R[o][:, 3, :])
                    if n < LAYERS2 * SLOTS:
                        if layer == 0:
                            pe.wait_ge(*after("h_high", it * 4 + 2, s))
                        else:
                            pe.wait_ge(*after("h_new", it * (LAYERS2 + 1) + layer - 1, s))
                        for t in range(TILES):
                            last = pe.transpose(B[s][:, 0, part(t)], HT[s][:, part(t)], ident[:, :])
                        last.then_inc(S["hn_rows"], 1)
                    if n >= 1:
                        mm3(B[o][:, 0, :], W("WI2", 3 * before + 1), agg_o, start=False).then_inc(S["z_banked"], 1)
                    if n < LAYERS2 * SLOTS:
                        if layer == 0:
                            pe.wait_ge(*after("h_low", it * 4 + 2, s))
                        else:
                            pe.wait_ge(*after("h_new_low", it * (LAYERS2 - 1) + layer - 1, s))
                        mm3(B[s][:, 2, :], W("hh2", 0), h, stop=False)
                        pe.wait_ge(*after("rows_low", turn, s))
                        pe.wait_ge(*after("adjacency", it, s))
                        for t in range(TILES):
                            for k in range(2):
                                last = pe.matmul(B[s][:, 1, :], R[s][:, k, part(t)], AN[s][:, t, :],
                                                 start=(t == 0 and k == 0), stop=(t == TILES - 1 and k == 1))
                        last.then_inc(S["agg_banked"], 1)
                        mm3(B[s][:, 3, :], W("hh2", 2), h).then_inc(S["hn_banked"], 1)
                        mm3(B[s][:, 0, :], W("hh2", 1), h, stop=False)
                        pe.wait_ge(*after("agg_low", turn, s))
                        mm3(B[s][:, 2, :], W("WI2", 3 * layer), agg, start=False).then_inc(S["r_banked"], 1)
                        mm3(B[s][:, 1, :], W("WI2", 3 * layer + 2), agg).then_inc(S["in_banked"], 1)
                for s in SL:
                    pe.wait_ge(*after("h_new", it * (LAYERS2 + 1) + LAYERS2 - 1, s))
                    transpose_out(s, 2, HT[s])

                for s in SL:
                    transpose_in(s, 3)
                for s in SL:
                    pe.wait_ge(*after("h_low", it * 4 + 3, s))
                    pe.wait_ge(*after("residual", it * 4 + 2, s))
                    mm3(B[s][:, 1, :], W("c1"), (HH[s], HL[s])).then_inc(S["c1_banked"], 1)
                    pe.matmul(B[s][0:5, 2, :], cols[:, CI["se0"]:CI["se0"] + 5], HT[s][:, :])\
                        .then_inc(S["s3_banked"], 1)
                    for t in range(TILES):
                        mm3(B[s][:, 3, part(t)], (HH[s][:, part(t)], HL[s][:, part(t)]), W("msg"), stop=False)
                        last = pe.matmul(B[s][:, 3, part(t)], rows[0:1, 1, :], rows[0:1, 0, :], start=False, stop=True)
                    last.then_inc(S["msg_banked"], 1)
                for s in SL:
                    pe.wait_ge(*after("sq3", it, s))
                    pe.matmul(B[s][0:5, 0, :], se2[:, :], HT[s][:, :], start=True, stop=False)
                    pe.matmul(B[s][0:5, 2, :], neg5[:, 1, :], F[s][0:5, 2, :], start=False, stop=True,
                              skip_group_check=True).then_inc(S["aug_banked"], 1)
                    pe.matmul(B[s][0:5, 0, :], neg5[:, 0, :], F[s][0:5, 2, :], start=False, stop=True)\
                        .then_inc(S["aug_banked"], 1)
                for t in range(TILES):
                    for s in SL:
                        if t == 0:
                            pe.wait_ge(*after("aug", it, s))
                            pe.wait_ge(*after("c1_low", it, s))
                        if t >= 2:
                            pe.wait_ge(*after("dist_exped", it, s, t - 1))
                        pe.matmul(B[s][:, t % 2, :], F[s][0:5, 1, part(t)], F[s][0:5, 0, :])\
                            .then_inc(S["dist_banked"], 1)
                for s in SL:
                    for k in range(TAPS):
                        last = mm3(B[s][:, 2, :], W("c2", k), (C1[s][:, 0, k:k + NODES], C1[s][:, 1, k:k + NODES]),
                                   start=(k == 0), stop=(k == TAPS - 1))
                    last.then_inc(S["c2_banked"], 1)
                    pe.wait_ge(*after("msg", it, s))
                    for t in range(TILES):
                        pe.wait_ge(*after("weights3", it, s, t + 1))
                        last = pe.matmul(B[s][:, 3, :], F[s][:, 7, part(t)], PT[s][:, t, :], start=(t == 0),
                                         stop=(t == TILES - 1))
                    last.then_inc(S["nmp_banked"], 1)
                for s in SL:
                    h, c, n = (HH[s], HL[s]), (R[s][:, 0, :], R[s][:, 1, :]), (R[s][:, 2, :], R[s][:, 3, :])
                    pe.wait_ge(*after("dist_exped", it, s))
                    mm3(B[s][:, 0, :], W("hh3", 0), h, stop=False)
                    mm3(B[s][:, 1, :], W("hh3", 1), h, stop=False)
                    pe.wait_ge(*after("xc_low", it, s))
                    mm3(B[s][:, 2, :], W("hh3", 2), h).then_inc(S["hn_banked"], 1)
                    mm3(B[s][:, 0, :], W("ih3c", 0), c, start=False, stop=False)
                    mm3(B[s][:, 1, :], W("ih3c", 1), c, start=False, stop=False)
                    pe.wait_ge(*after("nmp_low", it, s))
                    mm3(B[s][:, 0, :], W("ih3n", 0), n, start=False).then_inc(S["r_banked"], 1)
                    mm3(B[s][:, 3, :], W("ih3c", 2), c, stop=False)
                    mm3(B[s][:, 3, :], W("ih3n", 2), n, start=False).then_inc(S["in_banked"], 1)
                    mm3(B[s][:, 1, :], W("ih3n", 1), n, start=False).then_inc(S["z_banked"], 1)
                for s in SL:
                    pe.wait_ge(*after("h_new", it * (LAYERS2 + 1) + LAYERS2, s))
                    transpose_out(s, 3, Y[s])

        @block.scalar
        def _(act):
            act.wait_ge(w_loaded, 8 * 16)
            act.wait_ge(setup_dve, 3)
            act.activation(WH[:, 0:WFIRST], stage[0], ACT.Copy).then_inc(w_split, 1)
            act.activation(WH[:, WFIRST:WALL], stage[1][:, 0:WALL - WFIRST], ACT.Copy).then_inc(w_split, 1)
            act.activation(VQH[:, :], VQ[:, :], ACT.Copy).then_inc(setup_act, 1)
            act.wait_ge(setup_dve, 7)

            with act.Fori(0, ROUNDS) as it:
                def h_high(s, layer):
                    act.wait_ge(*after("h_banked", it * 4 + layer, s))
                    act.activation(HT[s][:, :], B[s][:, 0, :], ACT.Relu).then_inc(S["h_high"], 1)
                    act.activation(HH[s], B[s][:, 0, :], ACT.Relu).then_inc(S["h_high"], 1)

                for s in SL:
                    h_high(s, 0)
                for s in SL:
                    for t in range(TILES):
                        act.wait_ge(*after("g_banked", it, s, 2 * t + 1))
                        act.activation(G[s][:, t, 0:4 * DIM], B[s][:, 2, :], ACT.Copy).then_inc(S["g_act"], 1)

                def relu(u, t):
                    h, s = u // SLOTS, u % SLOTS
                    act.wait_ge(*after("masked", it * HEADS + h, s, t + 1))
                    if u >= 1:
                        act.wait_ge(*after("lifted", it * HEADS + (u - 1) // SLOTS, (u - 1) % SLOTS, t + 1))
                    act.activation(RELU[:, t, :], SC[u % 3][:, t, :], ACT.Relu, bias=Q99[s][:, t, h:h + 1], scale=99.0)\
                        .then_inc(S["relu"], 1)

                def softmax_exp(u, t):
                    h, s = u // SLOTS, u % SLOTS
                    turn = it * HEADS + h
                    if t == 0:
                        act.wait_ge(*after("exp_bias", turn, s))
                    act.wait_ge(*after("lifted", turn, s, t + 1))
                    act.activation(SC[u % 3][:, t, :], SC[u % 3][:, t, :], ACT.Exp, bias=nmx[s][:, t:t + 1], scale=0.01,
                                   accum_out=den[s][:, t:t + 1]).then_inc(S["exped"], 1)

                def tile_copy(u, j):
                    h, s = u // SLOTS, u % SLOTS
                    turn = it * HEADS + h
                    if h >= 1:
                        act.wait_ge(*after("o_banked", turn - 1, s))
                    act.wait_ge(*after("pt_banked", turn, s, j + 1))
                    act.activation(PT[s][:, j, :], B[j % 2][:, 1, :], ACT.Copy).then_inc(S["pt_act"], 1)

                UNITS = HEADS * SLOTS
                for u in range(-1, UNITS + 1):
                    for t in range(TILES):
                        if u + 1 < UNITS:
                            relu(u + 1, t)
                        if 0 <= u < UNITS:
                            softmax_exp(u, t)
                        if t == TILES - 1 and 0 <= u - 1 < UNITS:
                            tile_copy(u - 1, t)
                for s in SL:
                    act.wait_ge(*after("o_added", it * HEADS + HEADS - 1, s))
                    act.activation(Y[s], acc[s], ACT.Tanh, scale=0.5).then_inc(S["tanh0"], 1)

                for s in SL:
                    h_high(s, 1)
                for s in SL:
                    act.wait_ge(*after("h1_banked", it, s))
                    act.activation(F[s][:, 0, :], B[s][:, 1, :], ACT.Identity, bias=col("Wb")).then_inc(S["h1_high"], 1)
                    act.activation(R[s][:, 0, :], B[s][:, 1, :], ACT.Identity, bias=col("Wb")).then_inc(S["h1_high"], 1)
                for s in SL:
                    act.wait_ge(*after("t1_banked", it, s))
                    act.activation(R[s][:, 2, :], B[s][:, 2, :], ACT.Copy).then_inc(S["t1_high"], 1)
                for t in range(TILES):
                    for s in SL:
                        act.wait_ge(*after("s_negmax", it, s, t + 1))
                        act.activation(U[s][:, t, :], U[s][:, t, :], ACT.Exp, bias=nmx[s][:, t:t + 1],
                                       accum_out=den[s][:, t:t + 1]).then_inc(S["s_exped"], 1)
                for s in SL:
                    act.wait_ge(*after("hp_banked", it, s))
                    act.activation(F[s][:, 2, :], B[s][:, 2, :], ACT.Relu).then_inc(S["hp"], 1)
                for s in SL:
                    act.wait_ge(*after("gate_banked", it, s))
                    act.activation(F[s][:, 3, :], B[s][:, 3, :], ACT.Tanh, bias=dcol("gb"), scale=0.5)\
                        .then_inc(S["gate"], 1)

                def gate_act(s, cell, signal, bank, tile, bias, func):
                    act.wait_ge(*after(signal + "_banked", cell, s))
                    act.activation(F[s][:, tile, :], B[s][:, bank, :], func, bias=dcol(bias), scale=0.5)\
                        .then_inc(S[signal], 1)

                def cand_act(s, cell, bias):
                    act.wait_ge(*after("cand_b", cell, s))
                    act.activation(F[s][:, 4, :], F[s][:, 3, :], ACT.Tanh, bias=col(bias)).then_inc(S["cand"], 1)

                for s in SL:
                    h_high(s, 2)
                for n in range(LAYERS2 * SLOTS + 1):
                    s, layer = n % SLOTS, n // SLOTS
                    o, before = (n - 1) % SLOTS, (n - 1) // SLOTS
                    turn, cell = it * LAYERS2 + layer, it * (LAYERS2 + 1) + layer
                    cell_o = it * (LAYERS2 + 1) + before
                    start, end = n < LAYERS2 * SLOTS, n >= 1
                    if start:
                        act.wait_ge(*after("hn_rows", turn, s))
                        act.activation(R[s][:, 0, :], B[s][:, 0, :], ACT.Copy).then_inc(S["rows_high"], 1)
                    if end:
                        gate_act(o, cell_o, "z", 0, 1, "rz2z", ACT.Tanh)
                        cand_act(o, cell_o, "bih2n")
                    if start:
                        act.wait_ge(*after("agg_banked", turn, s))
                        act.activation(R[s][:, 2, :], B[s][:, 1, :], ACT.Copy).then_inc(S["agg_high"], 1)
                        gate_act(s, cell, "hn", 3, 2, "hn2", ACT.Identity)
                    if end and before < LAYERS2 - 1:
                        act.wait_ge(*after("h_new", cell_o, o))
                        act.activation(HH[o], HT[o][:, :], ACT.Copy).then_inc(S["h_new_high"], 1)
                    if start:
                        gate_act(s, cell, "r", 2, 0, "rz2r", ACT.Tanh)

                for s in SL:
                    h_high(s, 3)
                for s in SL:
                    act.wait_ge(*after("c1_banked", it, s))
                    act.activation(F[s][:, 6, :], B[s][:, 1, :], ACT.Relu, bias=dcol("sh1"), scale=dcol("s1"))\
                        .then_inc(S["c1_high"], 1)
                    act.activation(C1[s][:, 0, PAD:PAD + NODES], B[s][:, 1, :], ACT.Relu, bias=dcol("sh1"),
                                   scale=dcol("s1")).then_inc(S["c1_high"], 1)
                    act.wait_ge(*after("s3_banked", it, s))
                    act.activation(F[s][0:5, 2, :], B[s][0:5, 2, :], ACT.Square, bias=cols[0:5, CI["bse"]:CI["bse"] + 1])\
                        .then_inc(S["sq3"], 1)
                    act.wait_ge(*after("msg_banked", it, s))
                    act.activation(F[s][:, 7, :], B[s][:, 3, :], ACT.Relu).then_inc(S["msg"], 1)
                for s in SL:
                    act.wait_ge(*after("aug_banked", it, s, 1))
                    act.activation(F[s][0:5, 0, :], B[s][0:5, 2, :], ACT.Identity,
                                   bias=dcols[0:5, DI["bias2"]:DI["bias2"] + 1]).then_inc(S["aug"], 1)
                    act.wait_ge(*after("aug_banked", it, s, 2))
                    act.activation(F[s][0:5, 1, :], B[s][0:5, 0, :], ACT.Identity,
                                   bias=dcols[0:5, DI["bias1"]:DI["bias1"] + 1]).then_inc(S["aug"], 1)
                for t in range(TILES):
                    for s in SL:
                        act.wait_ge(*after("dist_banked", it, s, t + 1))
                        act.activation(U[s][:, t, :], B[s][:, t % 2, :], ACT.Exp).then_inc(S["dist_exped"], 1)
                for s in SL:
                    act.wait_ge(*after("c2_scaled", it, s))
                    act.activation(F[s][:, 4, :], F[s][:, 3, :], ACT.Relu, bias=dcol("sh2")).then_inc(S["xc_high"], 1)
                    act.activation(R[s][:, 0, :], F[s][:, 3, :], ACT.Relu, bias=dcol("sh2")).then_inc(S["xc_high"], 1)
                    act.wait_ge(*after("nmp_banked", it, s))
                    act.activation(R[s][:, 2, :], B[s][:, 3, :], ACT.Copy).then_inc(S["nmp_high"], 1)
                for s in SL:
                    cell = it * (LAYERS2 + 1) + LAYERS2
                    gate_act(s, cell, "hn", 2, 2, "hn3", ACT.Identity)
                    gate_act(s, cell, "r", 0, 0, "rz3r", ACT.Tanh)
                    gate_act(s, cell, "z", 1, 1, "rz3z", ACT.Tanh)
                    cand_act(s, cell, "bih3n")

        @block.vector
        def _(dve):
            for s in SL:
                dve.memset(X[s][:, :, :], 0.0).then_inc(x_free[s], 16)
            dve.wait_ge(w_loaded, 8 * 16)

            def c2(a, n=1):
                return cols[:, CI[a]:CI[a] + n]

            def d2(a, n=1):
                return dcols[:, DI[a]:DI[a] + n]

            dve.tensor_scalar(d2("t1", 2), c2("v1", 2), EPS, None, ALU.add).then_inc(setup_dve, 1)
            dve.tensor_tensor(d2("qkw"), c2("qw"), c2("kw"), ALU.add)
            for l in "23":
                dve.tensor_tensor(d2(f"rz{l}r", 2), c2(f"bih{l}r", 2), c2(f"bhh{l}r", 2), ALU.add)
                dve.tensor_scalar(d2(f"hn{l}"), c2(f"bhh{l}n"), 0.5, None, ALU.mult)
            dve.tensor_scalar(d2("gb"), c2("gateb"), 0.5, None, ALU.mult)
            dve.tensor_tensor(d2("bias2"), c2("bse"), c2("e3"), ALU.add)
            dve.tensor_scalar(se2[:, :], c2("se0", 5), 2.0, None, ALU.mult)
            dve.tensor_tensor(d2("tq"), c2("qb"), c2("kb"), ALU.add)
            asym = stage[1][:, WCOL["As"] - WFIRST:WCOL["As"] - WFIRST + DIM]
            dve.tensor_tensor(asym, asym, xin[1][:, 0, :], ALU.add)
            dve.scalar_tensor_tensor(d2("bias1"), c2("bse"), 2.0, c2("e4"), ALU.mult, ALU.add).then_inc(setup_dve, 1)
            dve.wait_ge(setup_dve, 2)
            for l in "23":
                dve.tensor_scalar(d2(f"rz{l}r", 2), d2(f"rz{l}r", 2), 0.5, None, ALU.mult)
            dve.wait_ge(setup_pe, 1)
            dve.tensor_copy(F[1][:, 0:2, :], B[0][:, 0:2, :])
            for layer, (b, bank) in enumerate(WI2_BANKS):
                dve.tensor_copy(stage[0][:, layer * 3 * DIM:(layer + 1) * 3 * DIM], B[b][:, bank, P:4 * P])
            dve.tensor_copy(VQ[:, :].rearrange("p (a h) -> p a h", a=2), B[0][:, 2, 0:2 * HEADS].rearrange("p (h a) -> p a h", a=2)).then_inc(setup_dve, 1)
            dve.memset(CQ[:, :], 0.0).then_inc(setup_dve, 1)
            dve.wait_ge(setup_dve, 4)
            dve.tensor_scalar(CQ[:, 0:HEADS], B[0][:, 3, 0:HEADS], d2("tq"), None, ALU.add)
            dve.tensor_copy(ob[:, :], B[1][:, 0, 0:DIM])
            dve.wait_ge(setup_pool, 3)
            dve.tensor_tensor(d2("s1", 2), c2("g1", 2), d2("r1", 2), ALU.mult).then_inc(setup_dve, 1)
            dve.wait_ge(setup_dve, 5)
            dve.tensor_tensor(d2("t1", 2), c2("m1", 2), d2("s1", 2), ALU.mult).then_inc(setup_dve, 1)
            dve.wait_ge(w_split, 1)
            dve.tensor_tensor(WLO[:, 0:WFIRST], stage[0], WH[:, 0:WFIRST].bitcast(F32),
                              ALU.subtract).then_inc(w_split, 1)
            dve.wait_ge(setup_dve, 6)
            dve.tensor_tensor(d2("sh1", 2), c2("b1", 2), d2("t1", 2), ALU.subtract)
            dve.wait_ge(setup_act, 1)
            dve.tensor_tensor(VQL[:, :], VQ[:, :], VQH[:, :].bitcast(F32), ALU.subtract).then_inc(setup_dve, 1)
            dve.wait_ge(w_split, 3)
            dve.tensor_tensor(WLO[:, WFIRST:WALL], stage[1][:, 0:WALL - WFIRST],
                              WH[:, WFIRST:WALL].bitcast(F32), ALU.subtract).then_inc(w_split, 1)

            with dve.Fori(0, ROUNDS) as it:
                def norm_stats(s, layer):
                    turn = it * 4 + layer
                    if layer == 0:
                        src = xin[s]
                        dve.wait_ge(loaded["xin"][s], it * 16 + 16)
                    else:
                        src = X[s]
                        dve.wait_ge(*after("residual", turn - 1, s))
                    for t in range(TILES):
                        last = dve.bn_stats(bst[s][:, t, :], src[:, t, :])
                    last.then_inc(S["stats"], 1)

                def norm_var(s, layer):
                    turn = it * 4 + layer
                    dve.wait_ge(*after("stats", turn, s))
                    dve.memset(tick_dve[:, 0, s:s + 1], 0.0)
                    for t in range(TILES):
                        last = dve.bn_aggr(mv[s][:, t, :], bst[s][:, t, :])
                    last.then_inc(S["aggregated"], 1)
                    dve.wait_ge(*after("aggregated", turn, s))
                    dve.tensor_scalar(var[s][:, :], mv[s][:, :, 1], EPS, None, ALU.add).then_inc(S["variance"], 1)

                def norm_scale(s, layer):
                    turn = it * 4 + layer
                    src = xin[s] if layer == 0 else X[s]
                    dve.wait_ge(*after("rstd", turn, s))
                    for t in range(TILES):
                        last = dve.tensor_scalar(hN[s][:, part(t)], src[:, t, :], mv[s][:, t, 0:1], rstd[s][:, t:t + 1],
                                                 ALU.subtract, ALU.mult)
                    last.then_inc(S["normed"], 1)

                def norm(layer):
                    for s in SL:
                        norm_stats(s, layer)
                        norm_var(s, layer)
                    for s in SL:
                        norm_scale(s, layer)
                    for s in SL:
                        dve.wait_ge(*after("h_high", it * 4 + layer, s))
                        dve.tensor_tensor(HL[s], HT[s][:, :], HH[s].bitcast(F32), ALU.subtract).then_inc(S["h_low"], 1)

                def add_residual(s, layer):
                    turn = it * 4 + layer
                    if layer == 0:
                        dve.wait_ge(*after("tanh0", it, s))
                        dve.wait_ge(*after("x_half", it, s))
                        last = dve.scalar_tensor_tensor(X[s][:, :, :], Y[s].rearrange("p (t n) -> p t n", t=TILES), 0.5,
                                                        X[s][:, :, :], ALU.mult, ALU.add)
                    else:
                        dve.wait_ge(*after("y_banked", it * 3 + layer - 1, s))
                    y = B[s][:, 1, :].rearrange("p (t n) -> p t n", t=TILES)
                    if layer == 2:
                        dve.wait_ge(loaded["nmask"][s], it * 16 + 16)
                        for t in range(TILES):
                            last = dve.scalar_tensor_tensor(X[s][:, t, :], y[:, t, :], nm[s][:, t:t + 1], X[s][:, t, :],
                                                            ALU.mult, ALU.add)
                    elif layer > 0:
                        last = dve.tensor_tensor(X[s][:, :, :], y, X[s][:, :, :], ALU.add)
                    last.then_inc(S["residual"], 1)

                norm(0)
                for s in SL:
                    dve.scalar_tensor_tensor(acc[s].rearrange("p (t n) -> p t n", t=TILES),
                                             hN[s][:, :].rearrange("p (t n) -> p t n", t=TILES), 0.0,
                                             ob[:, :].unsqueeze(1).broadcast_to([P, TILES, DIM]), ALU.max, ALU.add)\
                        .then_inc(S["acc_start"], 1)
                for s in SL:
                    dve.wait_ge(*after("qk_banked", it, s))
                    dve.tensor_tensor(QK[s][:, :, :], B[s][:, 1, 0:64].rearrange("p (t c) -> p t c", t=TILES),
                                      CQ[:, :].unsqueeze(1).broadcast_to([P, TILES, 2 * HEADS]), ALU.add).then_inc(S["qk"], 1)
                    dve.wait_ge(*after("qk", it, s))
                    dve.tensor_scalar(Q99[s][:, :, :], QK[s][:, :, 0:HEADS], 99.0, None, ALU.mult).then_inc(S["q99"], 1)
                    for t in range(TILES):
                        dve.wait_ge(*after("g_banked", it, s, 2 * t + 2))
                        dve.tensor_copy(G[s][:, t, 4 * DIM:8 * DIM], B[s][:, 3, :]).then_inc(S["g_dve"], 1)
                for s in SL:
                    dve.wait_ge(x_free[s], it * 16 + 16)
                    dve.tensor_scalar(X[s][:, :, :], xin[s][:, :, :], 0.5, None, ALU.add).then_inc(S["x_half"], 1)

                def masked_keys(u, t):
                    h, s = u // SLOTS, u % SLOTS
                    turn = it * HEADS + h
                    if t == 0:
                        if h == 0:
                            dve.wait_ge(*after("mask0", it, s))
                        if u >= 3:
                            dve.wait_ge(*after("pt_banked", it * HEADS + (u - 3) // SLOTS, (u - 3) % SLOTS))
                        dve.wait_ge(*after("kb_banked", turn, s))
                        dve.memset(tick_dve[:, 1, s:s + 1], 0.0)
                    dve.tensor_tensor_reduce(out=SC[u % 3][:, t, :], in0=adjN[s][:, t, :], in1=B[s][:, 0, :], scale=1.0,
                                             scalar=-3.0e38, op0=ALU.add, op1=ALU.max,
                                             accum_out=kmax[s][:, t:t + 1]).then_inc(S["masked"], 1)

                def exp_bias(u):
                    h, s = u // SLOTS, u % SLOTS
                    turn = it * HEADS + h
                    dve.wait_ge(*after("masked", turn, s))
                    dve.scalar_tensor_tensor(kq[s][:, :], kmax[s][:, :], -1.0, QK[s][:, :, h], ALU.mult, ALU.subtract)\
                        .then_inc(S["kmax_q"], 1)
                    dve.wait_ge(*after("kmax_q", turn, s))
                    dve.scalar_tensor_tensor(kmax[s][:, :], kq[s][:, :], 0.01, kq[s][:, :], ALU.mult, ALU.min)\
                        .then_inc(S["neg_max"], 1)
                    if u >= 2:
                        dve.wait_ge(*after("exped", turn - 1, s))
                    dve.wait_ge(*after("neg_max", turn, s))
                    dve.scalar_tensor_tensor(nmx[s][:, :], QK[s][:, :, h], 0.01, kmax[s][:, :], ALU.mult, ALU.add)\
                        .then_inc(S["exp_bias"], 1)

                def denominators(u):
                    h, s = u // SLOTS, u % SLOTS
                    dve.wait_ge(*after("exped", it * HEADS + h, s))
                    dve.reciprocal(rden[s][:, :], den[s][:, :]).then_inc(S["rden"], 1)

                def tile_copy(u, j):
                    h, s = u // SLOTS, u % SLOTS
                    turn = it * HEADS + h
                    if h >= 1 and j == 0:
                        dve.wait_ge(*after("o_banked", turn - 1, s))
                    dve.wait_ge(*after("pt_banked", turn, s, j + 1))
                    dve.tensor_copy(PT[s][:, j, :], B[j % 2][:, 1, :]).then_inc(S["pt_dve"], 1)

                def add_head(u):
                    h, s = u // SLOTS, u % SLOTS
                    turn = it * HEADS + h
                    if h == 0:
                        dve.wait_ge(*after("acc_start", it, s))
                    else:
                        dve.wait_ge(*after("o_added", turn - 1, s))
                    dve.wait_ge(*after("rden", turn, s))
                    dve.wait_ge(*after("o_banked", turn, s))
                    for t in range(TILES):
                        last = dve.scalar_tensor_tensor(acc[s][:, part(t)], B[s][:, 2 + h % 2, part(t)], rden[s][:, t:t + 1],
                                                        acc[s][:, part(t)], ALU.mult, ALU.add)
                    last.then_inc(S["o_added"], 1)

                UNITS = HEADS * SLOTS
                for u in range(-1, UNITS + 2):
                    for t in range(TILES):
                        if u + 1 < UNITS:
                            masked_keys(u + 1, t)
                        if t < TILES - 1 and 0 <= u - 1 < UNITS:
                            tile_copy(u - 1, t)
                    if 0 <= u - 1 < UNITS:
                        denominators(u - 1)
                    if u + 1 < UNITS:
                        exp_bias(u + 1)
                    if 0 <= u - 2 < UNITS:
                        add_head(u - 2)
                for s in SL:
                    add_residual(s, 0)

                norm(1)
                for s in SL:
                    dve.wait_ge(loaded["adjT"][s], it * 16 + 16)
                    dve.tensor_scalar(U[s][:, :, :], adjT[s][:, :, :], 0.0, NEG1, ALU.is_le, ALU.mult)\
                        .then_inc(S["mask1"], 1)
                for s in SL:
                    dve.wait_ge(*after("h1_high", it, s))
                    dve.tensor_tensor(R[s][:, 1, :], F[s][:, 0, :], R[s][:, 0, :].bitcast(F32), ALU.subtract)\
                        .then_inc(S["h1_low"], 1)
                for s in SL:
                    dve.wait_ge(*after("t1_high", it, s))
                    dve.tensor_tensor(R[s][:, 3, :], B[s][:, 2, :], R[s][:, 2, :].bitcast(F32), ALU.subtract)\
                        .then_inc(S["t1_low"], 1)
                for t in range(TILES):
                    for s in SL:
                        if t == 0:
                            dve.wait_ge(*after("mask1", it, s))
                        dve.wait_ge(*after("s_banked", it, s, t + 1))
                        dve.memset(tick_dve[:, 2 + t, s:s + 1], 0.0)
                        dve.tensor_tensor_reduce(out=U[s][:, t, :], in0=U[s][:, t, :], in1=B[s][:, t % 2, :], scale=1.0,
                                                 scalar=-3.0e38, op0=ALU.add, op1=ALU.max,
                                                 accum_out=kmax[s][:, t:t + 1]).then_inc(S["s_masked"], 1)
                    for s in SL:
                        dve.wait_ge(*after("s_masked", it, s, t + 1))
                        dve.tensor_scalar(nmx[s][:, t:t + 1], kmax[s][:, t:t + 1], -1.0, None, ALU.mult)\
                            .then_inc(S["s_negmax"], 1)
                for s in SL:
                    dve.wait_ge(*after("s_exped", it, s))
                    dve.reciprocal(rden[s][:, :], den[s][:, :]).then_inc(S["rden1"], 1)
                    dve.wait_ge(*after("rden1", it, s))
                    dve.wait_ge(*after("h1n_banked", it, s))
                    for t in range(TILES):
                        last = dve.tensor_scalar(F[s][:, 1, part(t)], B[s][:, 3, part(t)], rden[s][:, t:t + 1], None, ALU.mult)
                    last.then_inc(S["h1_scaled"], 1)
                for s in SL:
                    dve.wait_ge(*after("hp", it, s))
                    dve.tensor_tensor(F[s][:, 4, :], HT[s][:, :], F[s][:, 2, :], ALU.subtract).then_inc(S["h_less_hp"], 1)
                for s in SL:
                    dve.wait_ge(*after("gate", it, s))
                    dve.wait_ge(*after("h_less_hp", it, s))
                    dve.scalar_tensor_tensor(F[s][:, 5, :], F[s][:, 3, :], 1.0, F[s][:, 4, :], ALU.add, ALU.mult)\
                        .then_inc(S["gate_e"], 1)
                for s in SL:
                    dve.wait_ge(*after("gate_e", it, s))
                    dve.scalar_tensor_tensor(Y[s], F[s][:, 5, :], 0.5, F[s][:, 2, :], ALU.mult, ALU.add)\
                        .then_inc(S["y1"], 1)
                for s in SL:
                    add_residual(s, 1)

                def cand_a(s, cell):
                    dve.wait_ge(*after("hn", cell, s))
                    dve.wait_ge(*after("r", cell, s))
                    dve.scalar_tensor_tensor(F[s][:, 3, :], F[s][:, 0, :], 1.0, F[s][:, 2, :], ALU.add, ALU.mult)\
                        .then_inc(S["cand_a"], 1)

                def cand_b(s, cell, in_bank):
                    dve.wait_ge(*after("cand_a", cell, s))
                    dve.wait_ge(*after("in_banked", cell, s))
                    dve.tensor_tensor(F[s][:, 3, :], B[s][:, in_bank, :], F[s][:, 3, :], ALU.add).then_inc(S["cand_b"], 1)

                def cell_zh(s, cell):
                    dve.wait_ge(*after("z", cell, s))
                    dve.scalar_tensor_tensor(F[s][:, 5, :], F[s][:, 1, :], 1.0, HT[s][:, :], ALU.add, ALU.mult)\
                        .then_inc(S["zh"], 1)
                    dve.tensor_scalar(F[s][:, 6, :], F[s][:, 1, :], -0.5, 0.5, ALU.mult, ALU.add).then_inc(S["z_rest"], 1)

                def cell_end(s, cell, dst):
                    dve.wait_ge(*after("cand", cell, s))
                    dve.wait_ge(*after("z_rest", cell, s))
                    dve.tensor_tensor(F[s][:, 4, :], F[s][:, 6, :], F[s][:, 4, :], ALU.mult).then_inc(S["z_cand"], 1)
                    dve.wait_ge(*after("z_cand", cell, s))
                    dve.scalar_tensor_tensor(dst, F[s][:, 5, :], 0.5, F[s][:, 4, :], ALU.mult, ALU.add)\
                        .then_inc(S["h_new"], 1)

                for s in SL:
                    dve.wait_ge(loaded["adjN"][s], it * 32 + 32)
                    dve.wait_ge(*after("hp_banked", it, s))
                    dve.tensor_scalar(AN[s][:, :, :], adjN[s][:, :, :], 0.0, None, ALU.not_equal)\
                        .then_inc(S["adjacency"], 1)
                norm(2)
                for n in range(LAYERS2 * SLOTS + 1):
                    s, layer = n % SLOTS, n // SLOTS
                    o, before = (n - 1) % SLOTS, (n - 1) // SLOTS
                    turn, cell = it * LAYERS2 + layer, it * (LAYERS2 + 1) + layer
                    cell_o = it * (LAYERS2 + 1) + before
                    start, end = n < LAYERS2 * SLOTS, n >= 1
                    if end:
                        cand_a(o, cell_o)
                    if start:
                        dve.wait_ge(*after("rows_high", turn, s))
                        dve.tensor_tensor(R[s][:, 1, :], B[s][:, 0, :], R[s][:, 0, :].bitcast(F32), ALU.subtract)\
                            .then_inc(S["rows_low"], 1)
                    if end:
                        cand_b(o, cell_o, 1)
                        cell_zh(o, cell_o)
                        cell_end(o, cell_o, HT[o][:, :])
                    if start:
                        dve.wait_ge(*after("agg_high", turn, s))
                        dve.tensor_tensor(R[s][:, 3, :], B[s][:, 1, :], R[s][:, 2, :].bitcast(F32), ALU.subtract)\
                            .then_inc(S["agg_low"], 1)
                for s in SL:
                    add_residual(s, 2)

                norm(3)
                for s in SL:
                    for edge in (0, PAD + NODES):
                        dve.memset(C1[s][:, :, edge:edge + PAD].bitcast(F32), 0.0)
                for s in SL:
                    dve.wait_ge(*after("c1_high", it, s))
                    dve.tensor_tensor(C1[s][:, 1, PAD:PAD + NODES], F[s][:, 6, :],
                                      C1[s][:, 0, PAD:PAD + NODES].bitcast(F32), ALU.subtract).then_inc(S["c1_low"], 1)
                for s in SL:
                    dve.wait_ge(*after("c2_banked", it, s))
                    dve.scalar_tensor_tensor(F[s][:, 3, :], B[s][:, 2, :], dcol("s2"), HT[s][:, :], ALU.mult, ALU.add)\
                        .then_inc(S["c2_scaled"], 1)
                    dve.wait_ge(*after("xc_high", it, s))
                    dve.tensor_tensor(R[s][:, 1, :], F[s][:, 4, :], R[s][:, 0, :].bitcast(F32), ALU.subtract)\
                        .then_inc(S["xc_low"], 1)
                    dve.wait_ge(*after("nmp_high", it, s))
                    dve.tensor_tensor(R[s][:, 3, :], B[s][:, 3, :], R[s][:, 2, :].bitcast(F32), ALU.subtract)\
                        .then_inc(S["nmp_low"], 1)
                for s in SL:
                    cell = it * (LAYERS2 + 1) + LAYERS2
                    cand_a(s, cell)
                    cell_zh(s, cell)
                    cand_b(s, cell, 3)
                    cell_end(s, cell, Y[s])
                for s in SL:
                    add_residual(s, 3)


def kernel(**inputs):
    import numpy as _np
    import concourse.bacc as _bacc
    from concourse import mybir as _mybir
    from concourse.bass_utils import run_bass_kernel_spmd as _run

    v = {k: _np.asarray(a) for k, a in inputs.items()}

    def wide(a):
        return _np.ascontiguousarray(a).reshape(P, -1)

    fcw = wide(v["L0_gnn_fc_w"].reshape(DIM, HEADS, DIM).transpose(2, 1, 0))
    fpw = wide(v["L0_gnn_fp_w"].reshape(HEADS, DIM, DIM).transpose(1, 0, 2))
    wraw = _np.concatenate([
        wide(v["L2_gnn_w_hh"].T), wide(v["L1_gnn_W_w"].T), wide(v["L1_gnn_A"]), wide(v["L3_gnn_conv1_w"][:, :, 0].T),
        wide(v["L3_gnn_w_msg"].T), wide(v["L3_gnn_w_ih"][:, :DIM].T), wide(v["L3_gnn_w_ih"][:, DIM:].T),
        wide(v["L3_gnn_w_hh"].T), wide(v["L1_gnn_A"].T)], axis=1)
    prew = _np.concatenate([wide(v["L2_gnn_weight"].transpose(2, 0, 1)), wide(v["L2_gnn_w_ih"].T)], axis=1)
    c2w = wide(v["L3_gnn_conv2_w"].transpose(1, 2, 0))

    def spread(a):
        return _np.broadcast_to(a.reshape(1, 1), (P, 1))

    def head(a):
        z = _np.zeros((P, 1), _np.float32)
        z[:a.size, 0] = a
        return z

    def gates(a):
        return wide(a.reshape(3, DIM).T)

    se = _np.zeros((P, 5), _np.float32)
    se[:, :3] = v["L3_gnn_w_se"].T
    unit = _np.eye(P, dtype=_np.float32)
    columns = _np.concatenate([
        wide(v["L0_gnn_fc_b"].reshape(HEADS, DIM).T), v["L0_gnn_q_w"], v["L0_gnn_k_w"], wide(v["L0_gnn_fp_b"]),
        wide(v["L1_gnn_W_b"]), spread(v["L1_gnn_gate_b"]), spread(v["L0_gnn_q_b"]), spread(v["L0_gnn_k_b"]),
        gates(v["L2_gnn_b_ih"]), gates(v["L2_gnn_b_hh"])]
        + [wide(v[f"L3_gnn_bn{i}_{c}"]) for c in "vgbm" for i in (1, 2)]
        + [gates(v["L3_gnn_b_ih"]), gates(v["L3_gnn_b_hh"]), wide(v["L1_gnn_gate_w"].reshape(2, DIM).T), se,
           head(v["L3_gnn_b_se"]), unit[:, 3:4], unit[:, 4:5]], axis=1)
    rows = _np.stack([v["L3_gnn_b_msg"], _np.ones(DIM, _np.float32)])[None]
    host = [("x", v["x"]), ("adj", v["adj"]), ("adjt", v["adj"].transpose(0, 2, 1)), ("nodemask", v["nodemask"].reshape(GRAPHS, TILES, P).transpose(0, 2, 1)),
            ("c2w", c2w), ("wraw", wraw), ("prew", prew), ("fcw", fcw), ("fpw", fpw), ("cols", columns), ("rows", rows)]
    nc = _bacc.Bacc("TRN2", target_bir_lowering=False, num_devices=1)
    arrays, args = {}, []
    for name, a in host:
        a = _np.ascontiguousarray(a)
        arrays[f"in_{name}_dram"] = a
        args.append(nc.dram_tensor(f"in_{name}_dram", a.shape, _mybir.dt.from_np(a.dtype), kind="ExternalInput").ap())
    args.append(nc.dram_tensor("out_0_dram", (GRAPHS, NODES, DIM), _mybir.dt.float32, kind="ExternalOutput").ap())
    build(nc, *args)
    r = _run(nc, [arrays], core_ids=[0])
    return r.results[0]["out_0_dram"]
```

```python
import numpy as np
import concourse.bass as bass
from concourse import mybir
from contextlib import ExitStack

F32 = mybir.dt.float32
F32R = mybir.dt.float32r
ALU = mybir.AluOpType
ACT = mybir.ActivationFunctionType

GRAPHS, NODES, DIM = 16, 512, 128
P = 128
TILES = NODES // P
SLOTS = 2
ROUNDS = GRAPHS // SLOTS
HEADS = 8
LAYERS2 = 5
TAPS = 17
PAD = TAPS // 2
EPS = 1e-5
NEG0 = -1000000000.0
NEG1 = -9000000000000000.0

WIDTHS = [("WI2", LAYERS2 * 3 * DIM), ("c2", TAPS * DIM), ("M", HEADS * DIM), ("hh2", 3 * DIM), ("Ww", DIM), ("As", DIM),
          ("c1", DIM), ("msg", DIM), ("ih3c", 3 * DIM), ("ih3n", 3 * DIM), ("hh3", 3 * DIM)]
WCOL = {}
_at = 0
for _name, _width in WIDTHS:
    WCOL[_name] = _at
    _at += _width
WALL = _at
WFIRST = WCOL["M"]

COLS = (["fcb%d" % h for h in range(HEADS)] + ["qw", "kw", "fpb", "Wb", "gateb", "qb", "kb",
        "bih2r", "bih2z", "bih2n", "bhh2r", "bhh2z", "bhh2n", "v1", "v2", "g1", "g2", "b1", "b2", "m1", "m2",
        "bih3r", "bih3z", "bih3n", "bhh3r", "bhh3z", "bhh3n", "gw1", "gw2",
        "se0", "se1", "se2", "se3", "se4", "bse", "e3", "e4"])
CI = {n: i for i, n in enumerate(COLS)}
DCOLS = ["rz2r", "rz2z", "hn2", "rz3r", "rz3z", "hn3", "s1", "s2", "sh1", "sh2", "gb", "bias2", "bias1", "qkw",
         "t1", "t2", "r1", "r2", "tq"]
DI = {n: i for i, n in enumerate(DCOLS)}

PER = {
    "stats": 1, "aggregated": 1, "variance": 1, "rstd": 1, "normed": 1, "h_banked": 1, "h_high": 1, "h_low": 1,
    "h": 1,
    "y_banked": 1, "residual": 1,
    "mask0": 1, "qk_banked": 1, "qk": 1, "q99": 1, "g_banked": 8, "g_act": 4, "g_dve": 4,
    "kb_banked": 1, "masked": 4, "relu": 4, "lifted": 4, "kmax_q": 1, "neg_max": 1, "exp_bias": 1, "exped": 4,
    "pt_banked": 4, "pt_dve": 3, "pt_act": 1,
    "rden": 1, "o_banked": 1, "o_added": 1,
    "acc_start": 1, "x_half": 1, "tanh0": 1,
    "mask1": 1, "h1_banked": 1, "h1_high": 1, "h1": 1, "h1_low": 1, "t1_banked": 1, "t1_high": 1, "t1_low": 1, "h1n_banked": 1,
    "s_banked": 4, "s_masked": 4, "s_negmax": 4, "s_exped": 4, "att_pool": 2, "att_dve": 2, "rden1": 1, "h1_scaled": 1, "hp_banked": 1,
    "hp": 1, "gate_banked": 1, "gate": 1, "h_less_hp": 1, "gate_e": 1, "y1": 1,
    "adjacency": 1,
    "hn_rows": 1, "rows_high": 1, "rows_low": 1, "agg_banked": 1, "agg_high": 1, "agg_low": 1,
    "hn_banked": 1, "r_banked": 1, "z_banked": 1, "in_banked": 1, "hn": 1, "r": 1, "z": 1, "cand_a": 1, "cand_b": 1,
    "cand": 1, "zh": 1, "z_rest": 1, "z_cand": 1, "h_new": 1, "h_new_high": 1, "h_new_low": 1,
    "c1_banked": 1, "c1_high": 2, "c1_low": 1, "s3_banked": 1, "sq3": 1, "aug_banked": 2, "aug": 2, "msg_banked": 1,
    "msg": 1, "dist_banked": 4, "dist_exped": 4, "weights3": 4, "c2_banked": 1, "c2_scaled": 1, "xc_high": 2,
    "xc_low": 1, "nmp_banked": 1, "nmp_high": 1, "nmp_low": 1,
}


ALTERNATING = {"dist_banked", "dist_exped", "weights3"}


def build(nc, x, adj, adjt, nmask, c2w, wraw, prew, fcw, fpw, cols_d, rows_d, out):
    with ExitStack() as ctx:
        def sb(name, shape, dt=F32):
            return ctx.enter_context(nc.sbuf_tensor(name, shape, dt))

        def sem(name):
            return ctx.enter_context(nc.semaphore(name))

        SL = range(SLOTS)
        WH = sb("WH", [P, WALL], F32R)
        WLO = sb("WLO", [P, WALL], F32R)
        VQH = sb("VQH", [P, 2 * HEADS], F32R)
        VQL = sb("VQL", [P, 2 * HEADS], F32R)
        VQ = sb("VQ", [P, 2 * HEADS])
        CQ = sb("CQ", [P, 2 * HEADS])
        ident = sb("ident", [P, P])
        cols = sb("cols", [P, len(COLS)])
        dcols = sb("dcols", [P, len(DCOLS)])
        se2 = sb("se2", [P, 5])
        neg5 = sb("neg5", [5, 2, 5])
        ob = sb("ob", [P, DIM])
        rows = sb("rows", [1, 2, P])
        mhalf = sb("mhalf", [P, TILES])
        adjN = [sb(f"adjN{s}", [P, TILES, NODES]) for s in SL]
        adjT = [sb(f"adjT{s}", [P, TILES, NODES]) for s in SL]
        U = [sb(f"U{s}", [P, TILES, NODES]) for s in SL]
        AN = []
        PT = []
        for s in SL:
            with nc.sbuf_tensor(f"PT{s}", [P, TILES, NODES], F32) as pt:
                PT.append(pt)
            AN.append(sb(f"AN{s}", [P, TILES, NODES], F32R))
        F = [sb(f"F{s}", [P, 8, NODES]) for s in SL]
        G = [F[s][:, :, :].rearrange("p (t a) n -> p t (a n)", a=2) for s in SL]
        HS = [sb(f"HS{s}", [P, 2, NODES], F32R) for s in SL]
        R, tiles = [], []
        for s in SL:
            with nc.sbuf_tensor(f"tiles{s}", [P, TILES, NODES], F32) as t:
                tiles.append(t)
            R.append(sb(f"R{s}", [P, TILES, NODES], F32R))
        RELU = tiles[0]
        SC = [U[0], U[1], tiles[1]]
        C1, acc, Y = [], [], []
        for s in SL:
            with nc.sbuf_tensor(f"accY{s}", [P, 2, NODES], F32) as t:
                acc.append(t[:, 0, :])
                Y.append(t[:, 1, :])
            C1.append(sb(f"C1{s}", [P, 2, NODES + 2 * PAD], F32R))
        HT = [sb(f"HT{s}", [P, NODES]) for s in SL]
        hN = [sb(f"hN{s}", [P, NODES]) for s in SL]
        X = [sb(f"X{s}", [P, TILES, DIM]) for s in SL]
        xin = [sb(f"xin{s}", [P, TILES, DIM]) for s in SL]
        nm = [sb(f"nm{s}", [P, TILES]) for s in SL]
        QK = [sb(f"QK{s}", [P, TILES, 2 * HEADS]) for s in SL]
        Q99 = [sb(f"Q99{s}", [P, TILES, HEADS]) for s in SL]
        bst = [sb(f"bst{s}", [P, TILES, 6]) for s in SL]
        mv = [sb(f"mv{s}", [P, TILES, 2]) for s in SL]
        var = [sb(f"var{s}", [P, TILES]) for s in SL]
        rstd = [sb(f"rstd{s}", [P, TILES]) for s in SL]
        kmax = [sb(f"kmax{s}", [P, TILES]) for s in SL]
        kq = [sb(f"kq{s}", [P, TILES]) for s in SL]
        nmx = [sb(f"nmx{s}", [P, TILES]) for s in SL]
        den = [sb(f"den{s}", [P, TILES]) for s in SL]
        rden = [sb(f"rden{s}", [P, TILES]) for s in SL]
        B = [ctx.enter_context(nc.psum_tensor(f"banks{s}", [P, 4, 512], F32)) for s in SL]

        S = {name: sem(name) for name in PER}
        loaded = {n: [sem(f"{n}_loaded{s}") for s in SL] for n in ("xin", "adjN", "adjT", "nmask")}
        x_free = [sem(f"x_free{s}") for s in SL]
        w_loaded = sem("w_loaded")
        ones_ready = sem("ones_ready")
        ident_ready = sem("ident_ready")
        setup_dve = sem("setup_dve")
        setup_pool = sem("setup_pool")
        setup_pe = sem("setup_pe")
        setup_act = sem("setup_act")
        w_split = sem("w_split")

        def after(name, turn, s, k=None):
            n = PER[name]
            k = n if k is None else k
            return S[name], turn * (SLOTS * n) + (SLOTS * (k - 1) + s + 1 if name in ALTERNATING else s * n + k)

        def tile_out(turn, s, j):
            return after("pt_act", turn, s) if j == TILES - 1 else after("pt_dve", turn, s, j + 1)

        def attended(it, s, t):
            return after("att_dve" if t % 2 else "att_pool", it, s, t // 2 + 1)

        def col(name):
            return cols[:, CI[name]:CI[name] + 1]

        def dcol(name):
            return dcols[:, DI[name]:DI[name] + 1]

        def part(t):
            return slice(t * P, (t + 1) * P)

        stage = [F[s][:, :, :].rearrange("p t n -> p (t n)") for s in SL]
        HH = [HS[s][:, 0, :] for s in SL]
        HL = [HS[s][:, 1, :] for s in SL]

        tick_dve = sb("tick_dve", [P, 2 + TILES, SLOTS])
        tick_pool = sb("tick_pool", [P, SLOTS])

        WI2_BANKS = [(1, 1), (1, 2), (1, 3), (1, 0), (0, 3)]

        block = ctx.enter_context(nc.Block())

        @block.sync
        def _(sp):
            def load(dst, src, signal):
                sp.dma_start(dst, src).then_inc(signal, 16)

            def nodes(t, g):
                return t[bass.ds(g, 1), :, :].rearrange("g (t p) n -> p (g t) n", p=P)

            load(cols[:, :], cols_d, w_loaded)
            load(rows[:, :, :], rows_d, w_loaded)
            load(U[0][:, 0:2, :].rearrange("p t n -> p (t n)"), fcw, w_loaded)
            load(U[1][:, 0:2, :].rearrange("p t n -> p (t n)"), fpw, w_loaded)
            load(U[0][:, 2:4, :].rearrange("p t n -> p (t n)"), prew, w_loaded)
            load(stage[0][:, WCOL["c2"]:WFIRST], c2w, w_loaded)
            load(stage[1][:, HEADS * DIM:WALL - WFIRST], wraw[:, 0:WALL - WFIRST - HEADS * DIM], w_loaded)
            load(xin[1][:, 0, :], wraw[:, WALL - WFIRST - HEADS * DIM:WALL - WFIRST - HEADS * DIM + DIM], w_loaded)
            sp.wait_ge(setup_dve, 2)
            for s in SL:
                load(xin[s][:, :, :], nodes(x, s), loaded["xin"][s])
                load(adjN[s][:, :, :], nodes(adj, s), loaded["adjN"][s])
                load(adjT[s][:, :, :], nodes(adjt, s), loaded["adjT"][s])
                load(nm[s][:, :], nmask[s, :, :], loaded["nmask"][s])

            def round_of(it, more):
                for s in SL:
                    sp.wait_ge(*after("masked", it * HEADS + HEADS - 1, s))
                    load(adjN[s][:, :, :], nodes(adj, it * SLOTS + s), loaded["adjN"][s])
                for s in SL:
                    sp.wait_ge(*after("x_half", it, s))
                    load(xin[s][:, :, :], nodes(x, it * SLOTS + ((SLOTS if more else 0) + s)), loaded["xin"][s])
                if more:
                    for s in SL:
                        sp.wait_ge(*after("adjacency", it, s))
                        load(adjN[s][:, :, :], nodes(adj, it * SLOTS + (SLOTS + s)), loaded["adjN"][s])
                    for s in SL:
                        sp.wait_ge(*after("residual", it * 4 + 2, s))
                        load(nm[s][:, :], nmask[bass.ds(it * SLOTS + (SLOTS + s), 1), :, :].rearrange("g p t -> p (g t)"),
                             loaded["nmask"][s])
                    for s in SL:
                        sp.wait_ge(*after("weights3", it, s))
                        load(adjT[s][:, :, :], nodes(adjt, it * SLOTS + (SLOTS + s)), loaded["adjT"][s])
                for s in SL:
                    sp.wait_ge(*after("residual", it * 4 + 3, s))
                    sp.dma_start(nodes(out, it * SLOTS + s), X[s][:, :, :]).then_inc(x_free[s], 16)

            with sp.Fori(0, ROUNDS - 1) as it:
                round_of(it, True)
            round_of(ROUNDS - 1, False)
            for s in SL:
                sp.wait_ge(x_free[s], 16 * (ROUNDS + 1))

        @block.gpsimd
        def _(pool):
            pool.memset(ident[:, :], 0.0).then_inc(ident_ready, 1)
            pool.memset(mhalf[:, :], -0.5)
            pool.memset(neg5[:, :, :], 0.0).then_inc(setup_pool, 1)
            pool.wait_ge(ident_ready, 1)
            pool.affine_select(out=ident[:, :], in_=ident[:, :], compare_op=ALU.not_equal, fill=1.0, base=0,
                               pattern=[[-1, P]], channel_multiplier=1).then_inc(ident_ready, 1)
            pool.wait_ge(setup_pool, 1)
            pool.memset(neg5[:, 0, 3:4], -1.0)
            pool.memset(neg5[:, 1, 4:5], -1.0).then_inc(setup_pool, 1)
            pool.wait_ge(setup_dve, 1)
            pool.tensor_tensor(dcols[:, DI["r1"]:DI["r1"] + 2], dcols[:, DI["t1"]:DI["t1"] + 2], mhalf[:, 0:2],
                               ALU.pow).then_inc(setup_pool, 1)

            UNITS = HEADS * SLOTS

            def rstd_of(s, turn):
                pool.wait_ge(*after("variance", turn, s))
                pool.tensor_tensor(rstd[s][:, :], var[s][:, :], mhalf[:, :], ALU.pow).then_inc(S["rstd"], 1)

            for s in SL:
                rstd_of(s, 0)
            with pool.Fori(0, ROUNDS) as it:
                for s in SL:
                    pool.wait_ge(loaded["adjN"][s], it * 32 + 16)
                    pool.tensor_tensor(tick_pool[:, s:s + 1], mhalf[:, 0:1], mhalf[:, 0:1], ALU.add)
                    pool.tensor_scalar(adjN[s][:, :, :], adjN[s][:, :, :], -1.0, -NEG0, ALU.add, ALU.mult)\
                        .then_inc(S["mask0"], 1)

                def whole(s, turn):
                    pool.wait_ge(*after("h_low", it * 4 + turn + 1, s))
                    pool.tensor_tensor(HT[s][:, :], HH[s].bitcast(F32), HL[s].bitcast(F32), ALU.add).then_inc(S["h"], 1)

                def lift(u, t):
                    turn = it * HEADS + u // SLOTS
                    pool.wait_ge(*after("relu", turn, u % SLOTS, t + 1))
                    pool.tensor_tensor(SC[u % 3][:, t, :], SC[u % 3][:, t, :], RELU[:, t, :], ALU.add)\
                        .then_inc(S["lifted"], 1)

                for u in range(UNITS):
                    for t in range(TILES):
                        lift(u, t)
                for s in SL:
                    rstd_of(s, it * 4 + 1)
                for s in SL:
                    whole(s, 0)
                for s in SL:
                    pool.wait_ge(*after("h1_low", it, s))
                    pool.tensor_tensor(F[s][:, 0, :], R[s][:, 0, :].bitcast(F32), R[s][:, 1, :].bitcast(F32), ALU.add)\
                        .then_inc(S["h1"], 1)
                for s in SL:
                    for t in range(0, TILES, 2):
                        pool.wait_ge(*after("s_exped", it, s, t + 1))
                        pool.tensor_tensor(PT[s][:, t, :], U[s][:, t, :], adjT[s][:, t, :], ALU.mult)\
                            .then_inc(S["att_pool"], 1)
                for s in SL:
                    rstd_of(s, it * 4 + 2)
                for layer in range(LAYERS2 - 1):
                    for s in SL:
                        pool.wait_ge(*after("h_new_high", it * (LAYERS2 - 1) + layer, s))
                        pool.tensor_tensor(HL[s], HT[s][:, :], HH[s].bitcast(F32), ALU.subtract)\
                            .then_inc(S["h_new_low"], 1)
                for s in SL:
                    rstd_of(s, it * 4 + 3)
                    whole(s, 2)
                for t in range(TILES):
                    for s in SL:
                        pool.wait_ge(*after("dist_exped", it, s, t + 1))
                        pool.tensor_tensor(PT[s][:, t, :], U[s][:, t, :], adjT[s][:, t, :], ALU.mult)\
                            .then_inc(S["weights3"], 1)
                for s in SL:
                    rstd_of(s, it * 4 + 4)

        @block.tensor
        def _(pe):
            def mm3(dst, w, xs, start=True, stop=True):
                pe.matmul(dst, w[0], xs[0], start=start, stop=False)
                pe.matmul(dst, w[0], xs[1], start=False, stop=False)
                return pe.matmul(dst, w[1], xs[0], start=False, stop=stop)

            def W(name, j=0, n=DIM):
                a = WCOL[name] + j * DIM
                return WH[:, a:a + n], WLO[:, a:a + n]

            pe.wait_ge(w_loaded, 8 * 16)
            fcT = U[0][:, 0:2, :].rearrange("p t n -> p (t n)")
            fp = U[1][:, 0:2, :].rearrange("p t n -> p (t n)")
            for h in range(HEADS):
                pe.matmul(B[0][:, h // 4, (h % 4) * DIM:(h % 4 + 1) * DIM], fcT[:, part(h)], fp[:, part(h)])
            for h in range(HEADS):
                pe.matmul(B[0][:, 2, 2 * h:2 * h + 2], fcT[:, part(h)], cols[:, CI["qw"]:CI["qw"] + 2])
            pe.wait_ge(setup_dve, 2)
            pe.matmul(B[0][:, 3, 0:HEADS], dcol("qkw").broadcast_to([P, P]), cols[:, 0:HEADS])
            for h in range(HEADS):
                pe.matmul(B[1][:, 0, 0:DIM], cols[:, h:h + 1].broadcast_to([P, P]), fp[:, part(h)], start=(h == 0), stop=False)
            pe.wait_ge(ident_ready, 2)
            pe.matmul(B[1][:, 0, 0:DIM], col("fpb").broadcast_to([P, P]), ident[:, :], start=False, stop=True)
            pre = U[0][:, 2:4, :].rearrange("p t n -> p (t n)")
            for layer, (b, bank) in enumerate(WI2_BANKS):
                last = pe.matmul(B[b][:, bank, P:4 * P], pre[:, part(layer)], pre[:, LAYERS2 * DIM:(LAYERS2 + 3) * DIM])
            last.then_inc(setup_pe, 1)
            pe.wait_ge(w_split, 4)

            def transpose_in(s, turn):
                pe.wait_ge(*after("normed", turn, s))
                for t in range(TILES):
                    last = pe.transpose(B[s][:, 0, part(t)], hN[s][:, part(t)], ident[:, :])
                last.then_inc(S["h_banked"], 1)

            for s in SL:
                transpose_in(s, 0)
            with pe.Fori(0, ROUNDS) as it:
                def transpose_out(s, layer, y):
                    for t in range(TILES):
                        last = pe.transpose(B[s][:, 1, part(t)], y[:, part(t)], ident[:, :])
                    last.then_inc(S["y_banked"], 1)

                def query_keys(s):
                    pe.wait_ge(*after("h_low", it * 4, s))
                    for t in range(TILES):
                        last = mm3(B[s][:, 1, 16 * t:16 * t + 16], (HH[s][:, part(t)], HL[s][:, part(t)]),
                                   (VQH[:, :], VQL[:, :]))
                    last.then_inc(S["qk_banked"], 1)

                def values(s, t):
                    for half in range(2):
                        signal = "g_dve" if half else "g_act"
                        if t >= 2:
                            pe.wait_ge(*after(signal, it, s, t - 1))
                        elif s == 1:
                            pe.wait_ge(*after(signal, it, 0, t + 3))
                        mm3(B[t % 2][:, 2 + half, :], (HH[s][:, part(t)], HL[s][:, part(t)]),
                            W("M", 4 * half, 4 * DIM)).then_inc(S["g_banked"], 1)

                def rows_of(s, bank, column):
                    for t in range(TILES):
                        last = pe.transpose(B[s][:, bank, part(t)], column(t).broadcast_to([P, P]), ident[:, :])
                    return last

                def key_rows(u):
                    h, s = u // SLOTS, u % SLOTS
                    if h == 0:
                        pe.wait_ge(*after("qk", it, s))
                    else:
                        pe.wait_ge(*after("masked", it * HEADS + h - 1, s))
                    rows_of(s, 0, lambda t: QK[s][:, t, HEADS + h:HEADS + h + 1]).then_inc(S["kb_banked"], 1)

                UNITS = HEADS * SLOTS
                for s in SL:
                    query_keys(s)
                key_rows(0)
                for t in range(TILES):
                    values(0, t)
                key_rows(1)
                for t in range(TILES):
                    values(1, t)
                for u in range(UNITS + 1):
                    if u + 2 < UNITS:
                        key_rows(u + 2)
                    for j in range(TILES):
                        if u < UNITS:
                            h, s = u // SLOTS, u % SLOTS
                            turn = it * HEADS + h
                            if j == 0:
                                pe.wait_ge(*after("exped", turn, s))
                            if j >= 2:
                                pe.wait_ge(*tile_out(turn, s, j - 2))
                            elif u >= 1:
                                pe.wait_ge(*tile_out(it * HEADS + (u - 1) // SLOTS, (u - 1) % SLOTS, j + 2))
                            for t in range(TILES):
                                last = pe.transpose(B[j % 2][:, 1, part(t)], SC[u % 3][:, t, part(j)], ident[:, :])
                            last.then_inc(S["pt_banked"], 1)
                        if 1 <= u <= UNITS:
                            h, s = (u - 1) // SLOTS, (u - 1) % SLOTS
                            turn = it * HEADS + h
                            if j == 0:
                                if h < 2:
                                    pe.wait_ge(*after("g_act", it, 1))
                                    pe.wait_ge(*after("g_dve", it, 1))
                                else:
                                    pe.wait_ge(*after("o_added", turn - 2, s))
                                pe.wait_ge(*tile_out(turn, s, TILES - 2))
                                pe.wait_ge(*tile_out(turn, s, TILES - 1))
                            for k in range(TILES):
                                last = pe.matmul(B[s][:, 2 + h % 2, part(j)], PT[s][:, k, part(j)],
                                                 G[s][:, k, h * DIM:(h + 1) * DIM], start=(k == 0), stop=(k == TILES - 1))
                            if j == TILES - 1:
                                last.then_inc(S["o_banked"], 1)

                def h1(s):
                    pe.wait_ge(*after("h_low", it * 4 + 1, s))
                    mm3(B[s][:, 1, :], W("Ww"), (HH[s], HL[s])).then_inc(S["h1_banked"], 1)

                def t1(s):
                    pe.wait_ge(*after("h1_low", it, s))
                    mm3(B[s][:, 2, :], W("As"), (R[s][:, 0, :], R[s][:, 1, :])).then_inc(S["t1_banked"], 1)

                def h1_rows(s):
                    pe.wait_ge(*after("h1", it, s))
                    for t in range(TILES):
                        last = pe.transpose(B[s][:, 3, part(t)], F[s][:, 0, part(t)], ident[:, :])
                    last.then_inc(S["h1n_banked"], 1)

                def scores(s, t):
                    if t == 0:
                        pe.wait_ge(*after("t1_low", it, s))
                    if t >= 2:
                        pe.wait_ge(*after("s_masked", it, s, t - 1))
                    mm3(B[s][:, t % 2, :], (R[s][:, 2, part(t)], R[s][:, 3, part(t)]),
                        (R[s][:, 0, :], R[s][:, 1, :])).then_inc(S["s_banked"], 1)

                transpose_in(0, it * 4 + 1)
                h1(0)
                transpose_in(1, it * 4 + 1)
                t1(0)
                h1(1)
                scores(0, 0)
                t1(1)
                scores(0, 1)
                h1_rows(0)
                scores(0, 2)
                scores(0, 3)
                scores(1, 0)
                h1_rows(1)
                for t in range(1, TILES):
                    scores(1, t)

                def attend(s):
                    pe.wait_ge(*after("h1_scaled", it, s))
                    for t in range(TILES):
                        pe.wait_ge(*attended(it, s, t))
                        last = pe.matmul(B[s][:, 2, :], F[s][:, 1, part(t)], PT[s][:, t, :], start=(t == 0),
                                         stop=(t == TILES - 1))
                    last.then_inc(S["hp_banked"], 1)

                def gate(s):
                    pe.wait_ge(*after("h", it * 3, s))
                    pe.matmul(B[s][:, 3, :], col("gw1").broadcast_to([P, P]), HT[s][:, :], start=True, stop=False)
                    pe.wait_ge(*after("hp", it, s))
                    pe.matmul(B[s][:, 3, :], col("gw2").broadcast_to([P, P]), F[s][:, 2, :], start=False, stop=True)\
                        .then_inc(S["gate_banked"], 1)

                attend(0)
                gate(0)
                attend(1)
                pe.wait_ge(*after("y1", it, 0))
                transpose_out(0, 1, Y[0])
                gate(1)
                transpose_in(0, it * 4 + 2)
                pe.wait_ge(*after("y1", it, 1))
                transpose_out(1, 1, Y[1])

                for n in range(LAYERS2 * SLOTS + 1):
                    s, layer = n % SLOTS, n // SLOTS
                    o, before = (n - 1) % SLOTS, (n - 1) // SLOTS
                    turn = it * LAYERS2 + layer
                    h, agg, agg_o = (HH[s], HL[s]), (R[s][:, 2, :], R[s][:, 3, :]), (R[o][:, 2, :], R[o][:, 3, :])
                    if n < LAYERS2 * SLOTS:
                        if layer == 0:
                            pe.wait_ge(*after("h", it * 3 + 1, s))
                        else:
                            pe.wait_ge(*after("h_new", it * (LAYERS2 + 1) + layer - 1, s))
                        for t in range(TILES):
                            last = pe.transpose(B[s][:, 0, part(t)], HT[s][:, part(t)], ident[:, :])
                        last.then_inc(S["hn_rows"], 1)
                    if n >= 1:
                        mm3(B[o][:, 0, :], W("WI2", 3 * before + 1), agg_o, start=False).then_inc(S["z_banked"], 1)
                    if n < LAYERS2 * SLOTS:
                        if layer == 0:
                            pe.wait_ge(*after("h_low", it * 4 + 2, s))
                        else:
                            pe.wait_ge(*after("h_new_low", it * (LAYERS2 - 1) + layer - 1, s))
                        mm3(B[s][:, 2, :], W("hh2", 0), h, stop=False)
                        pe.wait_ge(*after("rows_low", turn, s))
                        pe.wait_ge(*after("adjacency", it, s))
                        for t in range(TILES):
                            for k in range(2):
                                last = pe.matmul(B[s][:, 1, :], R[s][:, k, part(t)], AN[s][:, t, :],
                                                 start=(t == 0 and k == 0), stop=(t == TILES - 1 and k == 1))
                        last.then_inc(S["agg_banked"], 1)
                        mm3(B[s][:, 3, :], W("hh2", 2), h).then_inc(S["hn_banked"], 1)
                        mm3(B[s][:, 0, :], W("hh2", 1), h, stop=False)
                        if n == LAYERS2 * SLOTS - 1:
                            pe.wait_ge(*after("h_new", it * (LAYERS2 + 1) + LAYERS2 - 1, 0))
                            transpose_out(0, 2, HT[0])
                        if n == 0:
                            transpose_in(1, it * 4 + 2)
                        pe.wait_ge(*after("agg_low", turn, s))
                        mm3(B[s][:, 2, :], W("WI2", 3 * layer), agg, start=False).then_inc(S["r_banked"], 1)
                        mm3(B[s][:, 1, :], W("WI2", 3 * layer + 2), agg).then_inc(S["in_banked"], 1)
                for s in SL:
                    transpose_in(s, it * 4 + 3)
                    pe.wait_ge(*after("h_low", it * 4 + 3, s))
                    pe.wait_ge(*after("residual", it * 4 + 2, s))
                    mm3(B[s][:, 1, :], W("c1"), (HH[s], HL[s])).then_inc(S["c1_banked"], 1)
                    for t in range(TILES):
                        mm3(B[s][:, 3, part(t)], (HH[s][:, part(t)], HL[s][:, part(t)]), W("msg"), stop=False)
                        last = pe.matmul(B[s][:, 3, part(t)], rows[0:1, 1, :], rows[0:1, 0, :], start=False, stop=True)
                    last.then_inc(S["msg_banked"], 1)
                    if s == 0:
                        pe.wait_ge(*after("h_new", it * (LAYERS2 + 1) + LAYERS2 - 1, 1))
                        transpose_out(1, 2, HT[1])
                    pe.wait_ge(*after("h", it * 3 + 2, s))
                    pe.matmul(B[s][0:5, 2, :], cols[:, CI["se0"]:CI["se0"] + 5], HT[s][:, :])\
                        .then_inc(S["s3_banked"], 1)
                for s in SL:
                    pe.wait_ge(*after("sq3", it, s))
                    pe.matmul(B[s][0:5, 0, :], se2[:, :], HT[s][:, :], start=True, stop=False)
                    pe.matmul(B[s][0:5, 2, :], neg5[:, 1, :], F[s][0:5, 2, :], start=False, stop=True,
                              skip_group_check=True).then_inc(S["aug_banked"], 1)
                    pe.matmul(B[s][0:5, 0, :], neg5[:, 0, :], F[s][0:5, 2, :], start=False, stop=True)\
                        .then_inc(S["aug_banked"], 1)
                for t in range(TILES):
                    for s in SL:
                        if t == 0:
                            pe.wait_ge(*after("aug", it, s))
                            pe.wait_ge(*after("c1_low", it, s))
                        if t >= 2:
                            pe.wait_ge(*after("dist_exped", it, s, t - 1))
                        pe.matmul(B[s][:, t % 2, :], F[s][0:5, 1, part(t)], F[s][0:5, 0, :])\
                            .then_inc(S["dist_banked"], 1)
                for s in SL:
                    for k in range(TAPS):
                        last = mm3(B[s][:, 2, :], W("c2", k), (C1[s][:, 0, k:k + NODES], C1[s][:, 1, k:k + NODES]),
                                   start=(k == 0), stop=(k == TAPS - 1))
                    last.then_inc(S["c2_banked"], 1)
                    pe.wait_ge(*after("msg", it, s))
                    for t in range(TILES):
                        pe.wait_ge(*after("weights3", it, s, t + 1))
                        last = pe.matmul(B[s][:, 3, :], F[s][:, 7, part(t)], PT[s][:, t, :], start=(t == 0),
                                         stop=(t == TILES - 1))
                    last.then_inc(S["nmp_banked"], 1)
                for s in SL:
                    if s == 1:
                        pe.wait_ge(*after("r", it * (LAYERS2 + 1) + LAYERS2, 0))
                        transpose_in(0, it * 4 + 4)
                    h, c, n = (HH[s], HL[s]), (R[s][:, 0, :], R[s][:, 1, :]), (R[s][:, 2, :], R[s][:, 3, :])
                    pe.wait_ge(*after("dist_exped", it, s))
                    mm3(B[s][:, 0, :], W("hh3", 0), h, stop=False)
                    mm3(B[s][:, 1, :], W("hh3", 1), h, stop=False)
                    pe.wait_ge(*after("xc_low", it, s))
                    mm3(B[s][:, 2, :], W("hh3", 2), h).then_inc(S["hn_banked"], 1)
                    mm3(B[s][:, 0, :], W("ih3c", 0), c, start=False, stop=False)
                    mm3(B[s][:, 1, :], W("ih3c", 1), c, start=False, stop=False)
                    pe.wait_ge(*after("nmp_low", it, s))
                    mm3(B[s][:, 0, :], W("ih3n", 0), n, start=False).then_inc(S["r_banked"], 1)
                    mm3(B[s][:, 3, :], W("ih3c", 2), c, stop=False)
                    mm3(B[s][:, 3, :], W("ih3n", 2), n, start=False).then_inc(S["in_banked"], 1)
                    mm3(B[s][:, 1, :], W("ih3n", 1), n, start=False).then_inc(S["z_banked"], 1)
                pe.wait_ge(*after("h_new", it * (LAYERS2 + 1) + LAYERS2, 0))
                transpose_out(0, 3, Y[0])
                pe.wait_ge(*after("r", it * (LAYERS2 + 1) + LAYERS2, 1))
                transpose_in(1, it * 4 + 4)
                pe.wait_ge(*after("h_new", it * (LAYERS2 + 1) + LAYERS2, 1))
                transpose_out(1, 3, Y[1])

        @block.scalar
        def _(act):
            act.wait_ge(w_loaded, 8 * 16)
            act.wait_ge(setup_dve, 3)
            act.activation(WH[:, 0:WFIRST], stage[0], ACT.Copy).then_inc(w_split, 1)
            act.activation(WH[:, WFIRST:WALL], stage[1][:, 0:WALL - WFIRST], ACT.Copy).then_inc(w_split, 1)
            act.activation(VQH[:, :], VQ[:, :], ACT.Copy).then_inc(setup_act, 1)
            act.wait_ge(setup_dve, 7)

            def h_high(s, turn):
                act.wait_ge(*after("h_banked", turn, s))
                act.activation(HH[s], B[s][:, 0, :], ACT.Relu).then_inc(S["h_high"], 1)

            for s in SL:
                h_high(s, 0)
            with act.Fori(0, ROUNDS) as it:
                def g_copy(s, t):
                    act.wait_ge(*after("g_banked", it, s, 2 * t + 1))
                    act.activation(G[s][:, t, 0:4 * DIM], B[t % 2][:, 2, :], ACT.Copy).then_inc(S["g_act"], 1)

                def relu(u, t):
                    h, s = u // SLOTS, u % SLOTS
                    act.wait_ge(*after("masked", it * HEADS + h, s, t + 1))
                    if u >= 1:
                        act.wait_ge(*after("lifted", it * HEADS + (u - 1) // SLOTS, (u - 1) % SLOTS, t + 1))
                    act.activation(RELU[:, t, :], SC[u % 3][:, t, :], ACT.Relu, bias=Q99[s][:, t, h:h + 1], scale=99.0)\
                        .then_inc(S["relu"], 1)

                def softmax_exp(u, t):
                    h, s = u // SLOTS, u % SLOTS
                    turn = it * HEADS + h
                    if t == 0:
                        act.wait_ge(*after("exp_bias", turn, s))
                    act.wait_ge(*after("lifted", turn, s, t + 1))
                    act.activation(SC[u % 3][:, t, :], SC[u % 3][:, t, :], ACT.Exp, bias=nmx[s][:, t:t + 1], scale=0.01,
                                   accum_out=den[s][:, t:t + 1]).then_inc(S["exped"], 1)

                def tile_copy(u, j):
                    h, s = u // SLOTS, u % SLOTS
                    turn = it * HEADS + h
                    if h >= 1:
                        act.wait_ge(*after("o_banked", turn - 1, s))
                    act.wait_ge(*after("pt_banked", turn, s, j + 1))
                    act.activation(PT[s][:, j, :], B[j % 2][:, 1, :], ACT.Copy).then_inc(S["pt_act"], 1)

                UNITS = HEADS * SLOTS
                for u in range(-1, UNITS + 1):
                    for t in range(TILES):
                        if u + 1 < UNITS:
                            relu(u + 1, t)
                        if 0 <= u < UNITS:
                            softmax_exp(u, t)
                        if t == TILES - 1 and 0 <= u - 1 < UNITS:
                            tile_copy(u - 1, t)
                        if u + 1 < SLOTS:
                            g_copy(u + 1, t)
                for s in SL:
                    act.wait_ge(*after("o_added", it * HEADS + HEADS - 1, s))
                    act.activation(Y[s], acc[s], ACT.Tanh, scale=0.5).then_inc(S["tanh0"], 1)

                def h1_high(s):
                    act.wait_ge(*after("h1_banked", it, s))
                    act.activation(R[s][:, 0, :], B[s][:, 1, :], ACT.Identity, bias=col("Wb")).then_inc(S["h1_high"], 1)

                def t1_high(s):
                    act.wait_ge(*after("t1_banked", it, s))
                    act.activation(R[s][:, 2, :], B[s][:, 2, :], ACT.Copy).then_inc(S["t1_high"], 1)

                h_high(0, it * 4 + 1)
                h1_high(0)
                h_high(1, it * 4 + 1)
                t1_high(0)
                h1_high(1)
                t1_high(1)
                for s in SL:
                    for t in range(TILES):
                        act.wait_ge(*after("s_negmax", it, s, t + 1))
                        act.activation(U[s][:, t, :], U[s][:, t, :], ACT.Exp, bias=nmx[s][:, t:t + 1],
                                       accum_out=den[s][:, t:t + 1]).then_inc(S["s_exped"], 1)
                for s in SL:
                    act.wait_ge(*after("hp_banked", it, s))
                    act.activation(F[s][:, 2, :], B[s][:, 2, :], ACT.Relu).then_inc(S["hp"], 1)
                    act.wait_ge(*after("gate_banked", it, s))
                    act.activation(F[s][:, 3, :], B[s][:, 3, :], ACT.Tanh, bias=dcol("gb"), scale=0.5)\
                        .then_inc(S["gate"], 1)

                def gate_act(s, cell, signal, bank, tile, bias, func):
                    act.wait_ge(*after(signal + "_banked", cell, s))
                    act.activation(F[s][:, tile, :], B[s][:, bank, :], func, bias=dcol(bias), scale=0.5)\
                        .then_inc(S[signal], 1)

                def cand_act(s, cell, bias):
                    act.wait_ge(*after("cand_b", cell, s))
                    act.activation(F[s][:, 4, :], F[s][:, 3, :], ACT.Tanh, bias=col(bias)).then_inc(S["cand"], 1)

                def h_of(s):
                    act.wait_ge(*after("h_banked", it * 4 + 2, s))
                    act.activation(HT[s][:, :], B[s][:, 0, :], ACT.Relu).then_inc(S["h"], 1)
                    act.wait_ge(*after("h", it * 3 + 1, s))
                    act.activation(HH[s], HT[s][:, :], ACT.Copy).then_inc(S["h_high"], 1)

                h_of(0)
                for n in range(LAYERS2 * SLOTS + 1):
                    s, layer = n % SLOTS, n // SLOTS
                    o, before = (n - 1) % SLOTS, (n - 1) // SLOTS
                    turn, cell = it * LAYERS2 + layer, it * (LAYERS2 + 1) + layer
                    cell_o = it * (LAYERS2 + 1) + before
                    start, end = n < LAYERS2 * SLOTS, n >= 1
                    if start:
                        act.wait_ge(*after("hn_rows", turn, s))
                        act.activation(R[s][:, 0, :], B[s][:, 0, :], ACT.Copy).then_inc(S["rows_high"], 1)
                    if end:
                        gate_act(o, cell_o, "z", 0, 1, "rz2z", ACT.Tanh)
                    if n == LAYERS2 * SLOTS:
                        h_high(0, it * 4 + 3)
                    if end:
                        cand_act(o, cell_o, "bih2n")
                    if start:
                        act.wait_ge(*after("agg_banked", turn, s))
                        act.activation(R[s][:, 2, :], B[s][:, 1, :], ACT.Copy).then_inc(S["agg_high"], 1)
                        gate_act(s, cell, "hn", 3, 2, "hn2", ACT.Identity)
                    if n == 0:
                        h_of(1)
                    if end and before < LAYERS2 - 1:
                        act.wait_ge(*after("h_new", cell_o, o))
                        act.activation(HH[o], HT[o][:, :], ACT.Copy).then_inc(S["h_new_high"], 1)
                    if start:
                        gate_act(s, cell, "r", 2, 0, "rz2r", ACT.Tanh)

                for s in SL:
                    if s == 1:
                        h_high(1, it * 4 + 3)
                    act.wait_ge(*after("c1_banked", it, s))
                    act.activation(F[s][:, 6, :], B[s][:, 1, :], ACT.Relu, bias=dcol("sh1"), scale=dcol("s1"))\
                        .then_inc(S["c1_high"], 1)
                    act.activation(C1[s][:, 0, PAD:PAD + NODES], B[s][:, 1, :], ACT.Relu, bias=dcol("sh1"),
                                   scale=dcol("s1")).then_inc(S["c1_high"], 1)
                    act.wait_ge(*after("msg_banked", it, s))
                    act.activation(F[s][:, 7, :], B[s][:, 3, :], ACT.Relu).then_inc(S["msg"], 1)
                    act.wait_ge(*after("s3_banked", it, s))
                    act.activation(F[s][0:5, 2, :], B[s][0:5, 2, :], ACT.Square, bias=cols[0:5, CI["bse"]:CI["bse"] + 1])\
                        .then_inc(S["sq3"], 1)
                for s in SL:
                    act.wait_ge(*after("aug_banked", it, s, 1))
                    act.activation(F[s][0:5, 0, :], B[s][0:5, 2, :], ACT.Identity,
                                   bias=dcols[0:5, DI["bias2"]:DI["bias2"] + 1]).then_inc(S["aug"], 1)
                    act.wait_ge(*after("aug_banked", it, s, 2))
                    act.activation(F[s][0:5, 1, :], B[s][0:5, 0, :], ACT.Identity,
                                   bias=dcols[0:5, DI["bias1"]:DI["bias1"] + 1]).then_inc(S["aug"], 1)
                for t in range(TILES):
                    for s in SL:
                        act.wait_ge(*after("dist_banked", it, s, t + 1))
                        act.activation(U[s][:, t, :], B[s][:, t % 2, :], ACT.Exp).then_inc(S["dist_exped"], 1)
                for s in SL:
                    act.wait_ge(*after("c2_scaled", it, s))
                    act.activation(F[s][:, 4, :], F[s][:, 3, :], ACT.Relu, bias=dcol("sh2")).then_inc(S["xc_high"], 1)
                    act.activation(R[s][:, 0, :], F[s][:, 3, :], ACT.Relu, bias=dcol("sh2")).then_inc(S["xc_high"], 1)
                    act.wait_ge(*after("nmp_banked", it, s))
                    act.activation(R[s][:, 2, :], B[s][:, 3, :], ACT.Copy).then_inc(S["nmp_high"], 1)
                cell = it * (LAYERS2 + 1) + LAYERS2
                for s in SL:
                    gate_act(s, cell, "hn", 2, 2, "hn3", ACT.Identity)
                    gate_act(s, cell, "r", 0, 0, "rz3r", ACT.Tanh)
                    if s == 1:
                        h_high(0, it * 4 + 4)
                    gate_act(s, cell, "z", 1, 1, "rz3z", ACT.Tanh)
                    cand_act(s, cell, "bih3n")
                h_high(1, it * 4 + 4)

        @block.vector
        def _(dve):
            for s in SL:
                dve.memset(X[s][:, :, :], 0.0).then_inc(x_free[s], 16)
            dve.wait_ge(w_loaded, 8 * 16)

            def c2(a, n=1):
                return cols[:, CI[a]:CI[a] + n]

            def d2(a, n=1):
                return dcols[:, DI[a]:DI[a] + n]

            dve.tensor_scalar(d2("t1", 2), c2("v1", 2), EPS, None, ALU.add).then_inc(setup_dve, 1)
            dve.tensor_tensor(d2("qkw"), c2("qw"), c2("kw"), ALU.add)
            for l in "23":
                dve.tensor_tensor(d2(f"rz{l}r", 2), c2(f"bih{l}r", 2), c2(f"bhh{l}r", 2), ALU.add)
                dve.tensor_scalar(d2(f"hn{l}"), c2(f"bhh{l}n"), 0.5, None, ALU.mult)
            dve.tensor_scalar(d2("gb"), c2("gateb"), 0.5, None, ALU.mult)
            dve.tensor_tensor(d2("bias2"), c2("bse"), c2("e3"), ALU.add)
            dve.tensor_scalar(se2[:, :], c2("se0", 5), 2.0, None, ALU.mult)
            dve.tensor_tensor(d2("tq"), c2("qb"), c2("kb"), ALU.add)
            asym = stage[1][:, WCOL["As"] - WFIRST:WCOL["As"] - WFIRST + DIM]
            dve.tensor_tensor(asym, asym, xin[1][:, 0, :], ALU.add)
            dve.scalar_tensor_tensor(d2("bias1"), c2("bse"), 2.0, c2("e4"), ALU.mult, ALU.add).then_inc(setup_dve, 1)
            dve.wait_ge(setup_dve, 2)
            for l in "23":
                dve.tensor_scalar(d2(f"rz{l}r", 2), d2(f"rz{l}r", 2), 0.5, None, ALU.mult)
            dve.wait_ge(setup_pe, 1)
            dve.tensor_copy(F[1][:, 0:2, :], B[0][:, 0:2, :])
            for layer, (b, bank) in enumerate(WI2_BANKS):
                dve.tensor_copy(stage[0][:, layer * 3 * DIM:(layer + 1) * 3 * DIM], B[b][:, bank, P:4 * P])
            dve.tensor_copy(VQ[:, :].rearrange("p (a h) -> p a h", a=2), B[0][:, 2, 0:2 * HEADS].rearrange("p (h a) -> p a h", a=2)).then_inc(setup_dve, 1)
            dve.memset(CQ[:, :], 0.0).then_inc(setup_dve, 1)
            dve.wait_ge(setup_dve, 4)
            dve.tensor_scalar(CQ[:, 0:HEADS], B[0][:, 3, 0:HEADS], d2("tq"), None, ALU.add)
            dve.tensor_copy(ob[:, :], B[1][:, 0, 0:DIM])
            dve.wait_ge(setup_pool, 3)
            dve.tensor_tensor(d2("s1", 2), c2("g1", 2), d2("r1", 2), ALU.mult).then_inc(setup_dve, 1)
            dve.wait_ge(setup_dve, 5)
            dve.tensor_tensor(d2("t1", 2), c2("m1", 2), d2("s1", 2), ALU.mult).then_inc(setup_dve, 1)
            dve.wait_ge(w_split, 1)
            dve.tensor_tensor(WLO[:, 0:WFIRST], stage[0], WH[:, 0:WFIRST].bitcast(F32),
                              ALU.subtract).then_inc(w_split, 1)
            dve.wait_ge(setup_dve, 6)
            dve.tensor_tensor(d2("sh1", 2), c2("b1", 2), d2("t1", 2), ALU.subtract)
            dve.wait_ge(setup_act, 1)
            dve.tensor_tensor(VQL[:, :], VQ[:, :], VQH[:, :].bitcast(F32), ALU.subtract).then_inc(setup_dve, 1)
            dve.wait_ge(w_split, 3)
            dve.tensor_tensor(WLO[:, WFIRST:WALL], stage[1][:, 0:WALL - WFIRST],
                              WH[:, WFIRST:WALL].bitcast(F32), ALU.subtract).then_inc(w_split, 1)

            def norm_stats(s, turn, src):
                if src is X:
                    dve.wait_ge(*after("residual", turn - 1, s))
                for t in range(TILES):
                    last = dve.bn_stats(bst[s][:, t, :], src[s][:, t, :])
                last.then_inc(S["stats"], 1)
                dve.wait_ge(*after("stats", turn, s))
                dve.memset(tick_dve[:, 0, s:s + 1], 0.0)
                for t in range(TILES):
                    last = dve.bn_aggr(mv[s][:, t, :], bst[s][:, t, :])
                last.then_inc(S["aggregated"], 1)
                dve.wait_ge(*after("aggregated", turn, s))
                dve.tensor_scalar(var[s][:, :], mv[s][:, :, 1], EPS, None, ALU.add).then_inc(S["variance"], 1)

            def norm_scale(s, turn, src):
                dve.wait_ge(*after("rstd", turn, s))
                for t in range(TILES):
                    last = dve.tensor_scalar(hN[s][:, part(t)], src[s][:, t, :], mv[s][:, t, 0:1], rstd[s][:, t:t + 1],
                                             ALU.subtract, ALU.mult)
                last.then_inc(S["normed"], 1)

            def h_low(s, turn):
                dve.wait_ge(*after("h_high", turn, s))
                dve.scalar_tensor_tensor(HL[s], B[s][:, 0, :], 0.0, HH[s].bitcast(F32), ALU.max, ALU.subtract)\
                    .then_inc(S["h_low"], 1)

            for s in SL:
                dve.wait_ge(loaded["xin"][s], 16)
                norm_stats(s, 0, xin)
            for s in SL:
                norm_scale(s, 0, xin)
            for s in SL:
                h_low(s, 0)
            with dve.Fori(0, ROUNDS) as it:
                def add_residual(s, layer):
                    turn = it * 4 + layer
                    if layer == 0:
                        dve.wait_ge(*after("tanh0", it, s))
                        dve.wait_ge(*after("x_half", it, s))
                        last = dve.scalar_tensor_tensor(X[s][:, :, :], Y[s].rearrange("p (t n) -> p t n", t=TILES), 0.5,
                                                        X[s][:, :, :], ALU.mult, ALU.add)
                    else:
                        dve.wait_ge(*after("y_banked", it * 3 + layer - 1, s))
                    y = B[s][:, 1, :].rearrange("p (t n) -> p t n", t=TILES)
                    if layer == 2:
                        dve.wait_ge(loaded["nmask"][s], it * 16 + 16)
                        for t in range(TILES):
                            last = dve.scalar_tensor_tensor(X[s][:, t, :], y[:, t, :], nm[s][:, t:t + 1], X[s][:, t, :],
                                                            ALU.mult, ALU.add)
                    elif layer > 0:
                        last = dve.tensor_tensor(X[s][:, :, :], y, X[s][:, :, :], ALU.add)
                    last.then_inc(S["residual"], 1)

                def query_keys(s):
                    dve.wait_ge(*after("qk_banked", it, s))
                    dve.tensor_tensor(QK[s][:, :, :], B[s][:, 1, 0:64].rearrange("p (t c) -> p t c", t=TILES),
                                      CQ[:, :].unsqueeze(1).broadcast_to([P, TILES, 2 * HEADS]), ALU.add).then_inc(S["qk"], 1)
                    dve.wait_ge(*after("qk", it, s))
                    dve.tensor_scalar(Q99[s][:, :, :], QK[s][:, :, 0:HEADS], 99.0, None, ALU.mult).then_inc(S["q99"], 1)

                def g_copy(s, t):
                    dve.wait_ge(*after("g_banked", it, s, 2 * t + 2))
                    dve.tensor_copy(G[s][:, t, 4 * DIM:8 * DIM], B[t % 2][:, 3, :]).then_inc(S["g_dve"], 1)

                def masked_keys(u, t):
                    h, s = u // SLOTS, u % SLOTS
                    turn = it * HEADS + h
                    if t == 0:
                        if h == 0:
                            dve.wait_ge(*after("mask0", it, s))
                        if u >= 3:
                            dve.wait_ge(*after("pt_banked", it * HEADS + (u - 3) // SLOTS, (u - 3) % SLOTS))
                        dve.wait_ge(*after("kb_banked", turn, s))
                        dve.memset(tick_dve[:, 1, s:s + 1], 0.0)
                    dve.tensor_tensor_reduce(out=SC[u % 3][:, t, :], in0=adjN[s][:, t, :], in1=B[s][:, 0, :], scale=1.0,
                                             scalar=-3.0e38, op0=ALU.add, op1=ALU.max,
                                             accum_out=kmax[s][:, t:t + 1]).then_inc(S["masked"], 1)

                def exp_bias(u):
                    h, s = u // SLOTS, u % SLOTS
                    turn = it * HEADS + h
                    dve.wait_ge(*after("masked", turn, s))
                    dve.scalar_tensor_tensor(kq[s][:, :], kmax[s][:, :], -1.0, QK[s][:, :, h], ALU.mult, ALU.subtract)\
                        .then_inc(S["kmax_q"], 1)
                    dve.wait_ge(*after("kmax_q", turn, s))
                    dve.scalar_tensor_tensor(kmax[s][:, :], kq[s][:, :], 0.01, kq[s][:, :], ALU.mult, ALU.min)\
                        .then_inc(S["neg_max"], 1)
                    if u >= 2:
                        dve.wait_ge(*after("exped", turn - 1, s))
                    dve.wait_ge(*after("neg_max", turn, s))
                    dve.scalar_tensor_tensor(nmx[s][:, :], QK[s][:, :, h], 0.01, kmax[s][:, :], ALU.mult, ALU.add)\
                        .then_inc(S["exp_bias"], 1)

                def denominators(u):
                    h, s = u // SLOTS, u % SLOTS
                    dve.wait_ge(*after("exped", it * HEADS + h, s))
                    dve.reciprocal(rden[s][:, :], den[s][:, :]).then_inc(S["rden"], 1)

                def tile_copy(u, j):
                    h, s = u // SLOTS, u % SLOTS
                    turn = it * HEADS + h
                    if h >= 1 and j == 0:
                        dve.wait_ge(*after("o_banked", turn - 1, s))
                    dve.wait_ge(*after("pt_banked", turn, s, j + 1))
                    dve.tensor_copy(PT[s][:, j, :], B[j % 2][:, 1, :]).then_inc(S["pt_dve"], 1)

                def add_head(u):
                    h, s = u // SLOTS, u % SLOTS
                    turn = it * HEADS + h
                    if h == 0:
                        dve.wait_ge(*after("acc_start", it, s))
                    else:
                        dve.wait_ge(*after("o_added", turn - 1, s))
                    dve.wait_ge(*after("rden", turn, s))
                    dve.wait_ge(*after("o_banked", turn, s))
                    for t in range(TILES):
                        last = dve.scalar_tensor_tensor(acc[s][:, part(t)], B[s][:, 2 + h % 2, part(t)], rden[s][:, t:t + 1],
                                                        acc[s][:, part(t)], ALU.mult, ALU.add)
                    last.then_inc(S["o_added"], 1)

                UNITS = HEADS * SLOTS
                for s in SL:
                    query_keys(s)
                for s in SL:
                    dve.scalar_tensor_tensor(acc[s].rearrange("p (t n) -> p t n", t=TILES),
                                             hN[s][:, :].rearrange("p (t n) -> p t n", t=TILES), 0.0,
                                             ob[:, :].unsqueeze(1).broadcast_to([P, TILES, DIM]), ALU.max, ALU.add)\
                        .then_inc(S["acc_start"], 1)
                for u in range(-1, UNITS + 2):
                    for t in range(TILES):
                        if u + 1 < UNITS:
                            masked_keys(u + 1, t)
                        if u + 1 < SLOTS:
                            g_copy(u + 1, t)
                        if t < TILES - 1 and 0 <= u - 1 < UNITS:
                            tile_copy(u - 1, t)
                    if 0 <= u - 1 < UNITS:
                        denominators(u - 1)
                    if u + 1 < UNITS:
                        exp_bias(u + 1)
                    if 0 <= u - 2 < UNITS:
                        add_head(u - 2)
                    if u == UNITS:
                        add_residual(0, 0)
                        norm_stats(0, it * 4 + 1, X)
                    if u == UNITS + 1:
                        norm_scale(0, it * 4 + 1, X)
                    if u == 1:
                        for s in SL:
                            dve.wait_ge(x_free[s], it * 16 + 16)
                            dve.tensor_scalar(X[s][:, :, :], xin[s][:, :, :], 0.5, None, ALU.add).then_inc(S["x_half"], 1)
                add_residual(1, 0)

                def mask1(s):
                    dve.wait_ge(loaded["adjT"][s], it * 16 + 16)
                    dve.tensor_scalar(U[s][:, :, :], adjT[s][:, :, :], 0.0, NEG1, ALU.is_le, ALU.mult)\
                        .then_inc(S["mask1"], 1)

                def h1_low(s):
                    dve.wait_ge(*after("h1_high", it, s))
                    dve.scalar_tensor_tensor(R[s][:, 1, :], B[s][:, 1, :], col("Wb"), R[s][:, 0, :].bitcast(F32), ALU.add,
                                             ALU.subtract).then_inc(S["h1_low"], 1)

                def t1_low(s):
                    dve.wait_ge(*after("t1_high", it, s))
                    dve.tensor_tensor(R[s][:, 3, :], B[s][:, 2, :], R[s][:, 2, :].bitcast(F32), ALU.subtract)\
                        .then_inc(S["t1_low"], 1)

                def masked_scores(s, t):
                    if t == 0:
                        dve.wait_ge(*after("mask1", it, s))
                    dve.wait_ge(*after("s_banked", it, s, t + 1))
                    dve.memset(tick_dve[:, 2 + t, s:s + 1], 0.0)
                    dve.tensor_tensor_reduce(out=U[s][:, t, :], in0=U[s][:, t, :], in1=B[s][:, t % 2, :], scale=1.0,
                                             scalar=-3.0e38, op0=ALU.add, op1=ALU.max,
                                             accum_out=kmax[s][:, t:t + 1]).then_inc(S["s_masked"], 1)

                def negative_max(s, t):
                    dve.wait_ge(*after("s_masked", it, s, t + 1))
                    dve.tensor_scalar(nmx[s][:, t:t + 1], kmax[s][:, t:t + 1], -1.0, None, ALU.mult)\
                        .then_inc(S["s_negmax"], 1)

                def attention(s, t):
                    dve.wait_ge(*after("s_exped", it, s, t + 1))
                    dve.tensor_tensor(PT[s][:, t, :], U[s][:, t, :], adjT[s][:, t, :], ALU.mult)\
                        .then_inc(S["att_dve"], 1)

                def scaled_h1(s):
                    dve.wait_ge(*after("s_exped", it, s))
                    dve.reciprocal(rden[s][:, :], den[s][:, :]).then_inc(S["rden1"], 1)
                    dve.wait_ge(*after("rden1", it, s))
                    dve.wait_ge(*after("h1n_banked", it, s))
                    for t in range(TILES):
                        last = dve.tensor_scalar(F[s][:, 1, part(t)], B[s][:, 3, part(t)], rden[s][:, t:t + 1], None, ALU.mult)
                    last.then_inc(S["h1_scaled"], 1)

                norm_stats(1, it * 4 + 1, X)
                h_low(0, it * 4 + 1)
                norm_scale(1, it * 4 + 1, X)
                mask1(0)
                h1_low(0)
                h_low(1, it * 4 + 1)
                mask1(1)
                t1_low(0)
                h1_low(1)
                masked_scores(0, 0)
                t1_low(1)
                for t in range(1, TILES):
                    masked_scores(0, t)
                    negative_max(0, t - 1)
                masked_scores(1, 0)
                negative_max(0, TILES - 1)
                masked_scores(1, 1)
                negative_max(1, 0)
                attention(0, 1)
                masked_scores(1, 2)
                negative_max(1, 1)
                scaled_h1(0)
                masked_scores(1, 3)
                negative_max(1, 2)
                attention(0, 3)
                negative_max(1, 3)
                attention(1, 1)
                scaled_h1(1)
                attention(1, 3)

                def gate_mix(s):
                    dve.wait_ge(*after("gate", it, s))
                    dve.wait_ge(*after("h_less_hp", it, s))
                    dve.scalar_tensor_tensor(F[s][:, 5, :], F[s][:, 3, :], 1.0, F[s][:, 4, :], ALU.add, ALU.mult)\
                        .then_inc(S["gate_e"], 1)
                    dve.wait_ge(*after("gate_e", it, s))
                    dve.scalar_tensor_tensor(Y[s], F[s][:, 5, :], 0.5, F[s][:, 2, :], ALU.mult, ALU.add)\
                        .then_inc(S["y1"], 1)

                def less_hp(s):
                    dve.wait_ge(*after("h", it * 3, s))
                    dve.wait_ge(*after("hp", it, s))
                    dve.tensor_tensor(F[s][:, 4, :], HT[s][:, :], F[s][:, 2, :], ALU.subtract).then_inc(S["h_less_hp"], 1)

                def nonzero(s):
                    dve.wait_ge(loaded["adjN"][s], it * 32 + 32)
                    dve.wait_ge(*after("hp_banked", it, s))
                    dve.tensor_scalar(AN[s][:, :, :], adjN[s][:, :, :], 0.0, None, ALU.not_equal)\
                        .then_inc(S["adjacency"], 1)

                def h_low_of_h(s):
                    dve.wait_ge(*after("h_high", it * 4 + 2, s))
                    dve.tensor_tensor(HL[s], HT[s][:, :], HH[s].bitcast(F32), ALU.subtract).then_inc(S["h_low"], 1)

                def rows_low(s, turn):
                    dve.wait_ge(*after("rows_high", turn, s))
                    dve.tensor_tensor(R[s][:, 1, :], B[s][:, 0, :], R[s][:, 0, :].bitcast(F32), ALU.subtract)\
                        .then_inc(S["rows_low"], 1)

                less_hp(0)
                gate_mix(0)
                add_residual(0, 1)
                norm_stats(0, it * 4 + 2, X)
                less_hp(1)
                norm_scale(0, it * 4 + 2, X)
                gate_mix(1)
                nonzero(0)
                h_low_of_h(0)
                add_residual(1, 1)
                norm_stats(1, it * 4 + 2, X)
                rows_low(0, it * LAYERS2)
                norm_scale(1, it * 4 + 2, X)

                def cand_a(s, cell):
                    dve.wait_ge(*after("hn", cell, s))
                    dve.wait_ge(*after("r", cell, s))
                    dve.scalar_tensor_tensor(F[s][:, 3, :], F[s][:, 0, :], 1.0, F[s][:, 2, :], ALU.add, ALU.mult)\
                        .then_inc(S["cand_a"], 1)

                def cand_b(s, cell, in_bank):
                    dve.wait_ge(*after("cand_a", cell, s))
                    dve.wait_ge(*after("in_banked", cell, s))
                    dve.tensor_tensor(F[s][:, 3, :], B[s][:, in_bank, :], F[s][:, 3, :], ALU.add).then_inc(S["cand_b"], 1)

                def cell_zh(s, cell):
                    dve.wait_ge(*after("z", cell, s))
                    dve.scalar_tensor_tensor(F[s][:, 5, :], F[s][:, 1, :], 1.0, HT[s][:, :], ALU.add, ALU.mult)\
                        .then_inc(S["zh"], 1)
                    dve.tensor_scalar(F[s][:, 6, :], F[s][:, 1, :], -0.5, 0.5, ALU.mult, ALU.add).then_inc(S["z_rest"], 1)

                def cell_end(s, cell, dst):
                    dve.wait_ge(*after("cand", cell, s))
                    dve.wait_ge(*after("z_rest", cell, s))
                    dve.tensor_tensor(F[s][:, 4, :], F[s][:, 6, :], F[s][:, 4, :], ALU.mult).then_inc(S["z_cand"], 1)
                    dve.wait_ge(*after("z_cand", cell, s))
                    dve.scalar_tensor_tensor(dst, F[s][:, 5, :], 0.5, F[s][:, 4, :], ALU.mult, ALU.add)\
                        .then_inc(S["h_new"], 1)

                for n in range(LAYERS2 * SLOTS + 1):
                    s, layer = n % SLOTS, n // SLOTS
                    o, before = (n - 1) % SLOTS, (n - 1) // SLOTS
                    turn, cell = it * LAYERS2 + layer, it * (LAYERS2 + 1) + layer
                    cell_o = it * (LAYERS2 + 1) + before
                    start, end = n < LAYERS2 * SLOTS, n >= 1
                    if end:
                        cand_a(o, cell_o)
                    if start and n > 0:
                        rows_low(s, turn)
                    if n == LAYERS2 * SLOTS:
                        norm_scale(0, it * 4 + 3, X)
                    if end:
                        cand_b(o, cell_o, 1)
                        cell_zh(o, cell_o)
                    if n == LAYERS2 * SLOTS:
                        h_low(0, it * 4 + 3)
                    if end:
                        cell_end(o, cell_o, HT[o][:, :])
                    if start:
                        dve.wait_ge(*after("agg_high", turn, s))
                        dve.tensor_tensor(R[s][:, 3, :], B[s][:, 1, :], R[s][:, 2, :].bitcast(F32), ALU.subtract)\
                            .then_inc(S["agg_low"], 1)
                    if n == 0:
                        nonzero(1)
                        h_low_of_h(1)
                    if n == LAYERS2 * SLOTS - 1:
                        add_residual(0, 2)
                        norm_stats(0, it * 4 + 3, X)

                add_residual(1, 2)
                norm_stats(1, it * 4 + 3, X)
                norm_scale(1, it * 4 + 3, X)
                h_low(1, it * 4 + 3)
                for s in SL:
                    for edge in (0, PAD + NODES):
                        dve.memset(C1[s][:, :, edge:edge + PAD].bitcast(F32), 0.0)
                for s in SL:
                    dve.wait_ge(*after("c1_high", it, s))
                    dve.tensor_tensor(C1[s][:, 1, PAD:PAD + NODES], F[s][:, 6, :],
                                      C1[s][:, 0, PAD:PAD + NODES].bitcast(F32), ALU.subtract).then_inc(S["c1_low"], 1)
                for s in SL:
                    dve.wait_ge(loaded["xin"][s], it * 16 + 32)
                    norm_stats(s, it * 4 + 4, xin)
                for s in SL:
                    norm_scale(s, it * 4 + 4, xin)
                for s in SL:
                    dve.wait_ge(*after("c2_banked", it, s))
                    dve.wait_ge(*after("h", it * 3 + 2, s))
                    dve.scalar_tensor_tensor(F[s][:, 3, :], B[s][:, 2, :], dcol("s2"), HT[s][:, :], ALU.mult, ALU.add)\
                        .then_inc(S["c2_scaled"], 1)
                    dve.wait_ge(*after("xc_high", it, s))
                    dve.tensor_tensor(R[s][:, 1, :], F[s][:, 4, :], R[s][:, 0, :].bitcast(F32), ALU.subtract)\
                        .then_inc(S["xc_low"], 1)
                    dve.wait_ge(*after("nmp_high", it, s))
                    dve.tensor_tensor(R[s][:, 3, :], B[s][:, 3, :], R[s][:, 2, :].bitcast(F32), ALU.subtract)\
                        .then_inc(S["nmp_low"], 1)
                cell = it * (LAYERS2 + 1) + LAYERS2
                for s in SL:
                    cand_a(s, cell)
                    cell_zh(s, cell)
                    cand_b(s, cell, 3)
                    cell_end(s, cell, Y[s])
                for s in SL:
                    add_residual(s, 3)
                    h_low(s, it * 4 + 4)


def kernel(**inputs):
    import numpy as _np
    import concourse.bacc as _bacc
    from concourse import mybir as _mybir
    from concourse.bass_utils import run_bass_kernel_spmd as _run

    v = {k: _np.asarray(a) for k, a in inputs.items()}

    def wide(a):
        return _np.ascontiguousarray(a).reshape(P, -1)

    fcw = wide(v["L0_gnn_fc_w"].reshape(DIM, HEADS, DIM).transpose(2, 1, 0))
    fpw = wide(v["L0_gnn_fp_w"].reshape(HEADS, DIM, DIM).transpose(1, 0, 2))
    wraw = _np.concatenate([
        wide(v["L2_gnn_w_hh"].T), wide(v["L1_gnn_W_w"].T), wide(v["L1_gnn_A"]), wide(v["L3_gnn_conv1_w"][:, :, 0].T),
        wide(v["L3_gnn_w_msg"].T), wide(v["L3_gnn_w_ih"][:, :DIM].T), wide(v["L3_gnn_w_ih"][:, DIM:].T),
        wide(v["L3_gnn_w_hh"].T), wide(v["L1_gnn_A"].T)], axis=1)
    prew = _np.concatenate([wide(v["L2_gnn_weight"].transpose(2, 0, 1)), wide(v["L2_gnn_w_ih"].T)], axis=1)
    c2w = wide(v["L3_gnn_conv2_w"].transpose(1, 2, 0))

    def spread(a):
        return _np.broadcast_to(a.reshape(1, 1), (P, 1))

    def head(a):
        z = _np.zeros((P, 1), _np.float32)
        z[:a.size, 0] = a
        return z

    def gates(a):
        return wide(a.reshape(3, DIM).T)

    se = _np.zeros((P, 5), _np.float32)
    se[:, :3] = v["L3_gnn_w_se"].T
    unit = _np.eye(P, dtype=_np.float32)
    columns = _np.concatenate([
        wide(v["L0_gnn_fc_b"].reshape(HEADS, DIM).T), v["L0_gnn_q_w"], v["L0_gnn_k_w"], wide(v["L0_gnn_fp_b"]),
        wide(v["L1_gnn_W_b"]), spread(v["L1_gnn_gate_b"]), spread(v["L0_gnn_q_b"]), spread(v["L0_gnn_k_b"]),
        gates(v["L2_gnn_b_ih"]), gates(v["L2_gnn_b_hh"])]
        + [wide(v[f"L3_gnn_bn{i}_{c}"]) for c in "vgbm" for i in (1, 2)]
        + [gates(v["L3_gnn_b_ih"]), gates(v["L3_gnn_b_hh"]), wide(v["L1_gnn_gate_w"].reshape(2, DIM).T), se,
           head(v["L3_gnn_b_se"]), unit[:, 3:4], unit[:, 4:5]], axis=1)
    rows = _np.stack([v["L3_gnn_b_msg"], _np.ones(DIM, _np.float32)])[None]
    host = [("x", v["x"]), ("adj", v["adj"]), ("adjt", v["adj"].transpose(0, 2, 1)), ("nodemask", v["nodemask"].reshape(GRAPHS, TILES, P).transpose(0, 2, 1)),
            ("c2w", c2w), ("wraw", wraw), ("prew", prew), ("fcw", fcw), ("fpw", fpw), ("cols", columns), ("rows", rows)]
    nc = _bacc.Bacc("TRN2", target_bir_lowering=False, num_devices=1)
    arrays, args = {}, []
    for name, a in host:
        a = _np.ascontiguousarray(a)
        arrays[f"in_{name}_dram"] = a
        args.append(nc.dram_tensor(f"in_{name}_dram", a.shape, _mybir.dt.from_np(a.dtype), kind="ExternalInput").ap())
    args.append(nc.dram_tensor("out_0_dram", (GRAPHS, NODES, DIM), _mybir.dt.float32, kind="ExternalOutput").ap())
    build(nc, *args)
    r = _run(nc, [arrays], core_ids=[0])
    return r.results[0]["out_0_dram"]
```

```python
import numpy as np
import concourse.bass as bass
from concourse import mybir
from contextlib import ExitStack

F32 = mybir.dt.float32
F32R = mybir.dt.float32r
ALU = mybir.AluOpType
ACT = mybir.ActivationFunctionType

GRAPHS, NODES, DIM = 16, 512, 128
P = 128
TILES = NODES // P
SLOTS = 2
ROUNDS = GRAPHS // SLOTS
HEADS = 8
LAYERS2 = 5
TAPS = 17
PAD = TAPS // 2
EPS = 1e-5
NEG0 = -1000000000.0
NEG1 = -9000000000000000.0

WIDTHS = [("WI2", LAYERS2 * 3 * DIM), ("c2", TAPS * DIM), ("M", HEADS * DIM), ("hh2", 3 * DIM), ("Ww", DIM), ("As", DIM),
          ("c1", DIM), ("msg", DIM), ("ih3c", 3 * DIM), ("ih3n", 3 * DIM), ("hh3", 3 * DIM)]
WCOL = {}
_at = 0
for _name, _width in WIDTHS:
    WCOL[_name] = _at
    _at += _width
WALL = _at
WFIRST = WCOL["M"]

COLS = (["fcb%d" % h for h in range(HEADS)] + ["qw", "kw", "fpb", "Wb", "gateb", "qb", "kb",
        "bih2r", "bih2z", "bih2n", "bhh2r", "bhh2z", "bhh2n", "v1", "v2", "g1", "g2", "b1", "b2", "m1", "m2",
        "bih3r", "bih3z", "bih3n", "bhh3r", "bhh3z", "bhh3n", "gw1", "gw2",
        "se0", "se1", "se2", "se3", "se4", "bse", "e3", "e4", "bmsg"])
CI = {n: i for i, n in enumerate(COLS)}
DCOLS = ["rz2r", "rz2z", "hn2", "rz3r", "rz3z", "hn3", "s1", "s2", "sh1", "sh2", "gb", "bias2", "bias1", "qkw",
         "t1", "t2", "r1", "r2", "tq"]
DI = {n: i for i, n in enumerate(DCOLS)}

PER = {
    "stats": 1, "aggregated": 1, "variance": 1, "rstd": 1, "normed": 1, "h_banked": 1, "h_high": 1, "h_low": 1,
    "h": 1,
    "y_banked": 1, "residual": 1,
    "mask0": 1, "qk_banked": 1, "qk": 1, "g_banked": 8, "g_act": 4, "g_dve": 4,
    "kb_banked": 1, "masked": 4, "relu": 4, "lifted": 4, "kmax_q": 1, "neg_max": 1, "exp_bias": 1, "exped": 4,
    "pt_banked": 4, "pt_dve": 3, "pt_act": 1,
    "rden": 1, "o_banked": 1, "o_added": 1,
    "acc_start": 1, "x_half": 1, "tanh0": 1,
    "mask1": 1, "h1_banked": 1, "h1_high": 1, "h1": 1, "h1_low": 1, "t1_banked": 1, "t1_high": 1, "t1_low": 1, "h1n_banked": 1,
    "s_banked": 4, "s_masked": 4, "s_negmax": 4, "s_exped": 4, "att_pool": 2, "att_dve": 2, "rden1": 1, "h1_scaled": 1, "hp_banked": 1,
    "hp": 1, "gate_banked": 1, "gate": 1, "h_less_hp": 1, "gate_e": 1, "y1": 1,
    "adjacency": 1,
    "hn_rows": 1, "rows_high": 1, "rows_low": 1, "agg_banked": 1, "agg_high": 1, "agg_low": 1,
    "hn_banked": 1, "r_banked": 1, "z_banked": 1, "in_banked": 1, "hn": 1, "r": 1, "z": 1, "cand_a": 1, "cand_b": 1,
    "cand": 1, "z_rest": 1, "z_cand": 1, "h_new": 1, "h_new_high": 1, "h_new_low": 1,
    "c1_banked": 1, "c1_high": 2, "c1_low": 1, "s3_banked": 1, "sq3": 1, "aug_banked": 2, "aug": 2, "msgt_banked": 1, "msgt": 1,
    "msg_banked": 1, "msg": 1, "dist_banked": 4, "dist_exped": 4, "weights3": 4, "c2_banked": 1, "c2_scaled": 1, "xc_high": 2,
    "xc_low": 1, "nmp_banked": 1, "nmp_high": 1, "nmp_low": 1,
}


def build(nc, x, adj, adjt, nmask, c2w, wraw, prew, fcw, fpw, cols_d, out):
    with ExitStack() as ctx:
        def sb(name, shape, dt=F32):
            return ctx.enter_context(nc.sbuf_tensor(name, shape, dt))

        def sem(name):
            return ctx.enter_context(nc.semaphore(name))

        SL = range(SLOTS)
        WH = sb("WH", [P, WALL], F32R)
        WLO = sb("WLO", [P, WALL], F32R)
        VQH = sb("VQH", [P, 2 * HEADS], F32R)
        VQL = sb("VQL", [P, 2 * HEADS], F32R)
        VQ = sb("VQ", [P, 2 * HEADS])
        CQ = sb("CQ", [P, 2 * HEADS])
        ident = sb("ident", [P, P])
        cols = sb("cols", [P, len(COLS)])
        dcols = sb("dcols", [P, len(DCOLS)])
        se2 = sb("se2", [P, 5])
        neg5 = sb("neg5", [5, 2, 5])
        ob = sb("ob", [P, DIM])
        mhalf = sb("mhalf", [P, TILES])
        adjN = [sb(f"adjN{s}", [P, TILES, NODES]) for s in SL]
        adjT = [sb(f"adjT{s}", [P, TILES, NODES]) for s in SL]
        U = [sb(f"U{s}", [P, TILES, NODES]) for s in SL]
        AN = []
        PT = []
        for s in SL:
            with nc.sbuf_tensor(f"PT{s}", [P, TILES, NODES], F32) as pt:
                PT.append(pt)
            AN.append(sb(f"AN{s}", [P, TILES, NODES], F32R))
        F = [sb(f"F{s}", [P, 8, NODES]) for s in SL]
        G = [F[s][:, :, :].rearrange("p (t a) n -> p t (a n)", a=2) for s in SL]
        HS = [sb(f"HS{s}", [P, 2, NODES], F32R) for s in SL]
        R, tiles = [], []
        for s in SL:
            with nc.sbuf_tensor(f"tiles{s}", [P, TILES, NODES], F32) as t:
                tiles.append(t)
            R.append(sb(f"R{s}", [P, TILES, NODES], F32R))
        RELU = tiles[0]
        SC = [U[0], U[1], tiles[1]]
        C1, acc, Y = [], [], []
        for s in SL:
            with nc.sbuf_tensor(f"accY{s}", [P, 2, NODES], F32) as t:
                acc.append(t[:, 0, :])
                Y.append(t[:, 1, :])
            C1.append(sb(f"C1{s}", [P, 2, NODES + 2 * PAD], F32R))
        HT = [sb(f"HT{s}", [P, NODES]) for s in SL]
        hN = [sb(f"hN{s}", [P, NODES]) for s in SL]
        X = [sb(f"X{s}", [P, TILES, DIM]) for s in SL]
        xin = [sb(f"xin{s}", [P, TILES, DIM]) for s in SL]
        nm = [sb(f"nm{s}", [P, TILES]) for s in SL]
        QK = [sb(f"QK{s}", [P, TILES, 2 * HEADS]) for s in SL]
        Q99 = [sb(f"Q99{s}", [P, TILES, HEADS]) for s in SL]
        bst = [sb(f"bst{s}", [P, TILES, 6]) for s in SL]
        mv = [sb(f"mv{s}", [P, TILES, 2]) for s in SL]
        var = [sb(f"var{s}", [P, TILES]) for s in SL]
        rstd = [sb(f"rstd{s}", [P, TILES]) for s in SL]
        kmax = [sb(f"kmax{s}", [P, TILES]) for s in SL]
        kq = [sb(f"kq{s}", [P, TILES]) for s in SL]
        nmx = [sb(f"nmx{s}", [P, TILES]) for s in SL]
        den = [sb(f"den{s}", [P, TILES]) for s in SL]
        rden = [sb(f"rden{s}", [P, TILES]) for s in SL]
        B = [ctx.enter_context(nc.psum_tensor(f"banks{s}", [P, 4, 512], F32)) for s in SL]

        S = {name: sem(name) for name in PER}
        loaded = {n: [sem(f"{n}_loaded{s}") for s in SL] for n in ("xin", "adjN", "adjT", "nmask")}
        x_free = [sem(f"x_free{s}") for s in SL]
        w_loaded = sem("w_loaded")
        ident_ready = sem("ident_ready")
        setup_dve = sem("setup_dve")
        setup_pool = sem("setup_pool")
        setup_pe = sem("setup_pe")
        setup_act = sem("setup_act")
        w_split = sem("w_split")

        def after(name, turn, s, k=None):
            n = PER[name]
            k = n if k is None else k
            return S[name], turn * (SLOTS * n) + s * n + k

        def tile_out(turn, s, j):
            return after("pt_act", turn, s) if j == TILES - 1 else after("pt_dve", turn, s, j + 1)

        def attended(it, s, t):
            return after("att_dve" if t % 2 else "att_pool", it, s, t // 2 + 1)

        def col(name):
            return cols[:, CI[name]:CI[name] + 1]

        def dcol(name):
            return dcols[:, DI[name]:DI[name] + 1]

        def part(t):
            return slice(t * P, (t + 1) * P)

        stage = [F[s][:, :, :].rearrange("p t n -> p (t n)") for s in SL]
        HH = [HS[s][:, 0, :] for s in SL]
        HL = [HS[s][:, 1, :] for s in SL]

        tick_dve = sb("tick_dve", [P, 2 + TILES, SLOTS])
        tick_pool = sb("tick_pool", [P, 2 * SLOTS])

        WI2_BANKS = [(1, 1), (1, 2), (1, 3), (1, 0), (0, 3)]

        block = ctx.enter_context(nc.Block())

        @block.sync
        def _(sp):
            def load(dst, src, signal):
                sp.dma_start(dst, src).then_inc(signal, 16)

            def nodes(t, g):
                return t[bass.ds(g, 1), :, :].rearrange("g (t p) n -> p (g t) n", p=P)

            load(cols[:, :], cols_d, w_loaded)
            load(U[0][:, 0:2, :].rearrange("p t n -> p (t n)"), fcw, w_loaded)
            load(U[1][:, 0:2, :].rearrange("p t n -> p (t n)"), fpw, w_loaded)
            load(U[0][:, 2:4, :].rearrange("p t n -> p (t n)"), prew, w_loaded)
            load(stage[0][:, WCOL["c2"]:WFIRST], c2w, w_loaded)
            load(stage[1][:, HEADS * DIM:WALL - WFIRST], wraw[:, 0:WALL - WFIRST - HEADS * DIM], w_loaded)
            load(xin[1][:, 0, :], wraw[:, WALL - WFIRST - HEADS * DIM:WALL - WFIRST - HEADS * DIM + DIM], w_loaded)
            sp.wait_ge(setup_dve, 2)
            for s in SL:
                load(xin[s][:, :, :], nodes(x, s), loaded["xin"][s])
                load(adjN[s][:, :, :], nodes(adj, s), loaded["adjN"][s])
                load(adjT[s][:, :, :], nodes(adjt, s), loaded["adjT"][s])
                load(nm[s][:, :], nmask[s, :, :], loaded["nmask"][s])

            def round_of(it, more):
                for s in SL:
                    sp.wait_ge(*after("masked", it * HEADS + HEADS - 1, s))
                    load(adjN[s][:, :, :], nodes(adj, it * SLOTS + s), loaded["adjN"][s])
                for s in SL:
                    sp.wait_ge(*after("x_half", it, s))
                    load(xin[s][:, :, :], nodes(x, it * SLOTS + ((SLOTS if more else 0) + s)), loaded["xin"][s])
                if more:
                    for s in SL:
                        sp.wait_ge(*after("adjacency", it, s))
                        load(adjN[s][:, :, :], nodes(adj, it * SLOTS + (SLOTS + s)), loaded["adjN"][s])
                    for s in SL:
                        sp.wait_ge(*after("residual", it * 4 + 2, s))
                        load(nm[s][:, :], nmask[bass.ds(it * SLOTS + (SLOTS + s), 1), :, :].rearrange("g p t -> p (g t)"),
                             loaded["nmask"][s])
                    for s in SL:
                        sp.wait_ge(*after("weights3", it, s))
                        load(adjT[s][:, :, :], nodes(adjt, it * SLOTS + (SLOTS + s)), loaded["adjT"][s])
                for s in SL:
                    sp.wait_ge(*after("residual", it * 4 + 3, s))
                    sp.dma_start(nodes(out, it * SLOTS + s), X[s][:, :, :]).then_inc(x_free[s], 16)

            with sp.Fori(0, ROUNDS - 1) as it:
                round_of(it, True)
            round_of(ROUNDS - 1, False)
            for s in SL:
                sp.wait_ge(x_free[s], 16 * (ROUNDS + 1))

        @block.gpsimd
        def _(pool):
            pool.memset(ident[:, :], 0.0).then_inc(ident_ready, 1)
            pool.memset(mhalf[:, :], -0.5)
            pool.memset(neg5[:, :, :], 0.0).then_inc(setup_pool, 1)
            pool.wait_ge(ident_ready, 1)
            pool.affine_select(out=ident[:, :], in_=ident[:, :], compare_op=ALU.not_equal, fill=1.0, base=0,
                               pattern=[[-1, P]], channel_multiplier=1).then_inc(ident_ready, 1)
            pool.wait_ge(setup_pool, 1)
            pool.memset(neg5[:, 0, 3:4], -1.0)
            pool.memset(neg5[:, 1, 4:5], -1.0).then_inc(setup_pool, 1)
            pool.wait_ge(setup_dve, 1)
            pool.tensor_tensor(dcols[:, DI["r1"]:DI["r1"] + 2], dcols[:, DI["t1"]:DI["t1"] + 2], mhalf[:, 0:2],
                               ALU.pow).then_inc(setup_pool, 1)

            UNITS = HEADS * SLOTS

            def rstd_of(s, turn):
                pool.wait_ge(*after("variance", turn, s))
                pool.tensor_tensor(rstd[s][:, :], var[s][:, :], mhalf[:, :], ALU.pow).then_inc(S["rstd"], 1)

            for s in SL:
                rstd_of(s, 0)
            with pool.Fori(0, ROUNDS) as it:
                for s in SL:
                    pool.wait_ge(loaded["adjN"][s], it * 32 + 16)
                    pool.tensor_tensor(tick_pool[:, s:s + 1], mhalf[:, 0:1], mhalf[:, 0:1], ALU.add)
                    pool.tensor_scalar(adjN[s][:, :, :], adjN[s][:, :, :], -1.0, -NEG0, ALU.add, ALU.mult)\
                        .then_inc(S["mask0"], 1)

                def whole(s, turn):
                    pool.wait_ge(*after("h_low", it * 4 + turn + 1, s))
                    pool.tensor_tensor(HT[s][:, :], HH[s].bitcast(F32), HL[s].bitcast(F32), ALU.add).then_inc(S["h"], 1)

                def lift(u, t):
                    turn = it * HEADS + u // SLOTS
                    pool.wait_ge(*after("relu", turn, u % SLOTS, t + 1))
                    pool.tensor_tensor(SC[u % 3][:, t, :], SC[u % 3][:, t, :], RELU[:, t, :], ALU.add)\
                        .then_inc(S["lifted"], 1)

                for u in range(UNITS):
                    for t in range(TILES):
                        lift(u, t)
                    if 4 <= u < 4 + SLOTS:
                        s = u - 4
                        pool.wait_ge(x_free[s], it * 16 + 16)
                        pool.tensor_tensor(tick_pool[:, SLOTS + s:SLOTS + s + 1], mhalf[:, 0:1], mhalf[:, 0:1], ALU.add)
                        pool.tensor_scalar(X[s][:, :, :], xin[s][:, :, :], 1.0, 0.5, ALU.mult, ALU.add)\
                            .then_inc(S["x_half"], 1)
                for s in SL:
                    rstd_of(s, it * 4 + 1)
                for s in SL:
                    whole(s, 0)
                for s in SL:
                    pool.wait_ge(*after("h1_low", it, s))
                    pool.tensor_tensor(F[s][:, 0, :], R[s][:, 0, :].bitcast(F32), R[s][:, 1, :].bitcast(F32), ALU.add)\
                        .then_inc(S["h1"], 1)
                for s in SL:
                    for t in range(0, TILES, 2):
                        pool.wait_ge(*after("s_exped", it, s, t + 1))
                        pool.tensor_tensor(PT[s][:, t, :], U[s][:, t, :], adjT[s][:, t, :], ALU.mult)\
                            .then_inc(S["att_pool"], 1)
                for s in SL:
                    rstd_of(s, it * 4 + 2)
                for layer in range(LAYERS2 - 1):
                    for s in SL:
                        pool.wait_ge(*after("h_new_high", it * (LAYERS2 - 1) + layer, s))
                        pool.tensor_tensor(HL[s], HT[s][:, :], HH[s].bitcast(F32), ALU.subtract)\
                            .then_inc(S["h_new_low"], 1)
                for s in SL:
                    rstd_of(s, it * 4 + 3)
                    whole(s, 2)
                for s in SL:
                    for t in range(TILES):
                        pool.wait_ge(*after("dist_exped", it, s, t + 1))
                        pool.tensor_tensor(PT[s][:, t, :], U[s][:, t, :], adjT[s][:, t, :], ALU.mult)\
                            .then_inc(S["weights3"], 1)
                    if s == 0:
                        for b in SL:
                            rstd_of(b, it * 4 + 4)

        @block.tensor
        def _(pe):
            def mm3(dst, w, xs, start=True, stop=True):
                pe.matmul(dst, w[0], xs[0], start=start, stop=False)
                pe.matmul(dst, w[0], xs[1], start=False, stop=False)
                return pe.matmul(dst, w[1], xs[0], start=False, stop=stop)

            def W(name, j=0, n=DIM):
                a = WCOL[name] + j * DIM
                return WH[:, a:a + n], WLO[:, a:a + n]

            pe.wait_ge(w_loaded, 7 * 16)
            fcT = U[0][:, 0:2, :].rearrange("p t n -> p (t n)")
            fp = U[1][:, 0:2, :].rearrange("p t n -> p (t n)")
            for h in range(HEADS):
                pe.matmul(B[0][:, h // 4, (h % 4) * DIM:(h % 4 + 1) * DIM], fcT[:, part(h)], fp[:, part(h)])
            for h in range(HEADS):
                pe.matmul(B[0][:, 2, 2 * h:2 * h + 2], fcT[:, part(h)], cols[:, CI["qw"]:CI["qw"] + 2])
            pe.wait_ge(setup_dve, 2)
            pe.matmul(B[0][:, 3, 0:HEADS], dcol("qkw").broadcast_to([P, P]), cols[:, 0:HEADS])
            for h in range(HEADS):
                pe.matmul(B[1][:, 0, 0:DIM], cols[:, h:h + 1].broadcast_to([P, P]), fp[:, part(h)], start=(h == 0), stop=False)
            pe.wait_ge(ident_ready, 2)
            pe.matmul(B[1][:, 0, 0:DIM], col("fpb").broadcast_to([P, P]), ident[:, :], start=False, stop=True)
            pre = U[0][:, 2:4, :].rearrange("p t n -> p (t n)")
            for layer, (b, bank) in enumerate(WI2_BANKS):
                last = pe.matmul(B[b][:, bank, P:4 * P], pre[:, part(layer)], pre[:, LAYERS2 * DIM:(LAYERS2 + 3) * DIM])
            last.then_inc(setup_pe, 1)
            pe.wait_ge(w_split, 4)

            def transpose_in(s, turn):
                pe.wait_ge(*after("normed", turn, s))
                for t in range(TILES):
                    last = pe.transpose(B[s][:, 0, part(t)], hN[s][:, part(t)], ident[:, :])
                last.then_inc(S["h_banked"], 1)

            def query_keys(s, turn):
                pe.wait_ge(*after("h_low", turn * 4, s))
                for t in range(TILES):
                    last = mm3(B[s][:, 1, 16 * t:16 * t + 16], (HH[s][:, part(t)], HL[s][:, part(t)]),
                               (VQH[:, :], VQL[:, :]))
                last.then_inc(S["qk_banked"], 1)

            def values(s, t, turn):
                for half in range(2):
                    signal = "g_dve" if half else "g_act"
                    if t >= 2:
                        pe.wait_ge(*after(signal, turn, s, t - 1))
                    elif s == 1:
                        pe.wait_ge(*after(signal, turn, 0, t + 3))
                    mm3(B[t % 2][:, 2 + half, :], (HH[s][:, part(t)], HL[s][:, part(t)]),
                        W("M", 4 * half, 4 * DIM)).then_inc(S["g_banked"], 1)

            for s in SL:
                transpose_in(s, 0)
            query_keys(0, 0)
            values(0, 0, 0)
            with pe.Fori(0, ROUNDS) as it:
                def transpose_out(s, layer, y):
                    for t in range(TILES):
                        last = pe.transpose(B[s][:, 1, part(t)], y[:, part(t)], ident[:, :])
                    last.then_inc(S["y_banked"], 1)

                def rows_of(s, bank, column):
                    for t in range(TILES):
                        last = pe.transpose(B[s][:, bank, part(t)], column(t).broadcast_to([P, P]), ident[:, :])
                    return last

                def key_rows(u):
                    h, s = u // SLOTS, u % SLOTS
                    if h == 0:
                        pe.wait_ge(*after("qk", it, s))
                    else:
                        pe.wait_ge(*after("masked", it * HEADS + h - 1, s))
                    rows_of(s, 0, lambda t: QK[s][:, t, HEADS + h:HEADS + h + 1]).then_inc(S["kb_banked"], 1)

                UNITS = HEADS * SLOTS
                key_rows(0)
                values(0, 1, it)
                query_keys(1, it)
                for t in range(2, TILES):
                    values(0, t, it)
                key_rows(1)
                for t in range(TILES):
                    values(1, t, it)
                for u in range(UNITS + 1):
                    if u == 0:
                        key_rows(2)
                    for j in range(TILES):
                        if j == TILES - 1 and u + 3 < UNITS:
                            key_rows(u + 3)
                        if u < UNITS:
                            h, s = u // SLOTS, u % SLOTS
                            turn = it * HEADS + h
                            if j == 0:
                                pe.wait_ge(*after("exped", turn, s))
                            if j >= 2:
                                pe.wait_ge(*tile_out(turn, s, j - 2))
                            elif u >= 1:
                                pe.wait_ge(*tile_out(it * HEADS + (u - 1) // SLOTS, (u - 1) % SLOTS, j + 2))
                            for t in range(TILES):
                                last = pe.transpose(B[j % 2][:, 1, part(t)], SC[u % 3][:, t, part(j)], ident[:, :])
                            last.then_inc(S["pt_banked"], 1)
                        if 1 <= u <= UNITS:
                            h, s = (u - 1) // SLOTS, (u - 1) % SLOTS
                            turn = it * HEADS + h
                            if j == 0:
                                if h < 2:
                                    pe.wait_ge(*after("g_act", it, 1))
                                    pe.wait_ge(*after("g_dve", it, 1))
                                else:
                                    pe.wait_ge(*after("o_added", turn - 2, s))
                                pe.wait_ge(*tile_out(turn, s, TILES - 2))
                                pe.wait_ge(*tile_out(turn, s, TILES - 1))
                            for k in range(TILES):
                                last = pe.matmul(B[s][:, 2 + h % 2, part(j)], PT[s][:, k, part(j)],
                                                 G[s][:, k, h * DIM:(h + 1) * DIM], start=(k == 0), stop=(k == TILES - 1))
                            if j == TILES - 1:
                                last.then_inc(S["o_banked"], 1)

                def h1(s):
                    pe.wait_ge(*after("h_low", it * 4 + 1, s))
                    mm3(B[s][:, 1, :], W("Ww"), (HH[s], HL[s])).then_inc(S["h1_banked"], 1)

                def t1(s):
                    pe.wait_ge(*after("h1_low", it, s))
                    mm3(B[s][:, 2, :], W("As"), (R[s][:, 0, :], R[s][:, 1, :])).then_inc(S["t1_banked"], 1)

                def h1_rows(s):
                    pe.wait_ge(*after("h1", it, s))
                    for t in range(TILES):
                        last = pe.transpose(B[s][:, 3, part(t)], F[s][:, 0, part(t)], ident[:, :])
                    last.then_inc(S["h1n_banked"], 1)

                def scores(s, t):
                    if t == 0:
                        pe.wait_ge(*after("t1_low", it, s))
                    if t >= 2:
                        pe.wait_ge(*after("s_masked", it, s, t - 1))
                    mm3(B[s][:, t % 2, :], (R[s][:, 2, part(t)], R[s][:, 3, part(t)]),
                        (R[s][:, 0, :], R[s][:, 1, :])).then_inc(S["s_banked"], 1)

                transpose_in(0, it * 4 + 1)
                h1(0)
                transpose_in(1, it * 4 + 1)
                t1(0)
                h1(1)
                scores(0, 0)
                t1(1)
                scores(0, 1)
                h1_rows(0)
                scores(0, 2)
                scores(0, 3)
                scores(1, 0)
                h1_rows(1)
                for t in range(1, TILES):
                    scores(1, t)

                def attend(s):
                    pe.wait_ge(*after("h1_scaled", it, s))
                    for t in range(TILES):
                        pe.wait_ge(*attended(it, s, t))
                        last = pe.matmul(B[s][:, 2, :], F[s][:, 1, part(t)], PT[s][:, t, :], start=(t == 0),
                                         stop=(t == TILES - 1))
                    last.then_inc(S["hp_banked"], 1)

                def gate(s):
                    pe.wait_ge(*after("h", it * 3, s))
                    pe.matmul(B[s][:, 3, :], col("gw1").broadcast_to([P, P]), HT[s][:, :], start=True, stop=False)
                    pe.wait_ge(*after("hp", it, s))
                    pe.matmul(B[s][:, 3, :], col("gw2").broadcast_to([P, P]), F[s][:, 2, :], start=False, stop=True)\
                        .then_inc(S["gate_banked"], 1)

                attend(0)
                gate(0)
                attend(1)
                pe.wait_ge(*after("y1", it, 0))
                transpose_out(0, 1, Y[0])
                gate(1)
                transpose_in(0, it * 4 + 2)
                pe.wait_ge(*after("y1", it, 1))
                transpose_out(1, 1, Y[1])

                def hidden_rows(s):
                    for t in range(TILES):
                        last = pe.transpose(B[s][:, 0, part(t)], HT[s][:, part(t)], ident[:, :])
                    last.then_inc(S["hn_rows"], 1)

                for n in range(LAYERS2 * SLOTS + 1):
                    s, layer = n % SLOTS, n // SLOTS
                    o, before = (n - 1) % SLOTS, (n - 1) // SLOTS
                    turn = it * LAYERS2 + layer
                    h, agg, agg_o = (HH[s], HL[s]), (R[s][:, 2, :], R[s][:, 3, :]), (R[o][:, 2, :], R[o][:, 3, :])
                    if n < SLOTS:
                        pe.wait_ge(*after("h", it * 3 + 1, s))
                        hidden_rows(s)
                    if n >= 1:
                        mm3(B[o][:, 0, :], W("WI2", 3 * before + 1), agg_o, start=False).then_inc(S["z_banked"], 1)
                    if n < LAYERS2 * SLOTS:
                        if layer == 0:
                            pe.wait_ge(*after("h_low", it * 4 + 2, s))
                        else:
                            pe.wait_ge(*after("h_new_low", it * (LAYERS2 - 1) + layer - 1, s))
                        mm3(B[s][:, 2, :], W("hh2", 0), h, stop=False)
                        pe.wait_ge(*after("rows_low", turn, s))
                        pe.wait_ge(*after("adjacency", it, s))
                        for t in range(TILES):
                            for k in range(2):
                                last = pe.matmul(B[s][:, 1, :], R[s][:, k, part(t)], AN[s][:, t, :],
                                                 start=(t == 0 and k == 0), stop=(t == TILES - 1 and k == 1))
                        last.then_inc(S["agg_banked"], 1)
                        mm3(B[s][:, 3, :], W("hh2", 2), h).then_inc(S["hn_banked"], 1)
                        mm3(B[s][:, 0, :], W("hh2", 1), h, stop=False)
                        if n == LAYERS2 * SLOTS - 1:
                            pe.wait_ge(*after("h_new", it * (LAYERS2 + 1) + LAYERS2 - 1, 0))
                            transpose_out(0, 2, HT[0])
                        elif n == 0:
                            transpose_in(1, it * 4 + 2)
                        else:
                            pe.wait_ge(*after("h_new", it * (LAYERS2 + 1) + before, o))
                            hidden_rows(o)
                        pe.wait_ge(*after("agg_low", turn, s))
                        mm3(B[s][:, 2, :], W("WI2", 3 * layer), agg, start=False).then_inc(S["r_banked"], 1)
                        mm3(B[s][:, 1, :], W("WI2", 3 * layer + 2), agg).then_inc(S["in_banked"], 1)
                cell = it * (LAYERS2 + 1) + LAYERS2

                def c1_and_message(s):
                    pe.wait_ge(*after("h_low", it * 4 + 3, s))
                    pe.wait_ge(*after("residual", it * 4 + 2, s))
                    mm3(B[s][:, 1, :], W("c1"), (HH[s], HL[s])).then_inc(S["c1_banked"], 1)
                    mm3(B[s][:, 3, :], W("msg"), (HH[s], HL[s])).then_inc(S["msgt_banked"], 1)

                def coordinates(s):
                    pe.wait_ge(*after("h", it * 3 + 2, s))
                    pe.matmul(B[s][0:5, 2, :], cols[:, CI["se0"]:CI["se0"] + 5], HT[s][:, :])\
                        .then_inc(S["s3_banked"], 1)

                def message_rows(s):
                    pe.wait_ge(*after("msgt", it, s))
                    for t in range(TILES):
                        last = pe.transpose(B[s][:, 1, part(t)], F[s][:, 5, part(t)], ident[:, :])
                    last.then_inc(S["msg_banked"], 1)

                def augment(s):
                    pe.wait_ge(*after("sq3", it, s))
                    pe.matmul(B[s][0:5, 0, :], se2[:, :], HT[s][:, :], start=True, stop=False)
                    pe.matmul(B[s][0:5, 2, :], neg5[:, 1, :], F[s][0:5, 2, :], start=False, stop=True,
                              skip_group_check=True).then_inc(S["aug_banked"], 1)
                    pe.matmul(B[s][0:5, 0, :], neg5[:, 0, :], F[s][0:5, 2, :], start=False, stop=True)\
                        .then_inc(S["aug_banked"], 1)

                def distances(s, t):
                    if t == 0:
                        pe.wait_ge(*after("aug", it, s))
                    elif t == 1:
                        pe.wait_ge(*after("msg", it, s))
                    else:
                        pe.wait_ge(*after("dist_exped", it, s, t - 1))
                    pe.matmul(B[s][:, t % 2, :], F[s][0:5, 1, part(t)], F[s][0:5, 0, :])\
                        .then_inc(S["dist_banked"], 1)

                def taps(s, first, end):
                    if first == 0:
                        pe.wait_ge(*after("msgt", it, s))
                        pe.wait_ge(*after("c1_low", it, s))
                    for k in range(first, end):
                        last = mm3(B[s][:, 3, :], W("c2", k), (C1[s][:, 0, k:k + NODES], C1[s][:, 1, k:k + NODES]),
                                   start=(k == 0), stop=(k == TAPS - 1))
                    if end == TAPS:
                        last.then_inc(S["c2_banked"], 1)

                def gather(s):
                    pe.wait_ge(*after("msg", it, s))
                    pe.wait_ge(*after("aug", it, s))
                    for t in range(TILES):
                        pe.wait_ge(*after("weights3", it, s, t + 1))
                        last = pe.matmul(B[s][:, 2, :], F[s][:, 7, part(t)], PT[s][:, t, :], start=(t == 0),
                                         stop=(t == TILES - 1))
                    last.then_inc(S["nmp_banked"], 1)

                def cell_start(s):
                    h, c = (HH[s], HL[s]), (R[s][:, 0, :], R[s][:, 1, :])
                    pe.wait_ge(*after("dist_exped", it, s))
                    mm3(B[s][:, 0, :], W("hh3", 0), h, stop=False)
                    mm3(B[s][:, 1, :], W("hh3", 1), h, stop=False)
                    pe.wait_ge(*after("xc_low", it, s))
                    mm3(B[s][:, 3, :], W("hh3", 2), h).then_inc(S["hn_banked"], 1)
                    mm3(B[s][:, 0, :], W("ih3c", 0), c, start=False, stop=False)
                    mm3(B[s][:, 1, :], W("ih3c", 1), c, start=False, stop=False)

                def cell_finish(s):
                    c, n = (R[s][:, 0, :], R[s][:, 1, :]), (R[s][:, 2, :], R[s][:, 3, :])
                    pe.wait_ge(*after("nmp_low", it, s))
                    mm3(B[s][:, 0, :], W("ih3n", 0), n, start=False).then_inc(S["r_banked"], 1)
                    mm3(B[s][:, 2, :], W("ih3c", 2), c, stop=False)
                    mm3(B[s][:, 2, :], W("ih3n", 2), n, start=False).then_inc(S["in_banked"], 1)
                    mm3(B[s][:, 1, :], W("ih3n", 1), n, start=False).then_inc(S["z_banked"], 1)

                transpose_in(0, it * 4 + 3)
                c1_and_message(0)
                pe.wait_ge(*after("h_new", it * (LAYERS2 + 1) + LAYERS2 - 1, 1))
                transpose_out(1, 2, HT[1])
                coordinates(0)
                message_rows(0)
                taps(0, 0, 2)
                augment(0)
                taps(0, 2, 5)
                transpose_in(1, it * 4 + 3)
                distances(0, 0)
                taps(0, 5, 6)
                c1_and_message(1)
                distances(0, 1)
                taps(0, 6, 8)
                coordinates(1)
                message_rows(1)
                distances(0, 2)
                taps(0, 8, 10)
                augment(1)
                distances(0, 3)
                taps(0, 10, TAPS)
                taps(1, 0, 3)
                distances(1, 0)
                gather(0)
                distances(1, 1)
                taps(1, 3, 5)
                cell_start(0)
                distances(1, 2)
                cell_finish(0)
                distances(1, 3)
                taps(1, 5, TAPS)
                pe.wait_ge(*after("r", cell, 0))
                transpose_in(0, it * 4 + 4)
                gather(1)
                pe.wait_ge(*after("h_new", cell, 0))
                transpose_out(0, 3, Y[0])
                cell_start(1)
                cell_finish(1)
                pe.wait_ge(*after("r", cell, 1))
                transpose_in(1, it * 4 + 4)
                query_keys(0, it + 1)
                values(0, 0, it + 1)
                pe.wait_ge(*after("h_new", cell, 1))
                transpose_out(1, 3, Y[1])

        @block.scalar
        def _(act):
            act.wait_ge(w_loaded, 7 * 16)
            act.wait_ge(setup_dve, 3)
            act.activation(WH[:, 0:WFIRST], stage[0], ACT.Copy).then_inc(w_split, 1)
            act.activation(WH[:, WFIRST:WALL], stage[1][:, 0:WALL - WFIRST], ACT.Copy).then_inc(w_split, 1)
            act.activation(VQH[:, :], VQ[:, :], ACT.Copy).then_inc(setup_act, 1)
            act.wait_ge(setup_dve, 7)

            def h_high(s, turn):
                act.wait_ge(*after("h_banked", turn, s))
                act.activation(HH[s], B[s][:, 0, :], ACT.Relu).then_inc(S["h_high"], 1)

            for s in SL:
                h_high(s, 0)
            with act.Fori(0, ROUNDS) as it:
                def g_copy(s, t):
                    act.wait_ge(*after("g_banked", it, s, 2 * t + 1))
                    act.activation(G[s][:, t, 0:4 * DIM], B[t % 2][:, 2, :], ACT.Copy).then_inc(S["g_act"], 1)

                def relu(u, t):
                    h, s = u // SLOTS, u % SLOTS
                    act.wait_ge(*after("masked", it * HEADS + h, s, t + 1))
                    if u >= 1:
                        act.wait_ge(*after("lifted", it * HEADS + (u - 1) // SLOTS, (u - 1) % SLOTS, t + 1))
                    act.activation(RELU[:, t, :], SC[u % 3][:, t, :], ACT.Relu, bias=Q99[s][:, t, h:h + 1], scale=99.0)\
                        .then_inc(S["relu"], 1)

                def softmax_exp(u, t):
                    h, s = u // SLOTS, u % SLOTS
                    turn = it * HEADS + h
                    if t == 0:
                        act.wait_ge(*after("exp_bias", turn, s))
                    act.wait_ge(*after("lifted", turn, s, t + 1))
                    act.activation(SC[u % 3][:, t, :], SC[u % 3][:, t, :], ACT.Exp, bias=nmx[s][:, t:t + 1], scale=0.01,
                                   accum_out=den[s][:, t:t + 1]).then_inc(S["exped"], 1)

                def tile_copy(u, j):
                    h, s = u // SLOTS, u % SLOTS
                    turn = it * HEADS + h
                    if h >= 1:
                        act.wait_ge(*after("o_banked", turn - 1, s))
                    act.wait_ge(*after("pt_banked", turn, s, j + 1))
                    act.activation(PT[s][:, j, :], B[j % 2][:, 1, :], ACT.Copy).then_inc(S["pt_act"], 1)

                UNITS = HEADS * SLOTS
                for u in range(-1, UNITS + 1):
                    for t in range(TILES):
                        if u + 1 < UNITS:
                            relu(u + 1, t)
                        if 0 <= u < UNITS:
                            softmax_exp(u, t)
                        if t == TILES - 1 and 0 <= u - 1 < UNITS:
                            tile_copy(u - 1, t)
                        if u + 1 < SLOTS:
                            g_copy(u + 1, t)
                for s in SL:
                    act.wait_ge(*after("o_added", it * HEADS + HEADS - 1, s))
                    act.activation(Y[s], acc[s], ACT.Tanh, scale=0.5).then_inc(S["tanh0"], 1)

                def h1_high(s):
                    act.wait_ge(*after("h1_banked", it, s))
                    act.activation(R[s][:, 0, :], B[s][:, 1, :], ACT.Identity, bias=col("Wb")).then_inc(S["h1_high"], 1)

                def t1_high(s):
                    act.wait_ge(*after("t1_banked", it, s))
                    act.activation(R[s][:, 2, :], B[s][:, 2, :], ACT.Copy).then_inc(S["t1_high"], 1)

                h_high(0, it * 4 + 1)
                h1_high(0)
                h_high(1, it * 4 + 1)
                t1_high(0)
                h1_high(1)
                t1_high(1)
                for s in SL:
                    for t in range(TILES):
                        act.wait_ge(*after("s_negmax", it, s, t + 1))
                        act.activation(U[s][:, t, :], U[s][:, t, :], ACT.Exp, bias=nmx[s][:, t:t + 1],
                                       accum_out=den[s][:, t:t + 1]).then_inc(S["s_exped"], 1)
                for s in SL:
                    act.wait_ge(*after("hp_banked", it, s))
                    act.activation(F[s][:, 2, :], B[s][:, 2, :], ACT.Relu).then_inc(S["hp"], 1)
                    act.wait_ge(*after("gate_banked", it, s))
                    act.activation(F[s][:, 3, :], B[s][:, 3, :], ACT.Tanh, bias=dcol("gb"), scale=0.5)\
                        .then_inc(S["gate"], 1)

                def gate_act(s, cell, signal, bank, tile, bias, func):
                    act.wait_ge(*after(signal + "_banked", cell, s))
                    act.activation(F[s][:, tile, :], B[s][:, bank, :], func, bias=dcol(bias), scale=0.5)\
                        .then_inc(S[signal], 1)

                def cand_act(s, cell, bias):
                    act.wait_ge(*after("cand_b", cell, s))
                    act.activation(F[s][:, 4, :], F[s][:, 3, :], ACT.Tanh, bias=col(bias)).then_inc(S["cand"], 1)

                def h_of(s):
                    act.wait_ge(*after("h_banked", it * 4 + 2, s))
                    act.activation(HT[s][:, :], B[s][:, 0, :], ACT.Relu).then_inc(S["h"], 1)
                    act.wait_ge(*after("h", it * 3 + 1, s))
                    act.activation(HH[s], HT[s][:, :], ACT.Copy).then_inc(S["h_high"], 1)

                def rows_high(s, turn):
                    act.wait_ge(*after("hn_rows", turn, s))
                    act.activation(R[s][:, 0, :], B[s][:, 0, :], ACT.Copy).then_inc(S["rows_high"], 1)

                h_of(0)
                for n in range(LAYERS2 * SLOTS + 1):
                    s, layer = n % SLOTS, n // SLOTS
                    o, before = (n - 1) % SLOTS, (n - 1) // SLOTS
                    turn, cell = it * LAYERS2 + layer, it * (LAYERS2 + 1) + layer
                    cell_o = it * (LAYERS2 + 1) + before
                    start, end = n < LAYERS2 * SLOTS, n >= 1
                    if n < SLOTS:
                        rows_high(s, turn)
                    if end:
                        gate_act(o, cell_o, "z", 0, 1, "rz2z", ACT.Tanh)
                    if n == LAYERS2 * SLOTS:
                        h_high(0, it * 4 + 3)
                    if end:
                        cand_act(o, cell_o, "bih2n")
                    if start:
                        act.wait_ge(*after("agg_banked", turn, s))
                        act.activation(R[s][:, 2, :], B[s][:, 1, :], ACT.Copy).then_inc(S["agg_high"], 1)
                        gate_act(s, cell, "hn", 3, 2, "hn2", ACT.Identity)
                    if n == 0:
                        h_of(1)
                    if end and before < LAYERS2 - 1:
                        act.wait_ge(*after("h_new", cell_o, o))
                        act.activation(HH[o], HT[o][:, :], ACT.Copy).then_inc(S["h_new_high"], 1)
                        rows_high(o, it * LAYERS2 + before + 1)
                    if start:
                        gate_act(s, cell, "r", 2, 0, "rz2r", ACT.Tanh)

                cell = it * (LAYERS2 + 1) + LAYERS2

                def c1_out(s):
                    act.wait_ge(*after("c1_banked", it, s))
                    act.activation(C1[s][:, 0, PAD:PAD + NODES], B[s][:, 1, :], ACT.Relu, bias=dcol("sh1"),
                                   scale=dcol("s1")).then_inc(S["c1_high"], 1)
                    act.activation(F[s][:, 6, :], B[s][:, 1, :], ACT.Relu, bias=dcol("sh1"), scale=dcol("s1"))\
                        .then_inc(S["c1_high"], 1)

                def message(s):
                    act.wait_ge(*after("msgt_banked", it, s))
                    act.activation(F[s][:, 5, :], B[s][:, 3, :], ACT.Relu, bias=col("bmsg")).then_inc(S["msgt"], 1)

                def squares(s):
                    act.wait_ge(*after("s3_banked", it, s))
                    act.activation(F[s][0:5, 2, :], B[s][0:5, 2, :], ACT.Square, bias=cols[0:5, CI["bse"]:CI["bse"] + 1])\
                        .then_inc(S["sq3"], 1)

                def message_rows(s):
                    act.wait_ge(*after("msg_banked", it, s))
                    act.activation(F[s][:, 7, :], B[s][:, 1, :], ACT.Copy).then_inc(S["msg"], 1)

                def augmented(s):
                    act.wait_ge(*after("aug_banked", it, s, 1))
                    act.activation(F[s][0:5, 0, :], B[s][0:5, 2, :], ACT.Identity,
                                   bias=dcols[0:5, DI["bias2"]:DI["bias2"] + 1]).then_inc(S["aug"], 1)
                    act.wait_ge(*after("aug_banked", it, s, 2))
                    act.activation(F[s][0:5, 1, :], B[s][0:5, 0, :], ACT.Identity,
                                   bias=dcols[0:5, DI["bias1"]:DI["bias1"] + 1]).then_inc(S["aug"], 1)

                def weights(s, t):
                    act.wait_ge(*after("dist_banked", it, s, t + 1))
                    act.activation(U[s][:, t, :], B[s][:, t % 2, :], ACT.Exp).then_inc(S["dist_exped"], 1)

                def convolved(s):
                    act.wait_ge(*after("c2_scaled", it, s))
                    act.activation(F[s][:, 4, :], F[s][:, 3, :], ACT.Relu, bias=dcol("sh2")).then_inc(S["xc_high"], 1)
                    act.activation(R[s][:, 0, :], F[s][:, 3, :], ACT.Relu, bias=dcol("sh2")).then_inc(S["xc_high"], 1)

                def gathered(s):
                    act.wait_ge(*after("nmp_banked", it, s))
                    act.activation(R[s][:, 2, :], B[s][:, 2, :], ACT.Copy).then_inc(S["nmp_high"], 1)

                c1_out(0)
                message(0)
                squares(0)
                message_rows(0)
                augmented(0)
                h_high(1, it * 4 + 3)
                weights(0, 0)
                c1_out(1)
                message(1)
                weights(0, 1)
                squares(1)
                message_rows(1)
                weights(0, 2)
                augmented(1)
                weights(0, 3)
                convolved(0)
                weights(1, 0)
                gathered(0)
                weights(1, 1)
                gate_act(0, cell, "hn", 3, 2, "hn3", ACT.Identity)
                weights(1, 2)
                gate_act(0, cell, "r", 0, 0, "rz3r", ACT.Tanh)
                gate_act(0, cell, "z", 1, 1, "rz3z", ACT.Tanh)
                weights(1, 3)
                cand_act(0, cell, "bih3n")
                h_high(0, it * 4 + 4)
                convolved(1)
                gathered(1)
                gate_act(1, cell, "hn", 3, 2, "hn3", ACT.Identity)
                gate_act(1, cell, "r", 0, 0, "rz3r", ACT.Tanh)
                gate_act(1, cell, "z", 1, 1, "rz3z", ACT.Tanh)
                cand_act(1, cell, "bih3n")
                h_high(1, it * 4 + 4)

        @block.vector
        def _(dve):
            for s in SL:
                dve.memset(X[s][:, :, :], 0.0).then_inc(x_free[s], 16)
            dve.wait_ge(w_loaded, 7 * 16)

            def c2(a, n=1):
                return cols[:, CI[a]:CI[a] + n]

            def d2(a, n=1):
                return dcols[:, DI[a]:DI[a] + n]

            dve.tensor_scalar(d2("t1", 2), c2("v1", 2), EPS, None, ALU.add).then_inc(setup_dve, 1)
            dve.tensor_tensor(d2("qkw"), c2("qw"), c2("kw"), ALU.add)
            for l in "23":
                dve.tensor_tensor(d2(f"rz{l}r", 2), c2(f"bih{l}r", 2), c2(f"bhh{l}r", 2), ALU.add)
                dve.tensor_scalar(d2(f"hn{l}"), c2(f"bhh{l}n"), 0.5, None, ALU.mult)
            dve.tensor_scalar(d2("gb"), c2("gateb"), 0.5, None, ALU.mult)
            dve.tensor_tensor(d2("bias2"), c2("bse"), c2("e3"), ALU.add)
            dve.tensor_scalar(se2[:, :], c2("se0", 5), 2.0, None, ALU.mult)
            dve.tensor_tensor(d2("tq"), c2("qb"), c2("kb"), ALU.add)
            asym = stage[1][:, WCOL["As"] - WFIRST:WCOL["As"] - WFIRST + DIM]
            dve.tensor_tensor(asym, asym, xin[1][:, 0, :], ALU.add)
            dve.scalar_tensor_tensor(d2("bias1"), c2("bse"), 2.0, c2("e4"), ALU.mult, ALU.add).then_inc(setup_dve, 1)
            dve.wait_ge(setup_dve, 2)
            for l in "23":
                dve.tensor_scalar(d2(f"rz{l}r", 2), d2(f"rz{l}r", 2), 0.5, None, ALU.mult)
            dve.wait_ge(setup_pe, 1)
            dve.tensor_copy(F[1][:, 0:2, :], B[0][:, 0:2, :])
            for layer, (b, bank) in enumerate(WI2_BANKS):
                dve.tensor_copy(stage[0][:, layer * 3 * DIM:(layer + 1) * 3 * DIM], B[b][:, bank, P:4 * P])
            dve.tensor_copy(VQ[:, :].rearrange("p (a h) -> p a h", a=2),
                            B[0][:, 2, 0:2 * HEADS].rearrange("p (h a) -> p a h", a=2)).then_inc(setup_dve, 1)
            dve.memset(CQ[:, :], 0.0).then_inc(setup_dve, 1)
            dve.wait_ge(setup_dve, 4)
            dve.tensor_scalar(CQ[:, 0:HEADS], B[0][:, 3, 0:HEADS], d2("tq"), None, ALU.add)
            dve.tensor_copy(ob[:, :], B[1][:, 0, 0:DIM])
            dve.wait_ge(setup_pool, 3)
            dve.tensor_tensor(d2("s1", 2), c2("g1", 2), d2("r1", 2), ALU.mult).then_inc(setup_dve, 1)
            dve.wait_ge(setup_dve, 5)
            dve.tensor_tensor(d2("t1", 2), c2("m1", 2), d2("s1", 2), ALU.mult).then_inc(setup_dve, 1)
            dve.wait_ge(w_split, 1)
            dve.tensor_tensor(WLO[:, 0:WFIRST], stage[0], WH[:, 0:WFIRST].bitcast(F32),
                              ALU.subtract).then_inc(w_split, 1)
            dve.wait_ge(setup_dve, 6)
            dve.tensor_tensor(d2("sh1", 2), c2("b1", 2), d2("t1", 2), ALU.subtract)
            dve.wait_ge(setup_act, 1)
            dve.tensor_tensor(VQL[:, :], VQ[:, :], VQH[:, :].bitcast(F32), ALU.subtract).then_inc(setup_dve, 1)
            dve.wait_ge(w_split, 3)
            dve.tensor_tensor(WLO[:, WFIRST:WALL], stage[1][:, 0:WALL - WFIRST],
                              WH[:, WFIRST:WALL].bitcast(F32), ALU.subtract).then_inc(w_split, 1)

            def norm_stats(s, turn, src):
                if src is X:
                    dve.wait_ge(*after("residual", turn - 1, s))
                for t in range(TILES):
                    last = dve.bn_stats(bst[s][:, t, :], src[s][:, t, :])
                last.then_inc(S["stats"], 1)
                dve.wait_ge(*after("stats", turn, s))
                dve.memset(tick_dve[:, 0, s:s + 1], 0.0)
                for t in range(TILES):
                    last = dve.bn_aggr(mv[s][:, t, :], bst[s][:, t, :])
                last.then_inc(S["aggregated"], 1)
                dve.wait_ge(*after("aggregated", turn, s))
                dve.tensor_scalar(var[s][:, :], mv[s][:, :, 1], EPS, None, ALU.add).then_inc(S["variance"], 1)

            def norm_scale(s, turn, src):
                dve.wait_ge(*after("rstd", turn, s))
                for t in range(TILES):
                    last = dve.tensor_scalar(hN[s][:, part(t)], src[s][:, t, :], mv[s][:, t, 0:1], rstd[s][:, t:t + 1],
                                             ALU.subtract, ALU.mult)
                last.then_inc(S["normed"], 1)

            def h_low(s, turn):
                dve.wait_ge(*after("h_high", turn, s))
                dve.scalar_tensor_tensor(HL[s], B[s][:, 0, :], 0.0, HH[s].bitcast(F32), ALU.max, ALU.subtract)\
                    .then_inc(S["h_low"], 1)

            for s in SL:
                dve.wait_ge(loaded["xin"][s], 16)
                norm_stats(s, 0, xin)
            for s in SL:
                norm_scale(s, 0, xin)
            for s in SL:
                h_low(s, 0)
            with dve.Fori(0, ROUNDS) as it:
                def add_residual(s, layer):
                    turn = it * 4 + layer
                    if layer == 0:
                        dve.wait_ge(*after("tanh0", it, s))
                        dve.wait_ge(*after("x_half", it, s))
                        last = dve.scalar_tensor_tensor(X[s][:, :, :], Y[s].rearrange("p (t n) -> p t n", t=TILES), 0.5,
                                                        X[s][:, :, :], ALU.mult, ALU.add)
                    else:
                        dve.wait_ge(*after("y_banked", it * 3 + layer - 1, s))
                    y = B[s][:, 1, :].rearrange("p (t n) -> p t n", t=TILES)
                    if layer == 2:
                        dve.wait_ge(loaded["nmask"][s], it * 16 + 16)
                        for t in range(TILES):
                            last = dve.scalar_tensor_tensor(X[s][:, t, :], y[:, t, :], nm[s][:, t:t + 1], X[s][:, t, :],
                                                            ALU.mult, ALU.add)
                    elif layer > 0:
                        last = dve.tensor_tensor(X[s][:, :, :], y, X[s][:, :, :], ALU.add)
                    last.then_inc(S["residual"], 1)

                def query_keys(s):
                    dve.wait_ge(*after("qk_banked", it, s))
                    dve.tensor_tensor(QK[s][:, :, :], B[s][:, 1, 0:64].rearrange("p (t c) -> p t c", t=TILES),
                                      CQ[:, :].unsqueeze(1).broadcast_to([P, TILES, 2 * HEADS]), ALU.add).then_inc(S["qk"], 1)
                    dve.wait_ge(*after("qk", it, s))
                    dve.tensor_scalar(Q99[s][:, :, :], QK[s][:, :, 0:HEADS], 99.0, None, ALU.mult)

                def g_copy(s, t):
                    dve.wait_ge(*after("g_banked", it, s, 2 * t + 2))
                    dve.tensor_copy(G[s][:, t, 4 * DIM:8 * DIM], B[t % 2][:, 3, :]).then_inc(S["g_dve"], 1)

                def masked_keys(u, t):
                    h, s = u // SLOTS, u % SLOTS
                    turn = it * HEADS + h
                    if t == 0:
                        if h == 0:
                            dve.wait_ge(*after("mask0", it, s))
                        if u >= 3:
                            dve.wait_ge(*after("pt_banked", it * HEADS + (u - 3) // SLOTS, (u - 3) % SLOTS))
                        dve.wait_ge(*after("kb_banked", turn, s))
                        dve.memset(tick_dve[:, 1, s:s + 1], 0.0)
                    dve.tensor_tensor_reduce(out=SC[u % 3][:, t, :], in0=adjN[s][:, t, :], in1=B[s][:, 0, :], scale=1.0,
                                             scalar=-3.0e38, op0=ALU.add, op1=ALU.max,
                                             accum_out=kmax[s][:, t:t + 1]).then_inc(S["masked"], 1)

                def kmax_q(u):
                    h, s = u // SLOTS, u % SLOTS
                    dve.wait_ge(*after("masked", it * HEADS + h, s))
                    dve.scalar_tensor_tensor(kq[s][:, :], kmax[s][:, :], -1.0, QK[s][:, :, h], ALU.mult, ALU.subtract)\
                        .then_inc(S["kmax_q"], 1)

                def neg_max(u):
                    h, s = u // SLOTS, u % SLOTS
                    dve.wait_ge(*after("kmax_q", it * HEADS + h, s))
                    dve.scalar_tensor_tensor(kmax[s][:, :], kq[s][:, :], 0.01, kq[s][:, :], ALU.mult, ALU.min)\
                        .then_inc(S["neg_max"], 1)

                def exp_bias(u):
                    h, s = u // SLOTS, u % SLOTS
                    turn = it * HEADS + h
                    if u >= 2:
                        dve.wait_ge(*after("exped", turn - 1, s))
                    dve.wait_ge(*after("neg_max", turn, s))
                    dve.scalar_tensor_tensor(nmx[s][:, :], QK[s][:, :, h], 0.01, kmax[s][:, :], ALU.mult, ALU.add)\
                        .then_inc(S["exp_bias"], 1)

                def denominators(u):
                    h, s = u // SLOTS, u % SLOTS
                    dve.wait_ge(*after("exped", it * HEADS + h, s))
                    dve.reciprocal(rden[s][:, :], den[s][:, :]).then_inc(S["rden"], 1)

                def tile_copy(u, j):
                    h, s = u // SLOTS, u % SLOTS
                    turn = it * HEADS + h
                    if h >= 1 and j == 0:
                        dve.wait_ge(*after("o_banked", turn - 1, s))
                    dve.wait_ge(*after("pt_banked", turn, s, j + 1))
                    dve.tensor_copy(PT[s][:, j, :], B[j % 2][:, 1, :]).then_inc(S["pt_dve"], 1)

                def add_head(u, first):
                    h, s = u // SLOTS, u % SLOTS
                    turn = it * HEADS + h
                    if first == 0:
                        if h == 0:
                            dve.wait_ge(*after("acc_start", it, s))
                        else:
                            dve.wait_ge(*after("o_added", turn - 1, s))
                        dve.wait_ge(*after("rden", turn, s))
                        dve.wait_ge(*after("o_banked", turn, s))
                    for t in (first, first + 1):
                        last = dve.scalar_tensor_tensor(acc[s][:, part(t)], B[s][:, 2 + h % 2, part(t)], rden[s][:, t:t + 1],
                                                        acc[s][:, part(t)], ALU.mult, ALU.add)
                    if first > 0:
                        last.then_inc(S["o_added"], 1)

                UNITS = HEADS * SLOTS

                def start_output(s):
                    dve.scalar_tensor_tensor(acc[s].rearrange("p (t n) -> p t n", t=TILES),
                                             hN[s][:, :].rearrange("p (t n) -> p t n", t=TILES), 0.0,
                                             ob[:, :].unsqueeze(1).broadcast_to([P, TILES, DIM]), ALU.max, ALU.add)\
                        .then_inc(S["acc_start"], 1)

                query_keys(0)
                masked_keys(0, 0)
                for u in range(-1, UNITS + 2):
                    for t in range(TILES):
                        if u + 1 < UNITS and t > 0:
                            masked_keys(u + 1, t)
                        if u == -1 and t == TILES - 1:
                            query_keys(1)
                        if u == -1 and t >= 2:
                            start_output(t - 2)
                        if u + 1 < SLOTS:
                            g_copy(u + 1, t)
                        if t < TILES - 1 and 0 <= u - 1 < UNITS:
                            tile_copy(u - 1, t)
                    if 0 <= u - 1 < UNITS:
                        denominators(u - 1)
                    if u + 1 < UNITS:
                        kmax_q(u + 1)
                    if u + 2 < UNITS:
                        masked_keys(u + 2, 0)
                    if u + 1 < UNITS:
                        neg_max(u + 1)
                    if 0 <= u - 2 < UNITS:
                        add_head(u - 2, 0)
                    if u + 1 < UNITS:
                        exp_bias(u + 1)
                    if 0 <= u - 2 < UNITS:
                        add_head(u - 2, 2)
                    if u == UNITS:
                        add_residual(0, 0)
                        norm_stats(0, it * 4 + 1, X)
                    if u == UNITS + 1:
                        norm_scale(0, it * 4 + 1, X)
                add_residual(1, 0)

                def mask1(s):
                    dve.wait_ge(loaded["adjT"][s], it * 16 + 16)
                    dve.tensor_scalar(U[s][:, :, :], adjT[s][:, :, :], 0.0, NEG1, ALU.is_le, ALU.mult)\
                        .then_inc(S["mask1"], 1)

                def h1_low(s):
                    dve.wait_ge(*after("h1_high", it, s))
                    dve.scalar_tensor_tensor(R[s][:, 1, :], B[s][:, 1, :], col("Wb"), R[s][:, 0, :].bitcast(F32), ALU.add,
                                             ALU.subtract).then_inc(S["h1_low"], 1)

                def t1_low(s):
                    dve.wait_ge(*after("t1_high", it, s))
                    dve.tensor_tensor(R[s][:, 3, :], B[s][:, 2, :], R[s][:, 2, :].bitcast(F32), ALU.subtract)\
                        .then_inc(S["t1_low"], 1)

                def masked_scores(s, t):
                    if t == 0:
                        dve.wait_ge(*after("mask1", it, s))
                    dve.wait_ge(*after("s_banked", it, s, t + 1))
                    dve.memset(tick_dve[:, 2 + t, s:s + 1], 0.0)
                    dve.tensor_tensor_reduce(out=U[s][:, t, :], in0=U[s][:, t, :], in1=B[s][:, t % 2, :], scale=1.0,
                                             scalar=-3.0e38, op0=ALU.add, op1=ALU.max,
                                             accum_out=kmax[s][:, t:t + 1]).then_inc(S["s_masked"], 1)

                def negative_max(s, t):
                    dve.wait_ge(*after("s_masked", it, s, t + 1))
                    dve.tensor_scalar(nmx[s][:, t:t + 1], kmax[s][:, t:t + 1], -1.0, None, ALU.mult)\
                        .then_inc(S["s_negmax"], 1)

                def attention(s, t):
                    dve.wait_ge(*after("s_exped", it, s, t + 1))
                    dve.tensor_tensor(PT[s][:, t, :], U[s][:, t, :], adjT[s][:, t, :], ALU.mult)\
                        .then_inc(S["att_dve"], 1)

                def scaled_h1(s):
                    dve.wait_ge(*after("s_exped", it, s))
                    dve.reciprocal(rden[s][:, :], den[s][:, :]).then_inc(S["rden1"], 1)
                    dve.wait_ge(*after("rden1", it, s))
                    dve.wait_ge(*after("h1n_banked", it, s))
                    for t in range(TILES):
                        last = dve.tensor_scalar(F[s][:, 1, part(t)], B[s][:, 3, part(t)], rden[s][:, t:t + 1], None, ALU.mult)
                    last.then_inc(S["h1_scaled"], 1)

                norm_stats(1, it * 4 + 1, X)
                h_low(0, it * 4 + 1)
                norm_scale(1, it * 4 + 1, X)
                mask1(0)
                h1_low(0)
                h_low(1, it * 4 + 1)
                mask1(1)
                t1_low(0)
                h1_low(1)
                masked_scores(0, 0)
                t1_low(1)
                for t in range(1, TILES):
                    masked_scores(0, t)
                    negative_max(0, t - 1)
                masked_scores(1, 0)
                negative_max(0, TILES - 1)
                masked_scores(1, 1)
                negative_max(1, 0)
                attention(0, 1)
                masked_scores(1, 2)
                negative_max(1, 1)
                scaled_h1(0)
                masked_scores(1, 3)
                negative_max(1, 2)
                attention(0, 3)
                negative_max(1, 3)
                attention(1, 1)
                scaled_h1(1)
                attention(1, 3)

                def gate_mix(s):
                    dve.wait_ge(*after("gate", it, s))
                    dve.wait_ge(*after("h_less_hp", it, s))
                    dve.scalar_tensor_tensor(F[s][:, 5, :], F[s][:, 3, :], 1.0, F[s][:, 4, :], ALU.add, ALU.mult)\
                        .then_inc(S["gate_e"], 1)
                    dve.wait_ge(*after("gate_e", it, s))
                    dve.scalar_tensor_tensor(Y[s], F[s][:, 5, :], 0.5, F[s][:, 2, :], ALU.mult, ALU.add)\
                        .then_inc(S["y1"], 1)

                def less_hp(s):
                    dve.wait_ge(*after("h", it * 3, s))
                    dve.wait_ge(*after("hp", it, s))
                    dve.tensor_tensor(F[s][:, 4, :], HT[s][:, :], F[s][:, 2, :], ALU.subtract).then_inc(S["h_less_hp"], 1)

                def nonzero(s):
                    dve.wait_ge(loaded["adjN"][s], it * 32 + 32)
                    dve.wait_ge(*after("hp_banked", it, s))
                    dve.tensor_scalar(AN[s][:, :, :], adjN[s][:, :, :], 0.0, None, ALU.not_equal)\
                        .then_inc(S["adjacency"], 1)

                def h_low_of_h(s):
                    dve.wait_ge(*after("h_high", it * 4 + 2, s))
                    dve.tensor_tensor(HL[s], HT[s][:, :], HH[s].bitcast(F32), ALU.subtract).then_inc(S["h_low"], 1)

                def rows_low(s, turn):
                    dve.wait_ge(*after("rows_high", turn, s))
                    dve.tensor_tensor(R[s][:, 1, :], B[s][:, 0, :], R[s][:, 0, :].bitcast(F32), ALU.subtract)\
                        .then_inc(S["rows_low"], 1)

                less_hp(0)
                gate_mix(0)
                add_residual(0, 1)
                norm_stats(0, it * 4 + 2, X)
                less_hp(1)
                norm_scale(0, it * 4 + 2, X)
                gate_mix(1)
                nonzero(0)
                h_low_of_h(0)
                add_residual(1, 1)
                norm_stats(1, it * 4 + 2, X)
                rows_low(0, it * LAYERS2)
                norm_scale(1, it * 4 + 2, X)

                def cand_a(s, cell):
                    dve.wait_ge(*after("hn", cell, s))
                    dve.wait_ge(*after("r", cell, s))
                    dve.scalar_tensor_tensor(F[s][:, 3, :], F[s][:, 0, :], 1.0, F[s][:, 2, :], ALU.add, ALU.mult)\
                        .then_inc(S["cand_a"], 1)

                def cand_b(s, cell, in_bank):
                    dve.wait_ge(*after("cand_a", cell, s))
                    dve.wait_ge(*after("in_banked", cell, s))
                    dve.tensor_tensor(F[s][:, 3, :], B[s][:, in_bank, :], F[s][:, 3, :], ALU.add).then_inc(S["cand_b"], 1)

                def cell_zh(s, cell):
                    dve.wait_ge(*after("z", cell, s))
                    dve.scalar_tensor_tensor(F[s][:, 5, :], F[s][:, 1, :], 1.0, HT[s][:, :], ALU.add, ALU.mult)
                    dve.tensor_scalar(F[s][:, 6, :], F[s][:, 1, :], -0.5, 0.5, ALU.mult, ALU.add).then_inc(S["z_rest"], 1)

                def cell_end(s, cell, dst):
                    dve.wait_ge(*after("cand", cell, s))
                    dve.wait_ge(*after("z_rest", cell, s))
                    dve.tensor_tensor(F[s][:, 4, :], F[s][:, 6, :], F[s][:, 4, :], ALU.mult).then_inc(S["z_cand"], 1)
                    dve.wait_ge(*after("z_cand", cell, s))
                    dve.scalar_tensor_tensor(dst, F[s][:, 5, :], 0.5, F[s][:, 4, :], ALU.mult, ALU.add)\
                        .then_inc(S["h_new"], 1)

                for n in range(LAYERS2 * SLOTS + 1):
                    s, layer = n % SLOTS, n // SLOTS
                    o, before = (n - 1) % SLOTS, (n - 1) // SLOTS
                    turn, cell = it * LAYERS2 + layer, it * (LAYERS2 + 1) + layer
                    cell_o = it * (LAYERS2 + 1) + before
                    start, end = n < LAYERS2 * SLOTS, n >= 1
                    if end:
                        cand_a(o, cell_o)
                    if n == 1:
                        rows_low(1, turn)
                    if n == LAYERS2 * SLOTS:
                        norm_scale(0, it * 4 + 3, X)
                    if end:
                        cand_b(o, cell_o, 1)
                        cell_zh(o, cell_o)
                    if n == LAYERS2 * SLOTS:
                        h_low(0, it * 4 + 3)
                    if end:
                        cell_end(o, cell_o, HT[o][:, :])
                    if start:
                        dve.wait_ge(*after("agg_high", turn, s))
                        dve.tensor_tensor(R[s][:, 3, :], B[s][:, 1, :], R[s][:, 2, :].bitcast(F32), ALU.subtract)\
                            .then_inc(S["agg_low"], 1)
                    if end and before < LAYERS2 - 1:
                        rows_low(o, it * LAYERS2 + before + 1)
                    if n == 0:
                        nonzero(1)
                        h_low_of_h(1)
                    if n == LAYERS2 * SLOTS - 1:
                        add_residual(0, 2)
                        norm_stats(0, it * 4 + 3, X)

                cell = it * (LAYERS2 + 1) + LAYERS2

                def c1_low(s):
                    dve.wait_ge(*after("c1_high", it, s))
                    dve.tensor_tensor(C1[s][:, 1, PAD:PAD + NODES], F[s][:, 6, :],
                                      C1[s][:, 0, PAD:PAD + NODES].bitcast(F32), ALU.subtract).then_inc(S["c1_low"], 1)

                def convolved(s):
                    dve.wait_ge(*after("c2_banked", it, s))
                    dve.wait_ge(*after("h", it * 3 + 2, s))
                    dve.scalar_tensor_tensor(F[s][:, 3, :], B[s][:, 3, :], dcol("s2"), HT[s][:, :], ALU.mult, ALU.add)\
                        .then_inc(S["c2_scaled"], 1)
                    dve.wait_ge(*after("xc_high", it, s))
                    dve.tensor_tensor(R[s][:, 1, :], F[s][:, 4, :], R[s][:, 0, :].bitcast(F32), ALU.subtract)\
                        .then_inc(S["xc_low"], 1)

                def gathered(s):
                    dve.wait_ge(*after("nmp_high", it, s))
                    dve.tensor_tensor(R[s][:, 3, :], B[s][:, 2, :], R[s][:, 2, :].bitcast(F32), ALU.subtract)\
                        .then_inc(S["nmp_low"], 1)

                def cell3(s):
                    cand_a(s, cell)
                    cell_zh(s, cell)
                    cand_b(s, cell, 2)
                    cell_end(s, cell, Y[s])

                for s in SL:
                    for edge in (0, PAD + NODES):
                        dve.memset(C1[s][:, :, edge:edge + PAD].bitcast(F32), 0.0)
                add_residual(1, 2)
                c1_low(0)
                norm_stats(1, it * 4 + 3, X)
                norm_scale(1, it * 4 + 3, X)
                h_low(1, it * 4 + 3)
                c1_low(1)
                for s in SL:
                    dve.wait_ge(loaded["xin"][s], it * 16 + 32)
                    norm_stats(s, it * 4 + 4, xin)
                for s in SL:
                    norm_scale(s, it * 4 + 4, xin)
                convolved(0)
                gathered(0)
                cell3(0)
                convolved(1)
                add_residual(0, 3)
                h_low(0, it * 4 + 4)
                gathered(1)
                cell3(1)
                add_residual(1, 3)
                h_low(1, it * 4 + 4)


def kernel(**inputs):
    import numpy as _np
    import concourse.bacc as _bacc
    from concourse import mybir as _mybir
    from concourse.bass_utils import run_bass_kernel_spmd as _run

    v = {k: _np.asarray(a) for k, a in inputs.items()}

    def wide(a):
        return _np.ascontiguousarray(a).reshape(P, -1)

    fcw = wide(v["L0_gnn_fc_w"].reshape(DIM, HEADS, DIM).transpose(2, 1, 0))
    fpw = wide(v["L0_gnn_fp_w"].reshape(HEADS, DIM, DIM).transpose(1, 0, 2))
    wraw = _np.concatenate([
        wide(v["L2_gnn_w_hh"].T), wide(v["L1_gnn_W_w"].T), wide(v["L1_gnn_A"]), wide(v["L3_gnn_conv1_w"][:, :, 0].T),
        wide(v["L3_gnn_w_msg"].T), wide(v["L3_gnn_w_ih"][:, :DIM].T), wide(v["L3_gnn_w_ih"][:, DIM:].T),
        wide(v["L3_gnn_w_hh"].T), wide(v["L1_gnn_A"].T)], axis=1)
    prew = _np.concatenate([wide(v["L2_gnn_weight"].transpose(2, 0, 1)), wide(v["L2_gnn_w_ih"].T)], axis=1)
    c2w = wide(v["L3_gnn_conv2_w"].transpose(1, 2, 0))

    def spread(a):
        return _np.broadcast_to(a.reshape(1, 1), (P, 1))

    def head(a):
        z = _np.zeros((P, 1), _np.float32)
        z[:a.size, 0] = a
        return z

    def gates(a):
        return wide(a.reshape(3, DIM).T)

    se = _np.zeros((P, 5), _np.float32)
    se[:, :3] = v["L3_gnn_w_se"].T
    unit = _np.eye(P, dtype=_np.float32)
    columns = _np.concatenate([
        wide(v["L0_gnn_fc_b"].reshape(HEADS, DIM).T), v["L0_gnn_q_w"], v["L0_gnn_k_w"], wide(v["L0_gnn_fp_b"]),
        wide(v["L1_gnn_W_b"]), spread(v["L1_gnn_gate_b"]), spread(v["L0_gnn_q_b"]), spread(v["L0_gnn_k_b"]),
        gates(v["L2_gnn_b_ih"]), gates(v["L2_gnn_b_hh"])]
        + [wide(v[f"L3_gnn_bn{i}_{c}"]) for c in "vgbm" for i in (1, 2)]
        + [gates(v["L3_gnn_b_ih"]), gates(v["L3_gnn_b_hh"]), wide(v["L1_gnn_gate_w"].reshape(2, DIM).T), se,
           head(v["L3_gnn_b_se"]), unit[:, 3:4], unit[:, 4:5], wide(v["L3_gnn_b_msg"])], axis=1)
    host = [("x", v["x"]), ("adj", v["adj"]), ("adjt", v["adj"].transpose(0, 2, 1)), ("nodemask", v["nodemask"].reshape(GRAPHS, TILES, P).transpose(0, 2, 1)),
            ("c2w", c2w), ("wraw", wraw), ("prew", prew), ("fcw", fcw), ("fpw", fpw), ("cols", columns)]
    nc = _bacc.Bacc("TRN2", target_bir_lowering=False, num_devices=1)
    arrays, args = {}, []
    for name, a in host:
        a = _np.ascontiguousarray(a)
        arrays[f"in_{name}_dram"] = a
        args.append(nc.dram_tensor(f"in_{name}_dram", a.shape, _mybir.dt.from_np(a.dtype), kind="ExternalInput").ap())
    args.append(nc.dram_tensor("out_0_dram", (GRAPHS, NODES, DIM), _mybir.dt.float32, kind="ExternalOutput").ap())
    build(nc, *args)
    r = _run(nc, [arrays], core_ids=[0])
    return r.results[0]["out_0_dram"]
```
